# Optimizing a Trainium2 kernel written in Bass

```python
import numpy as np
import jax
import jax.numpy as jnp

def _softmax(x, axis=-1):
    return jax.nn.softmax(x, axis=axis)

def _gelu(x):
    return jax.nn.gelu(x, approximate=True)

def _silu(x):
    return jax.nn.silu(x)

def _sigmoid(x):
    return jax.nn.sigmoid(x)

def _layernorm(x, axis=-1, eps=1e-05):
    m = jnp.mean(x, axis=axis, keepdims=True)
    v = jnp.var(x, axis=axis, keepdims=True)
    return (x - m) / jnp.sqrt(v + eps)

def _scatter_add(tgt, idx, src, axis=0):
    return tgt.at[idx].add(src)

def _segment_sum(src, seg, n):
    return jax.ops.segment_sum(src, seg, n)
kernel_name = 'mk_gnn_preln_d4_gnn_r8_732382'

def setup_inputs(seed: int=0):
    np.random.seed(seed)
    _w = jnp.asarray

    def _rec_inputs():
        import jax
        import jax.numpy as jnp
        _gk = jax.random.key(seed)
        x = -0.000202 + 1 * jax.random.normal(jax.random.fold_in(_gk, 1), (6250, 128), jnp.float32)
        _s = jax.random.randint(jax.random.fold_in(_gk, 2), (100000,), 0, 6250, jnp.int32)
        _d = jax.random.randint(jax.random.fold_in(_gk, 3), (100000,), 0, 6250, jnp.int32)
        _loop = jnp.arange(6250, dtype=jnp.int32)
        src = jnp.concatenate([_s, _d, _loop])
        dst = jnp.concatenate([_d, _s, _loop])
        _o = jnp.argsort(dst, stable=True)
        src = src[_o]
        dst = dst[_o]
        edge_attr_64 = 0.000189758 + 1.00013 * jax.random.normal(jax.random.fold_in(_gk, 11), (206250, 64), jnp.float32)
        edge_weight = jax.random.uniform(jax.random.fold_in(_gk, 13), (206250,), jnp.float32, 0.0, 0.999998)
        return (x, src, dst, edge_attr_64, edge_weight)
    x, src, dst, edge_attr_64, edge_weight = _rec_inputs()

    def _L0_gnn_setup():
        import jax, jax.numpy as jnp
        import numpy as np
        N, E, D, H = (6250, 100000, 128, 4)
        DH = D // H
        BN_EPS = 1e-05
        key = jax.random.key(seed)
        ks = jax.random.split(key, 16)
        s = 0.02
        inp = {'x': jax.random.normal(ks[0], (N, D), dtype=jnp.float32), 'edge_index': jax.random.randint(ks[1], (2, E), 0, N, dtype=jnp.int64), 'Wk': jax.random.normal(ks[2], (D, D), dtype=jnp.float32) * s, 'bk': jnp.zeros((D,), jnp.float32), 'Wm': jax.random.normal(ks[3], (D, D), dtype=jnp.float32) * s, 'bm': jnp.zeros((D,), jnp.float32), 'Wq': jax.random.normal(ks[4], (D, D), dtype=jnp.float32) * s, 'bq': jnp.zeros((D,), jnp.float32), 'W1': jax.random.normal(ks[5], (D, D), dtype=jnp.float32) * s, 'b1': jnp.zeros((D,), jnp.float32), 'gamma': jnp.ones((D,), jnp.float32), 'beta': jnp.zeros((D,), jnp.float32), 'W2': jax.random.normal(ks[6], (D, D), dtype=jnp.float32) * s, 'b2': jnp.zeros((D,), jnp.float32)}
        return inp
    _L0_gnn_all = _L0_gnn_setup()
    _L0_gnn_in = {k: v for k, v in _L0_gnn_all.items() if k in ('Wk', 'bk', 'Wm', 'bm', 'Wq', 'bq', 'W1', 'b1', 'gamma', 'beta', 'W2', 'b2')}
    del _L0_gnn_all

    def _L1_gnn_setup():
        import jax, jax.numpy as jnp
        import numpy as np
        N_NODES = 6250
        N_EDGES = 100000
        IN_F = 128
        OUT_F = 128
        HEADS = 8
        HEAD_DIM = OUT_F // HEADS
        EDGE_F = 64
        key = jax.random.key(seed)
        ks = jax.random.split(key, 12)
        s = 0.05
        return {'node_features': jax.random.normal(ks[0], (N_NODES, IN_F), jnp.float32), 'edge_index': jax.random.randint(ks[1], (2, N_EDGES), 0, N_NODES, jnp.int32), 'edge_features': jax.random.normal(ks[2], (N_EDGES, EDGE_F), jnp.float32), 'Wq': jax.random.normal(ks[3], (IN_F, OUT_F), jnp.float32) * s, 'bq': jnp.zeros((OUT_F,), jnp.float32), 'Wk': jax.random.normal(ks[4], (IN_F, OUT_F), jnp.float32) * s, 'bk': jnp.zeros((OUT_F,), jnp.float32), 'Wv': jax.random.normal(ks[5], (IN_F, OUT_F), jnp.float32) * s, 'bv': jnp.zeros((OUT_F,), jnp.float32), 'We': jax.random.normal(ks[6], (EDGE_F, HEADS), jnp.float32) * s, 'be': jnp.zeros((HEADS,), jnp.float32), 'Wo': jax.random.normal(ks[7], (OUT_F, OUT_F), jnp.float32) * s, 'bo': jnp.zeros((OUT_F,), jnp.float32)}
    _L1_gnn_all = _L1_gnn_setup()
    _L1_gnn_in = {k: v for k, v in _L1_gnn_all.items() if k in ('Wq', 'bq', 'Wk', 'bk', 'Wv', 'bv', 'We', 'be', 'Wo', 'bo')}
    del _L1_gnn_all

    def _L2_gnn_setup():
        import jax, jax.numpy as jnp
        import numpy as np
        N_NODES = 6250
        N_EDGES = 100000
        IN_F = 128
        OUT_F = 32
        HEADS = 4
        NEG_SLOPE = 0.2
        EPS = 1e-10

        def _xavier(key, shape):
            fan_in, fan_out = (shape[-2], shape[-1])
            bound = float(np.sqrt(6.0 / (fan_in + fan_out)))
            return jax.random.uniform(key, shape, jnp.float32, -bound, bound)
        key = jax.random.key(seed)
        kx, ke, kw, ks, kd = jax.random.split(key, 5)
        x = jax.random.normal(kx, (N_NODES, IN_F), jnp.float32)
        edge_index = jax.random.randint(ke, (2, N_EDGES), 0, N_NODES, jnp.int32)
        W = _xavier(kw, (HEADS, IN_F, OUT_F))
        a_src = _xavier(ks, (HEADS, OUT_F, 1))
        a_dst = _xavier(kd, (HEADS, OUT_F, 1))
        return {'x': x, 'edge_index': edge_index, 'W': W, 'a_src': a_src, 'a_dst': a_dst}
    _L2_gnn_all = _L2_gnn_setup()
    _L2_gnn_in = {k: v for k, v in _L2_gnn_all.items() if k in ('W', 'a_src', 'a_dst')}
    del _L2_gnn_all

    def _L3_gnn_setup():
        import jax, jax.numpy as jnp
        import numpy as np
        N = 12500
        D = 128
        E = 75000
        key = jax.random.key(seed)
        k = jax.random.split(key, 7)
        x = jax.random.normal(k[0], (N, D), dtype=jnp.float32)
        edge_index = jax.random.randint(k[1], (2, E), 0, N, dtype=jnp.int32)
        edge_weight = jax.random.uniform(k[2], (E,), dtype=jnp.float32)
        s = 1.0 / np.sqrt(D)
        W1 = jax.random.uniform(k[3], (D, D), minval=-s, maxval=s, dtype=jnp.float32)
        b1 = jax.random.uniform(k[4], (D,), minval=-s, maxval=s, dtype=jnp.float32)
        W2 = jax.random.uniform(k[5], (D, D), minval=-s, maxval=s, dtype=jnp.float32)
        b2 = jax.random.uniform(k[6], (D,), minval=-s, maxval=s, dtype=jnp.float32)
        return {'x': x, 'edge_index': edge_index, 'edge_weight': edge_weight, 'W1': W1, 'b1': b1, 'W2': W2, 'b2': b2}
    _L3_gnn_all = _L3_gnn_setup()
    _L3_gnn_in = {k: v for k, v in _L3_gnn_all.items() if k in ('W1', 'b1', 'W2', 'b2')}
    del _L3_gnn_all
    return {'x': x, 'src': src, 'dst': dst, 'edge_attr_64': edge_attr_64, 'edge_weight': edge_weight, 'L0_gnn_Wk': _L0_gnn_in['Wk'], 'L0_gnn_bk': _L0_gnn_in['bk'], 'L0_gnn_Wm': _L0_gnn_in['Wm'], 'L0_gnn_bm': _L0_gnn_in['bm'], 'L0_gnn_Wq': _L0_gnn_in['Wq'], 'L0_gnn_bq': _L0_gnn_in['bq'], 'L0_gnn_W1': _L0_gnn_in['W1'], 'L0_gnn_b1': _L0_gnn_in['b1'], 'L0_gnn_gamma': _L0_gnn_in['gamma'], 'L0_gnn_beta': _L0_gnn_in['beta'], 'L0_gnn_W2': _L0_gnn_in['W2'], 'L0_gnn_b2': _L0_gnn_in['b2'], 'L1_gnn_Wq': _L1_gnn_in['Wq'], 'L1_gnn_bq': _L1_gnn_in['bq'], 'L1_gnn_Wk': _L1_gnn_in['Wk'], 'L1_gnn_bk': _L1_gnn_in['bk'], 'L1_gnn_Wv': _L1_gnn_in['Wv'], 'L1_gnn_bv': _L1_gnn_in['bv'], 'L1_gnn_We': _L1_gnn_in['We'], 'L1_gnn_be': _L1_gnn_in['be'], 'L1_gnn_Wo': _L1_gnn_in['Wo'], 'L1_gnn_bo': _L1_gnn_in['bo'], 'L2_gnn_W': _L2_gnn_in['W'], 'L2_gnn_a_src': _L2_gnn_in['a_src'], 'L2_gnn_a_dst': _L2_gnn_in['a_dst'], 'L3_gnn_W1': _L3_gnn_in['W1'], 'L3_gnn_b1': _L3_gnn_in['b1'], 'L3_gnn_W2': _L3_gnn_in['W2'], 'L3_gnn_b2': _L3_gnn_in['b2']}

def reference(x, src, dst, edge_attr_64, edge_weight, L0_gnn_Wk, L0_gnn_bk, L0_gnn_Wm, L0_gnn_bm, L0_gnn_Wq, L0_gnn_bq, L0_gnn_W1, L0_gnn_b1, L0_gnn_gamma, L0_gnn_beta, L0_gnn_W2, L0_gnn_b2, L1_gnn_Wq, L1_gnn_bq, L1_gnn_Wk, L1_gnn_bk, L1_gnn_Wv, L1_gnn_bv, L1_gnn_We, L1_gnn_be, L1_gnn_Wo, L1_gnn_bo, L2_gnn_W, L2_gnn_a_src, L2_gnn_a_dst, L3_gnn_W1, L3_gnn_b1, L3_gnn_W2, L3_gnn_b2):
    import jax
    import jax.numpy as jnp

    def _L0_gnn_ref(x, edge_index, Wk, bk, Wm, bm, Wq, bq, W1, b1, gamma, beta, W2, b2):
        import jax, jax.numpy as jnp
        import numpy as np
        N, E, D, H = (6250, 100000, 128, 4)
        DH = D // H
        BN_EPS = 1e-05
        src = edge_index[0]
        dst = edge_index[1]
        x_i = x[dst]
        x_j = x[src]
        key = (x_i @ Wk + bk).reshape(-1, H, DH)
        msg = (x_j @ Wm + bm).reshape(-1, H, DH)
        query = (x_j @ Wq + bq).reshape(-1, H, DH) / jnp.sqrt(jnp.float32(DH))
        scores = jnp.sum(query * key, axis=2)
        smax = jax.ops.segment_max(scores, src, num_segments=N)
        e = jnp.exp(scores - smax[src])
        ssum = jax.ops.segment_sum(e, src, num_segments=N)
        alpha = e / ssum[src]
        cnt = jax.ops.segment_sum(jnp.ones((scores.shape[0],), jnp.float32), src, num_segments=N)
        alpha = alpha * cnt[src][:, None]
        out_e = (msg * alpha[:, :, None]).reshape(-1, D)
        out = jax.ops.segment_sum(out_e, dst, num_segments=N)
        h = out @ W1 + b1
        mean = jnp.mean(h, axis=0)
        var = jnp.var(h, axis=0)
        h = (h - mean) * jax.lax.rsqrt(var + BN_EPS) * gamma + beta
        h = jax.nn.relu(h)
        return h @ W2 + b2

    def _L1_gnn_ref(node_features, edge_index, edge_features, Wq, bq, Wk, bk, Wv, bv, We, be, Wo, bo):
        import jax, jax.numpy as jnp
        import numpy as np
        N_NODES = 6250
        N_EDGES = 100000
        IN_F = 128
        OUT_F = 128
        HEADS = 8
        HEAD_DIM = OUT_F // HEADS
        EDGE_F = 64
        n_nodes = node_features.shape[0]
        scale = HEAD_DIM ** (-0.5)
        sources = edge_index[0]
        targets = edge_index[1]
        q = (node_features @ Wq + bq).reshape(n_nodes, HEADS, HEAD_DIM)
        k = (node_features @ Wk + bk).reshape(n_nodes, HEADS, HEAD_DIM)
        v = (node_features @ Wv + bv).reshape(n_nodes, HEADS, HEAD_DIM)
        q_t = q[targets]
        k_s = k[sources]
        v_s = v[sources]
        scores = jnp.sum(q_t * k_s, axis=-1) * scale + (edge_features @ We + be)
        max_s = jax.ops.segment_max(scores, targets, num_segments=n_nodes)
        e = jnp.exp(scores - max_s[targets])
        denom = jax.ops.segment_sum(e, targets, num_segments=n_nodes) + 1e-10
        probs = e / denom[targets]
        weighted = (probs[:, :, None] * v_s).reshape(scores.shape[0], -1)
        agg = jax.ops.segment_sum(weighted, targets, num_segments=n_nodes)
        return agg @ Wo + bo

    def _L2_gnn_ref(x, edge_index, W, a_src, a_dst):
        import jax, jax.numpy as jnp
        import numpy as np
        N_NODES = 6250
        N_EDGES = 100000
        IN_F = 128
        OUT_F = 32
        HEADS = 4
        NEG_SLOPE = 0.2
        EPS = 1e-10

        def _xavier(key, shape):
            fan_in, fan_out = (shape[-2], shape[-1])
            bound = float(np.sqrt(6.0 / (fan_in + fan_out)))
            return jax.random.uniform(key, shape, jnp.float32, -bound, bound)
        num_nodes = x.shape[0]
        h = jnp.einsum('ni,hio->nho', x, W)
        src, dst = (edge_index[0], edge_index[1])
        e_src = jnp.einsum('nho,ho->nh', h, a_src[..., 0])
        e_dst = jnp.einsum('nho,ho->nh', h, a_dst[..., 0])
        e = e_src[src] + e_dst[dst]
        e = jnp.where(e >= 0, e, NEG_SLOPE * e)
        seg_max = jax.ops.segment_max(e, dst, num_segments=num_nodes)
        e_max = jnp.maximum(seg_max, 0.0)
        exp_e = jnp.exp(e - e_max[dst])
        sum_exp = jax.ops.segment_sum(exp_e, dst, num_segments=num_nodes)
        alpha = exp_e / (sum_exp[dst] + EPS)
        weighted = alpha[..., None] * h[src]
        out = jax.ops.segment_sum(weighted, dst, num_segments=num_nodes)
        return out.reshape(num_nodes, -1)

    def _L3_gnn_ref(x, edge_index, edge_weight, W1, b1, W2, b2):
        import jax, jax.numpy as jnp
        import numpy as np
        N = 12500
        D = 128
        E = 75000
        row, col = (edge_index[0], edge_index[1])
        msgs = edge_weight[:, None] * x[row]
        agg = jax.ops.segment_sum(msgs, col, num_segments=x.shape[0])
        h = (agg + x) @ W1.T + b1 + agg * x @ W2.T + b2
        out = jax.nn.leaky_relu(h, negative_slope=0.2)
        return out
    edge_index = jnp.stack([src, dst])
    h = jnp.maximum(_layernorm(x, axis=-1), 0.0)
    x = x + _L0_gnn_ref(h, edge_index, L0_gnn_Wk, L0_gnn_bk, L0_gnn_Wm, L0_gnn_bm, L0_gnn_Wq, L0_gnn_bq, L0_gnn_W1, L0_gnn_b1, L0_gnn_gamma, L0_gnn_beta, L0_gnn_W2, L0_gnn_b2)
    h = jnp.maximum(_layernorm(x, axis=-1), 0.0)
    x = x + _L1_gnn_ref(h, edge_index, edge_attr_64, L1_gnn_Wq, L1_gnn_bq, L1_gnn_Wk, L1_gnn_bk, L1_gnn_Wv, L1_gnn_bv, L1_gnn_We, L1_gnn_be, L1_gnn_Wo, L1_gnn_bo)
    h = jnp.maximum(_layernorm(x, axis=-1), 0.0)
    x = x + _L2_gnn_ref(h, edge_index, L2_gnn_W, L2_gnn_a_src, L2_gnn_a_dst)
    h = jnp.maximum(_layernorm(x, axis=-1), 0.0)
    x = x + _L3_gnn_ref(h, edge_index, edge_weight, L3_gnn_W1, L3_gnn_b1, L3_gnn_W2, L3_gnn_b2)
    return x

_drawn_inputs = setup_inputs


def setup_inputs(seed=0):
    import zlib

    import numpy as np

    out = dict(_drawn_inputs(seed))
    spreads = {'L0_gnn_bk': (0.0, 0.8),
     'L0_gnn_bm': (0.0, 0.1),
     'L0_gnn_bq': (0.0, 0.8),
     'L0_gnn_b1': (0.0, 0.8),
     'L0_gnn_gamma': (1.0, 0.2),
     'L0_gnn_beta': (0.0, 0.385),
     'L0_gnn_b2': (0.0, 0.1),
     'L1_gnn_bq': (0.0, 0.8),
     'L1_gnn_bk': (0.0, 0.8),
     'L1_gnn_bv': (0.0, 0.1),
     'L1_gnn_be': (0.0, 0.8),
     'L1_gnn_bo': (0.0, 0.1)}
    factors = {'edge_attr_64': 5.735,
     'L0_gnn_Wk': 6.784,
     'L0_gnn_Wq': 8.0,
     'L1_gnn_Wq': 8.0,
     'L1_gnn_Wk': 8.0,
     'L1_gnn_We': 5.81,
     'L3_gnn_b1': 6.355,
     'L3_gnn_b2': 6.156}
    for name, (base, spread) in spreads.items():
        noise = np.random.default_rng([zlib.crc32(name.encode()), seed]).standard_normal(out[name].shape)
        drawn = base * np.exp(spread * noise) if base else spread * noise
        out[name] = jnp.asarray(drawn.astype(out[name].dtype))
    for name, factor in factors.items():
        out[name] = (out[name] * factor).astype(out[name].dtype)
    return out
```

```python
from contextlib import ExitStack

import concourse.bass as bass
from concourse import mybir

F32 = mybir.dt.float32
I32 = mybir.dt.int32
ALU = mybir.AluOpType
ACT = mybir.ActivationFunctionType
AX = mybir.AxisListType

P = 128
N, D, E = 6250, 128, 206250
EF = 64
BPG = 4
NG = -(-N // (P * BPG))
NB = NG * BPG
NPAD = NB * P
GN = BPG * P
T = 1612
EP = P * T
K = 13
IT = T // K
assert EP >= E and T % (2 * K) == 0
PADN = 6271
assert N <= PADN < NPAD
KW = 1616
C = 2048
LOGC, LOGP = 11, 7
KE = 2 * K
NPAY = EP // (P * KE)
PW = 16
BIG = 1.0e30
H0, H1, H2 = 4, 8, 4
EPS = 1e-5


class Seq:

    def __init__(self, eng, sem, base=0, i=None, per=0):
        self.eng, self.sem, self.base, self.i, self.per, self.k = eng, sem, base, i, per, 0

    def did(self, ins):
        self.k += 1
        ins.then_inc(self.sem, 1)

    def value(self, k):
        return self.base + k if self.i is None else self.i * self.per + (self.base + k)

    def wait(self):
        self.eng.wait_ge(self.sem, self.value(self.k))

    def do(self, ins):
        self.did(ins)
        self.wait()


def graph_layers_kernel(nc, A, out):
    with ExitStack() as ctx:
        def sb(name, shape, dt=F32):
            return ctx.enter_context(nc.sbuf_tensor(name, shape, dt))

        sems = {}

        def S(name):
            if name not in sems:
                sems[name] = ctx.enter_context(nc.semaphore(name))
            return sems[name]

        def dram(name, shape, dt=F32):
            return nc.dram_tensor(name, shape, dt).ap()

        psA = ctx.enter_context(nc.psum_tensor("psA", [P, 512], F32))
        psB = ctx.enter_context(nc.psum_tensor("psB", [P, 4, 512], F32))
        psC = ctx.enter_context(nc.psum_tensor("psC", [P, 1024], F32))
        psD = ctx.enter_context(nc.psum_tensor("psD", [P, 512], F32))

        xsb = sb("xsb", [P, NB, D])
        ident = sb("ident", [P, P])
        ones = sb("ones", [P, P])
        before = sb("before", [P, P])
        after = sb("after", [P, P])
        nid = sb("nid", [P, NB])
        sgn = sb("sgn", [P, 8])
        wcat0 = sb("wcat0", [P, 3 * D])
        bcat0 = sb("bcat0", [1, 3 * D])
        wcat1 = sb("wcat1", [P, 3 * D])
        bcat1 = sb("bcat1", [1, 3 * D])
        w1_0 = sb("w1_0", [P, D])
        w2_0 = sb("w2_0", [P, D])
        b2_0 = sb("b2_0", [1, D])
        bncol = sb("bncol", [P, 8])
        we2 = sb("we2", [P, 16])
        be2 = sb("be2", [1, 16])
        wo_1 = sb("wo_1", [P, D])
        bo_1 = sb("bo_1", [1, D])
        w_2 = sb("w_2", [P, D])
        avec = sb("avec", [P, 2, D])
        w3raw = sb("w3raw", [P, 2, D])
        w3t = sb("w3t", [P, 2, D])
        b3 = sb("b3", [1, 2, D])

        seg_i = sb("seg_i", [P, T], I32)
        oth_i = sb("oth_i", [P, T], I32)
        restart = sb("restart", [P, T])
        ew = sb("ew", [P, T])
        endix = sb("endix", [P, NB], I32)
        carix = sb("carix", [P, NB], I32)
        bias2 = sb("bias2", [P, P])
        contT = sb("contT", [P, P])

        rows_s = [sb(f"rows_s{b}", [P, K, 260]) for b in range(2)]
        rows_d = [sb(f"rows_d{b}", [P, K, D]) for b in range(2)]
        ix_s = [sb(f"ix_s{b}", [P, K], I32) for b in range(2)]
        ix_d = [sb(f"ix_d{b}", [P, K], I32) for b in range(2)]
        pay = [sb(f"pay{b}", [P, K, PW]) for b in range(2)]
        s_ext = sb("s_ext", [P, 8, K + 1])
        s_max = sb("s_max", [P, 8, K + 1])
        m_ext = sb("m_ext", [P, 8, K + 1])
        rst = sb("rst", [P, 8, K + 1])
        dd = sb("dd", [P, 8, K + 1])
        ww = sb("ww", [P, 8, K])
        dtmp = sb("dtmp", [P, 8, K])

        long = sb("long", [P, NPAD])
        work = sb("work", [P, 9500])
        at = [0]

        def w_view(n):
            a = work[:, at[0]:at[0] + n]
            at[0] += n
            assert at[0] <= 9500
            return a

        FM = 136
        bv = w_view(FM * (K + 1))
        abig = w_view(FM * (K + 1))
        st = w_view(FM * (K + 1))
        psrow = [w_view(K * 144) for _ in range(2)]
        keyin = [work[:, i * C:(i + 1) * C] for i in range(2)]
        rows4 = work[:, 0:4 * KW].rearrange("p (j w) -> p j w", w=KW)
        rsign = work[:, 4 * KW:5 * KW]

        attr = work[:, 100:100 + KE * EF].rearrange("p (t w) -> p t w", w=EF)
        attrT = work[:, 2000:2000 + KE // 2 * P].rearrange("p (u r) -> p u r", r=P)
        pay0 = sb("payrow", [P, KE, PW])
        pcol_i = sb("pcol_i", [P, KE], I32)
        pcol_f = sb("pcol_f", [P, KE])

        X = long[:, 0:C]
        Y = long[:, C:2 * C]
        eid_i = long[:, 2 * C:3 * C].bitcast(I32)
        raw = long[:, 2 * C:2 * C + T].bitcast(I32)
        eid_a = Y[:, 0:T].bitcast(I32)
        cnt_tmp = work[:, 4000:4000 + T]
        nid_i = sb("nid_i", [P, NB], I32)
        part_i = sb("part_i", [P, 8], I32)
        diag2 = sb("diag2", [P, 2, P])
        firstrow = sb("firstrow", [P, P])
        cmp4 = sb("cmp4", [P, BPG, P])
        nt_c = sb("nt_c", [P, 2, BPG])
        ctm = sb("ctm", [1, 8])
        segf = X[:, 0:KW]
        hT_all = long

        hst = sb("hst", [P, BPG, D])
        hst2 = sb("hst2", [P, BPG, D])
        hT = sb("hT", [P, 2, GN])
        tab = sb("tab", [P, BPG, 3 * D])
        ln_s = sb("ln_s", [P, 4, BPG])
        nt_f = sb("nt_f", [P, 6, BPG])
        nt_i = sb("nt_i", [P, BPG], I32)
        fe_i = sb("fe_i", [P, BPG], I32)
        fc_i = sb("fc_i", [P, BPG], I32)
        end4 = sb("end4", [P, BPG, 144])
        car4 = sb("car4", [P, BPG, 144])
        mx4 = sb("mx4", [P, 3, BPG, 8])
        cst = sb("cst", [P, 144])
        ctst = sb("ctst", [P, 144])
        ctz = sb("ctz", [1, 144])
        mcar = sb("mcar", [P, 8])
        dwide = work[:, 0:1024]
        wwide = work[:, 1024:2048]

        keys_dram = dram("keys_in", [2, P, C])
        sorted_dram = dram("keys_sorted", [2, P * C])
        pay_dram = dram("payload", [EP, PW])
        paya_dram = dram("payload_by_dst", [EP, PW])
        q0_t = dram("q0", [NPAD, D])
        k0_t = dram("k0", [NPAD, D])
        m0_t = dram("m0", [NPAD, D])
        qm0_t = dram("qm0", [NPAD, 260])
        q1_t = dram("q1", [NPAD, D])
        kv1_t = dram("kv1", [NPAD, 2 * D])
        h2_t = dram("h2", [NPAD, D + 4])
        ed2_t = dram("ed2", [NPAD, 4])
        x3_t = dram("x3", [NPAD, D])
        keyrow_t = [dram(f"keyrow{o}", [P, KW]) for o in range(2)]

        class Pass:
            def __init__(self, name, H, dh, soft, tabs, tabd, W):
                self.name, self.H, self.dh, self.soft = name, H, dh, soft
                self.tabs, self.tabd, self.W = tabs, tabd, W
                self.F = H * (dh + 1) if soft else D
                self.ps = dram(f"state_{name}", [EP + 1, W])
                self.ct = dram(f"carry_{name}", [P + 1, W])

            def s(self, what):
                return S(f"pass_{what}")

            def own(self, what):
                return S(f"{self.name}_{what}")

            def total(self, what):
                half = IT // 2
                exps = IT if self.soft or self is PA else 0
                return {"free0": 1 + half, "free1": 1 + half, "ix0": IT, "ix1": IT, "prep": 2, "steps": self.steps * IT,
                        "laid": 1 + IT, "laid0": half, "laid1": half, "arg": IT, "expw": exps, "decay": IT, "scanned": IT,
                        "sent0": 16 + 16 * half, "sent1": 16 + 16 * half, "ends_free": 1 + NG, "fix": 2 * NG,
                        "ends_in": 32 * BPG * NG, "mg_arg": NG * self.soft, "mg_exp": 2 * NG * self.soft, "tails": 1,
                        "maxrows": int(self.soft), "cw_arg": int(self.soft), "cw": int(self.soft), "cwT": int(self.soft),
                        "cwT_in": int(self.soft), "carried": 1, "carry_made": 1, "carry_out": 16}[what]

            def base(self, what):
                return sum(q.total(what) for q in passes[:passes.index(self)])

            def on(self, what, value):
                return self.s(what), value + self.base(what)

        PB = Pass("pB", H0, 0, True, k0_t, q0_t, 12)
        PA = Pass("pA", H0, 32, False, qm0_t, k0_t, D)
        P1 = Pass("p1", H1, 16, True, kv1_t, q1_t, 144)
        P2 = Pass("p2", H2, 32, True, h2_t, ed2_t, 136)
        P3 = Pass("p3", 1, D, False, x3_t, None, D)
        passes = [PB, PA, P1, P2, P3]
        PB.steps, PB.needs = 10, [("ix_ready", 1), ("j0_out", 16 * 3 * NG)]
        PA.steps, PA.needs = 7, [("ix_ready", 3), ("qm_out", 48 * NG)]
        P1.steps, P1.needs = 12, [("j1_out", 32 * NG)]
        P2.steps, P2.needs = 12, [("j2_out", 32 * NG)]
        P3.steps, P3.needs = 4, [("j3_out", 16 * NG)]

        cnt = ew

        def grows(t, g):
            return t[bass.ds(g * GN, GN), :].rearrange("(j p) w -> p j w", p=P)

        def constants_pool(g):
            g.memset(ident[:, :], 0.0).then_inc(S("c_fill"), 1)
            g.memset(before[:, :], 1.0).then_inc(S("c_fill"), 1)
            g.memset(after[:, :], 1.0).then_inc(S("c_fill"), 1)
            g.memset(ones[:, :], 1.0).then_inc(S("consts"), 1)
            g.iota(nid_i[:, :], [[P, NB]], base=0, channel_multiplier=1).then_inc(S("consts"), 1)
            g.iota(eid_i, [[1, C]], base=0, channel_multiplier=C).then_inc(S("consts"), 1)
            g.iota(part_i[:, :], [[0, 8]], base=0, channel_multiplier=1).then_inc(S("consts"), 1)
            g.wait_ge(S("c_fill"), 3)
            g.affine_select(out=ident[:, :], in_=ident[:, :], compare_op=ALU.not_equal, fill=1.0, base=0,
                            pattern=[[-1, P]], channel_multiplier=1).then_inc(S("consts"), 1)
            g.affine_select(out=before[:, :], in_=before[:, :], compare_op=ALU.is_gt, fill=0.0, base=0,
                            pattern=[[-1, P]], channel_multiplier=1).then_inc(S("consts"), 1)
            g.affine_select(out=after[:, :], in_=after[:, :], compare_op=ALU.is_gt, fill=0.0, base=0,
                            pattern=[[1, P]], channel_multiplier=-1).then_inc(S("consts"), 1)

        CONSTS = 7

        def padding_dve(v):
            nc.vector.memset(X.bitcast(I32), PADN).then_inc(S("padded"), 1)
            nc.vector.memset(Y.bitcast(I32), PADN).then_inc(S("padded"), 1)
            nc.vector.memset(xsb[:, N // P:NB, :], 0.0).then_inc(S("padded"), 1)
            nc.vector.memset(ctz[:, :], 0.0).then_inc(S("dummies"), 1)
            nc.vector.memset(ctm[:, :], -BIG).then_inc(S("dummies"), 1)
            nc.vector.memset(we2[:, :], 0.0).then_inc(S("dummies"), 1)
            nc.vector.memset(pay0[:, :, :], 0.0).then_inc(S("dummies"), 1)
            nc.vector.memset(attr[:, :, :], 0.0).then_inc(S("dummies"), 1)
            nc.vector.memset(pcol_i[:, :], 0).then_inc(S("dummies"), 1)
            nc.vector.memset(pcol_f[:, :], 0.0).then_inc(S("dummies"), 1)
            nc.vector.memset(rst[:, :, :], -BIG).then_inc(S("dummies"), 1)
            nc.vector.memset(dd[:, :, :], -BIG).then_inc(S("dummies"), 1)
            for b in range(2):
                nc.vector.memset(psrow[b], 0.0).then_inc(S("dummies"), 1)
            v.wait_ge(S("consts"), CONSTS)
            q = Seq(v, S("pad_steps"))
            for k in range(8):
                q.did(nc.vector.tensor_scalar(part_i[:, k:k + 1], part_i[:, k:k + 1], k, 1, ALU.logical_shift_right, ALU.bitwise_and))
            q.did(nc.vector.tensor_copy(nid[:, :], nid_i[:, :]))
            q.wait()
            q.do(nc.vector.tensor_scalar(sgn[:, :], part_i[:, :], -2.0, 1.0, ALU.mult, ALU.add))

        DUMMIES = 11

        def loads_sp(sp):
            n = [0]

            def load(dst, src):
                n[0] += 1
                sp.dma_start(dst, src).then_inc(S("loaded"), 16)

            def row(name):
                return A[name].rearrange("(a d) -> a d", a=1)

            sp.wait_ge(S("padded"), 3)
            full, rest = E // C, E % C
            for name, dst in (("src", X), ("dst", Y)):
                d = dst.bitcast(I32)
                sp.dma_start(d[0:full, :], A[name][0:full * C].rearrange("(p c) -> p c", c=C)).then_inc(S("ends_in"), 16)
                sp.dma_start(d[full:full + 1, 0:rest], A[name][full * C:E].rearrange("(p c) -> p c", p=1)).then_inc(S("ends_in"), 16)
            whole = N // P
            load(xsb[:, 0:whole, :], A["x"][0:whole * P, :].rearrange("(j p) w -> p j w", p=P))
            load(xsb[0:N - whole * P, whole, :], A["x"][whole * P:N, :])
            for j, nm in enumerate("qkm"):
                load(wcat0[:, j * D:(j + 1) * D], A["L0_gnn_W" + nm])
                load(bcat0[:, j * D:(j + 1) * D], row("L0_gnn_b" + nm))
            for j, nm in enumerate("qkv"):
                load(wcat1[:, j * D:(j + 1) * D], A["L1_gnn_W" + nm])
                load(bcat1[:, j * D:(j + 1) * D], row("L1_gnn_b" + nm))
            load(w1_0[:, :], A["L0_gnn_W1"])
            load(w2_0[:, :], A["L0_gnn_W2"])
            load(b2_0[:, :], row("L0_gnn_b2"))
            with nc.allow_non_contiguous_dma(reason="a column of 128 values"):
                for j, nm in enumerate(("b1", "gamma", "beta")):
                    load(bncol[:, j:j + 1], A["L0_gnn_" + nm].rearrange("(p a) -> p a", a=1))
            sp.wait_ge(S("dummies"), DUMMIES)
            for j in range(2):
                load(we2[j * EF:(j + 1) * EF, j * 8:(j + 1) * 8], A["L1_gnn_We"])
                load(be2[:, j * 8:(j + 1) * 8], row("L1_gnn_be"))
            load(wo_1[:, :], A["L1_gnn_Wo"])
            load(bo_1[:, :], row("L1_gnn_bo"))
            load(w_2[:, :].rearrange("i (h o) -> i h o", h=H2), A["L2_gnn_W"].rearrange("h i o -> i h o"))
            for j, nm in enumerate(("src", "dst")):
                load(avec[:, j, :], A["L2_gnn_a_" + nm].rearrange("(a h) o b -> a (h o b)", a=1).to_broadcast([P, D]))
                load(w3raw[:, j, :], A[f"L3_gnn_W{j + 1}"])
                load(b3[:, j, :], row(f"L3_gnn_b{j + 1}"))
            assert n[0] == NLOADS, n[0]
            for q in passes:
                f = q.F
                sp.dma_start(q.ps[EP:EP + 1, :], ctz[:, 0:q.W]).then_inc(S("dummy_rows"), 16)
                if q.soft:
                    sp.dma_start(q.ct[P:P + 1, 0:f], ctz[:, 0:f]).then_inc(S("dummy_rows"), 16)
                    sp.dma_start(q.ct[P:P + 1, f:f + q.H], ctm[:, 0:q.H]).then_inc(S("dummy_rows"), 16)
                    if q.W > f + q.H:
                        sp.dma_start(q.ct[P:P + 1, f + q.H:q.W], ctz[:, 0:q.W - f - q.H]).then_inc(S("dummy_rows"), 16)
                else:
                    sp.dma_start(q.ct[P:P + 1, :], ctz[:, 0:q.W]).then_inc(S("dummy_rows"), 16)

        NLOADS = 2 + 6 + 6 + 3 + 3 + 4 + 2 + 1 + 6
        NDUMMY = 5 + 3 * 2 + 1 + 2

        def keys_dve(v):
            v.wait_ge(S("ends_in"), 64)
            v.wait_ge(S("consts"), CONSTS)
            q = Seq(v, S("key_steps"))
            srcs, dsts = X.bitcast(I32), Y.bitcast(I32)
            kb, ka = keyin[0].bitcast(I32), keyin[1].bitcast(I32)
            q.did(nc.vector.tensor_scalar(kb, srcs, 13, 1 << 30, ALU.logical_shift_left, ALU.bitwise_or))
            q.do(nc.vector.tensor_scalar(ka, dsts, 32.0, None, ALU.add))
            q.did(nc.vector.tensor_tensor(kb, kb, dsts, ALU.bitwise_or))
            q.do(nc.vector.tensor_scalar(ka, ka, 18, 0, ALU.logical_shift_left, ALU.bitwise_or))
            q.did(nc.vector.tensor_tensor(ka, ka, eid_i, ALU.bitwise_or))
            q.wait()
            v.sem_inc(S("keys_made"), 1)

        def keys_sp(sp):
            sp.wait_ge(S("keys_made"), 1)
            for o in range(2):
                sp.dma_start(keys_dram[o], keyin[o]).then_inc(S("keys_out"), 16)
            sp.wait_ge(S("keys_out"), 32)

        SORT_STEPS = sum(4 * k for k in range(1, LOGC)) + 2 * LOGC * (LOGP + 1) + sum(4 * q for q in range(1, LOGP)) + 2 * LOGP
        SORT_TURNS = 2 * LOGP
        SORT_SIGNS = 2 * LOGP + 1

        class Sort:

            def __init__(self):
                self.cur, self.oth = X, Y

            def swap(self):
                self.cur, self.oth = self.oth, self.cur

        def stage_views(a, j, k, directed):
            s = 1 << j
            if directed:
                w = a.rearrange("p (g d n h s) -> p d h g n s", d=2, n=1 << (k - 1 - j), h=2, s=s)
                return [(w[:, d, 0], w[:, d, 1]) for d in range(2)]
            w = a.rearrange("p (n h s) -> p h n s", h=2, s=s)
            return [(w[:, 0], w[:, 1])]

        def sort_dve(v):
            with v.Fori(0, 2) as o:
                q = Seq(v, S("sort_steps"), 0, o, SORT_STEPS)
                b = Sort()
                turn, sign = [0], [0]

                def stage(j, k, directed):
                    for d, ((lo, hi), (lo2, hi2)) in enumerate(zip(stage_views(b.cur, j, k, directed), stage_views(b.oth, j, k, directed))):
                        q.did(nc.vector.tensor_tensor(lo2, lo, hi, ALU.max if d else ALU.min))
                        q.did(nc.vector.tensor_tensor(hi2, lo, hi, ALU.min if d else ALU.max))
                    b.swap()
                    q.wait()

                def signed():
                    sign[0] += 1
                    v.wait_ge(S("sort_signs"), o * SORT_SIGNS + sign[0])
                    b.swap()

                v.wait_ge(S("sort_in"), o * 16 + 16)
                for k in range(1, LOGC):
                    for j in reversed(range(k)):
                        stage(j, k, True)
                for k in range(LOGC, LOGC + LOGP + 1):
                    if k > LOGC:
                        signed()
                        turn[0] += 1
                        v.wait_ge(S("sort_turns"), o * SORT_TURNS + turn[0])
                        nc.vector.tensor_copy(b.oth, psB[:, :, :].rearrange("p a b -> p (a b)")).then_inc(S("sort_evacs"), 1)
                        b.swap()
                        v.wait_ge(S("sort_evacs"), o * LOGP + turn[0] // 2 + 1)
                        lp = k - LOGC
                        for j in reversed(range(lp)):
                            stage(j, lp, k < LOGC + LOGP)
                        turn[0] += 1
                    signed()
                    for j in reversed(range(LOGC)):
                        stage(j, LOGC, False)
                assert q.k == SORT_STEPS, (q.k, SORT_STEPS)
                assert b.cur is sorted_at(), "the sorted keys' buffer"

        def sorted_at():
            n = sum(range(1, LOGC)) + LOGC * (LOGP + 1) + sum(range(1, LOGP + 1)) + SORT_SIGNS + LOGP
            return Y if n % 2 else X

        def sort_act(act):
            with act.Fori(0, 2) as o:
                b = Sort()
                steps = sum(4 * k for k in range(1, LOGC))
                for _ in range(sum(range(1, LOGC))):
                    b.swap()
                turn = 0
                for k in range(LOGC, LOGC + LOGP + 1):
                    lp = k - LOGC
                    if lp:
                        act.wait_ge(S("sort_steps"), o * SORT_STEPS + steps)
                        nc.scalar.mul(b.oth, b.cur, sgn[:, lp - 1:lp]).then_inc(S("sort_signs"), 1)
                        b.swap()
                        b.swap()
                        steps += (4 if lp < LOGP else 2) * lp
                        for _ in range(lp):
                            b.swap()
                        turn += 2
                        act.wait_ge(S("sort_turns"), o * SORT_TURNS + turn)
                        nc.scalar.mul(b.oth, psB[:, :, :].rearrange("p a b -> p (a b)"),
                                      sgn[:, lp:lp + 1]).then_inc(S("sort_signs"), 1)
                    else:
                        act.wait_ge(S("sort_steps"), o * SORT_STEPS + steps)
                        nc.scalar.mul(b.oth, b.cur, sgn[:, 0:1]).then_inc(S("sort_signs"), 1)
                    b.swap()
                    steps += 2 * LOGC
                    for _ in range(LOGC):
                        b.swap()

        def sort_pe(pe):
            with pe.Fori(0, 2) as o:
                b = Sort()
                steps = sum(4 * k for k in range(1, LOGC)) + 2 * LOGC
                for _ in range(sum(range(1, LOGC)) + 1 + LOGC):
                    b.swap()

                def turn_all():
                    for c in range(C // P):
                        ins = nc.tensor.transpose(psB[:, c // 4, (c % 4) * P:(c % 4 + 1) * P], b.cur[:, c * P:(c + 1) * P], ident[:, :])
                    ins.then_inc(S("sort_turns"), 1)

                sign = 1
                for lp in range(1, LOGP + 1):
                    b.swap()
                    sign += 1
                    pe.wait_ge(S("sort_signs"), o * SORT_SIGNS + sign)
                    turn_all()
                    b.swap()
                    for _ in range(lp):
                        b.swap()
                    steps += (4 if lp < LOGP else 2) * lp
                    pe.wait_ge(S("sort_evacs"), o * LOGP + lp)
                    pe.wait_ge(S("sort_steps"), o * SORT_STEPS + steps)
                    turn_all()
                    b.swap()
                    sign += 1
                    steps += 2 * LOGC
                    for _ in range(LOGC):
                        b.swap()

        def sort_sp(sp):
            sp.sem_inc(S("sort_free"), 1)
            with sp.Fori(0, 2) as o:
                sp.wait_ge(S("sort_free"), o + 1)
                sp.dma_start(X, keys_dram[bass.ds(o, 1), :, :].rearrange("o p c -> (o p) c")).then_inc(S("sort_in"), 16)
                sp.wait_ge(S("sort_steps"), (o + 1) * SORT_STEPS)
                sp.dma_start(sorted_dram[bass.ds(o, 1), :].rearrange("o (p c) -> (o p) c", c=C), sorted_at()).then_inc(S("sort_out"), 16)
                sp.wait_ge(S("sort_out"), o * 16 + 16)
                sp.sem_inc(S("sort_free"), 1)

        LN_STEPS = 8

        def proj_on(nm, what, value):
            before = "j0 j1 j2 j3".split().index(nm)
            return S("proj_" + what), value + before * (NG + (what in ("tr", "ht", "psfree", "tabfree")))

        def norm_group(v, nm, g, q, first_write):
            xg = xsb[:, bass.ds(g * BPG, BPG), :]
            bc = lambda k: ln_s[:, k, :].unsqueeze(2).to_broadcast([P, BPG, D])
            q.do(nc.vector.tensor_reduce(ln_s[:, 0, :], xg, AX.X, ALU.add))
            q.do(nc.vector.tensor_scalar(ln_s[:, 1, :], ln_s[:, 0, :], -1.0 / D, None, ALU.mult))
            first_write()
            q.do(nc.vector.tensor_tensor(hst[:, :, :], xg, bc(1), ALU.add))
            q.do(nc.vector.tensor_tensor(hst2[:, :, :], hst[:, :, :], hst[:, :, :], ALU.mult))
            q.do(nc.vector.tensor_reduce(ln_s[:, 0, :], hst2[:, :, :], AX.X, ALU.add))
            q.did(nc.vector.tensor_scalar(ln_s[:, 2, :], ln_s[:, 0, :], 1.0 / D, EPS, ALU.mult, ALU.add))
            v.wait_ge(*proj_on(nm, "sqrt", g + 1))
            q.do(nc.vector.reciprocal(ln_s[:, 1, :], ln_s[:, 3, :]))
            q.do(nc.vector.tensor_tensor(hst[:, :, :], hst[:, :, :], bc(1), ALU.mult))

        def proj_dve(v, nm, ncol):
            steps = LN_STEPS + 1 + (4 if nm == "j2" else 0)
            if nm == "j0":
                v.wait_ge(S("loaded"), 16 * NLOADS)
            with v.Fori(0, NG) as g:
                q = Seq(v, S(nm + "_steps"), 0, g, steps)
                left = "tr" if ncol else "tabfree"
                norm_group(v, nm, g, q, lambda: v.wait_ge(*proj_on(nm, left, g + 1)))
                q.did(nc.vector.tensor_scalar(hst[:, :, :], hst[:, :, :], 0.0, None, ALU.max))
                if nm == "j2":
                    v.wait_ge(*proj_on(nm, "tab", g + 1))
                    for j in range(2):
                        q.do(nc.vector.tensor_tensor(hst2[:, :, :], tab[:, :, 0:D],
                                                     avec[:, j, :].unsqueeze(1).to_broadcast([P, BPG, D]), ALU.mult))
                        q.do(nc.vector.tensor_reduce(tab[:, :, D + 4 * j:D + 4 * j + 4],
                                                     hst2[:, :, :].rearrange("p j (h o) -> p j h o", h=H2), AX.X, ALU.add))
                assert q.k == steps, (q.k, steps)

        def proj_pe(pe, nm, w, brow, ncol):
            pe.sem_inc(S("proj_tr"), 1)
            steps = LN_STEPS + 1 + (4 if nm == "j2" else 0)
            with pe.Fori(0, NG) as g:
                pe.wait_ge(S(nm + "_steps"), g * steps + LN_STEPS + 1)
                pe.wait_ge(*proj_on(nm, "ht", g + 1))
                for j in range(BPG):
                    ins = nc.tensor.transpose(psA[:, j * P:(j + 1) * P], hst[:, j, :], ident[:, :])
                ins.then_inc(S("proj_tr"), 1)
                pe.wait_ge(*proj_on(nm, "ht", g + 2))
                pe.wait_ge(*proj_on(nm, "psfree", g + 1))
                for j in range(BPG):
                    ins = nc.tensor.matmul(psB[:, j, 0:ncol], hT[:, 0, j * P:(j + 1) * P], w, start=True, stop=brow is None)
                    if brow is not None:
                        ins = nc.tensor.matmul(psB[:, j, 0:ncol], ones[0:1, :], brow, start=False, stop=True)
                ins.then_inc(S("proj_mm"), 1)

        def proj_act(act, nm, ncol):
            steps = LN_STEPS + 1 + (4 if nm == "j2" else 0)
            if ncol:
                act.sem_inc(S("proj_ht"), 1)
                act.sem_inc(S("proj_psfree"), 1)
            with act.Fori(0, NG) as g:
                act.wait_ge(S(nm + "_steps"), g * steps + 6)
                nc.scalar.activation(ln_s[:, 3, :], ln_s[:, 2, :], ACT.Sqrt).then_inc(S("proj_sqrt"), 1)
                if ncol:
                    act.wait_ge(*proj_on(nm, "tr", g + 2))
                    nc.scalar.copy(hT[:, 0, :], psA[:, :]).then_inc(S("proj_ht"), 1)
                    act.wait_ge(*proj_on(nm, "mm", g + 1))
                    act.wait_ge(*proj_on(nm, "tabfree", g + 1))
                    if nm == "j0":
                        nc.scalar.mul(tab[:, :, 0:D], psB[:, :, 0:D], 1.0 / (32 ** 0.5)).then_inc(S(nm + "_q"), 1)
                        ins = nc.scalar.copy(tab[:, :, D:ncol], psB[:, :, D:ncol])
                    else:
                        ins = nc.scalar.copy(tab[:, :, 0:ncol], psB[:, :, 0:ncol])
                    ins.then_inc(S("proj_tab"), 1)
                    act.wait_ge(*proj_on(nm, "tab", g + 1))
                    act.sem_inc(S("proj_psfree"), 1)

        def proj_sp(sp, nm, tabs):
            sp.sem_inc(S("proj_tabfree"), 1)
            steps = LN_STEPS + 1 + (4 if nm == "j2" else 0)
            with sp.Fori(0, NG) as g:
                if nm in ("j2", "j3"):
                    sp.wait_ge(S(nm + "_steps"), (g + 1) * steps)
                else:
                    sp.wait_ge(*proj_on(nm, "tab", g + 1))
                if nm == "j0":
                    sp.wait_ge(S("j0_q"), g + 1)
                for t, a, z in tabs:
                    src = hst if nm == "j3" else tab
                    sp.dma_start(grows(t, g), src[:, :, a:z]).then_inc(S(nm + "_out"), 16)
                sp.wait_ge(S(nm + "_out"), g * (16 * len(tabs)) + 16 * len(tabs))
                sp.sem_inc(S("proj_tabfree"), 1)

        def order_sp(sp, o):
            if o:
                sp.wait_ge(S("stats_done"), 1)
            sp.dma_start(raw, sorted_dram[o, 0:EP].bitcast(I32).rearrange("(p t) -> p t", t=T)).then_inc(S("raw_in"), 16)
            sp.wait_ge(S("keyrow_made"), o + 1)
            sp.dma_start(keyrow_t[o], segf).then_inc(S("keyrow_out"), 16)

        def order_dve(v, o):
            q = Seq(v, S(f"order_steps{o}"))
            v.wait_ge(S("raw_in"), 16 * (o + 1))
            if o == 0:
                q.did(nc.vector.tensor_scalar(seg_i[:, :], raw, 13, 0x1FFF, ALU.logical_shift_right, ALU.bitwise_and))
                q.do(nc.vector.tensor_scalar(oth_i[:, :], raw, 0x1FFF, 0, ALU.bitwise_and, ALU.bitwise_or))
            else:
                q.did(nc.vector.tensor_scalar(seg_i[:, :], raw, 18, 0x1FFF, ALU.logical_shift_right, ALU.bitwise_and))
                q.do(nc.vector.tensor_scalar(eid_a, raw, 0x3FFFF, 0, ALU.bitwise_and, ALU.bitwise_or))
                q.do(nc.vector.tensor_scalar(seg_i[:, :], seg_i[:, :], 32.0, None, ALU.subtract))
            v.sem_inc(S("ix_ready"), 1)
            q.did(nc.vector.memset(segf[:, T:KW], 0.0))
            q.do(nc.vector.tensor_copy(segf[:, 0:T], seg_i[:, :]))
            q.do(nc.vector.tensor_tensor(restart[:, 1:T], segf[:, 1:T], segf[:, 0:T - 1], ALU.is_equal))
            q.did(nc.vector.tensor_scalar(restart[:, 1:T], restart[:, 1:T], BIG, -BIG, ALU.mult, ALU.add))
            q.did(nc.vector.memset(restart[:, 0:1], -BIG))
            q.did(nc.vector.tensor_scalar(diag2[:, 0, :], ident[:, :], segf[:, 0:1], None, ALU.mult))
            q.do(nc.vector.tensor_scalar(diag2[:, 1, :], ident[:, :], segf[:, T - 1:T], None, ALU.mult))
            v.sem_inc(S("ends_made"), 1)
            v.wait_ge(S("ends_rows"), o + 1)
            q.do(nc.vector.tensor_copy(firstrow[:, :], psC[:, 0:P]))
            q.did(nc.vector.scalar_tensor_tensor(out=contT[:, :], in0=firstrow[:, :], scalar=segf[:, T - 1:T], in1=after[:, :],
                                                 op0=ALU.is_equal, op1=ALU.mult))
            q.do(nc.vector.scalar_tensor_tensor(out=bias2[:, :], in0=psC[:, P:2 * P], scalar=segf[:, 0:1], in1=before[:, :],
                                                op0=ALU.is_equal, op1=ALU.mult))
            q.do(nc.vector.tensor_reduce(segf[:, T:T + 1], bias2[:, :], AX.X, ALU.max))
            v.sem_inc(S("keyrow_made"), 1)
            q.do(nc.vector.tensor_scalar(bias2[:, :], bias2[:, :], BIG, -BIG, ALU.mult, ALU.add))
            if o == 0:
                q.do(nc.vector.tensor_scalar(cnt_tmp, restart[:, :], 1.0 / BIG, 1.0, ALU.mult, ALU.add))
                q.do(nc.vector.tensor_tensor_scan(cnt[:, :], cnt_tmp, ones[:, 0:1].to_broadcast([P, T]), 0.0, ALU.mult, ALU.add))
            v.sem_inc(S("order_ready"), 1)

        def order_pe(pe, o):
            pe.wait_ge(S("ends_made"), o + 1)
            nc.tensor.matmul(psC[:, 0:2 * P], ones[:, :], diag2[:, :, :].rearrange("p a b -> p (a b)"), start=True, stop=True).then_inc(S("ends_rows"), 1)

        NT_STEPS = 13

        def nodes_dve(v, o):
            with v.Fori(0, NG) as g:
                q = Seq(v, S(f"nt_steps{o}"), 0, g, NT_STEPS)
                nb = nid[:, bass.ds(g * BPG, BPG)]
                q.do(nc.vector.tensor_tensor(cmp4[:, :, :], firstrow[:, :].unsqueeze(1).to_broadcast([P, BPG, P]),
                                             nb.unsqueeze(2).to_broadcast([P, BPG, P]), ALU.is_le))
                q.do(nc.vector.tensor_reduce(nt_f[:, 0, :], cmp4[:, :, :], AX.X, ALU.add))
                q.do(nc.vector.tensor_scalar(nt_f[:, 0, :], nt_f[:, 0, :], -1.0, 0.0, ALU.add, ALU.max))
                q.did(nc.vector.tensor_copy(nt_i[:, :], nt_f[:, 0, :]))
                q.did(nc.vector.tensor_scalar(nt_f[:, 1, :], nb, 0.5, None, ALU.add))
                q.did(nc.vector.tensor_scalar(nt_f[:, 2, :], nb, -0.5, None, ALU.add))
                v.wait_ge(S(f"nt_counted{o}"), g * (2 * BPG) + 2 * BPG)
                q.did(nc.vector.tensor_scalar(nt_c[:, :, :], nt_c[:, :, :], 0.5, T / 2, ALU.mult, ALU.add))
                q.wait()
                q.did(nc.vector.tensor_tensor(nt_f[:, 3, :], nt_c[:, 0, :], nt_c[:, 1, :], ALU.is_gt))
                q.did(nc.vector.tensor_scalar(nt_f[:, 4, :], nt_c[:, 1, :], 0.0, None, ALU.is_equal))
                q.did(nc.vector.scalar_tensor_tensor(out=nt_f[:, 5, :], in0=nt_f[:, 0, :], scalar=float(T), in1=nt_c[:, 0, :],
                                                     op0=ALU.mult, op1=ALU.add))
                q.wait()
                q.do(nc.vector.scalar_tensor_tensor(out=nt_f[:, 5, :], in0=nt_f[:, 5, :], scalar=-float(EP + 1), in1=nt_f[:, 3, :],
                                                    op0=ALU.add, op1=ALU.mult))
                q.did(nc.vector.tensor_scalar(endix[:, bass.ds(g * BPG, BPG)], nt_f[:, 5, :], float(EP), None, ALU.add))
                nc.vector.tensor_tensor(nt_f[:, 4, :], nt_f[:, 4, :], rows4[:, :, T], ALU.mult).then_inc(S(f"nt_tail{o}"), 1)
                v.wait_ge(S(f"nt_tail{o}"), g * 3 + 1)
                nc.vector.tensor_tensor(nt_f[:, 4, :], nt_f[:, 4, :], nt_f[:, 3, :], ALU.mult).then_inc(S(f"nt_tail{o}"), 1)
                v.wait_ge(S(f"nt_tail{o}"), g * 3 + 2)
                nc.vector.scalar_tensor_tensor(out=nt_f[:, 0, :], in0=nt_f[:, 0, :], scalar=-float(P), in1=nt_f[:, 4, :],
                                               op0=ALU.add, op1=ALU.mult).then_inc(S(f"nt_tail{o}"), 1)
                v.wait_ge(S(f"nt_tail{o}"), g * 3 + 3)
                q.did(nc.vector.tensor_scalar(carix[:, bass.ds(g * BPG, BPG)], nt_f[:, 0, :], float(P), None, ALU.add))
                q.wait()
                assert q.k == NT_STEPS, q.k
            v.sem_inc(S("nodes_ready"), 1)

        def nodes_pool(g_, o):
            g_.wait_ge(S("keyrow_out"), 16 * (o + 1))
            if o == 0:
                for b in range(2):
                    g_.wait_ge(*PB.on(f"sent{b}", 16 * (IT // 2) + 16))
            with g_.Fori(0, NG) as g:
                g_.wait_ge(S(f"nt_steps{o}"), g * NT_STEPS + 6)
                g_.sem_inc(S("pool_go"), 1)
                for j in range(BPG):
                    g_.indirect_dma_start(rows4[:, j, :], None, keyrow_t[o], bass.IndirectOffsetOnAxis(ap=nt_i[:, j:j + 1], axis=0))\
                      .then_inc(S(f"nt_in{o}"), 16)

        def nodes_act(act, o):
            with act.Fori(0, NG) as g:
                act.wait_ge(S(f"nt_in{o}"), g * (16 * BPG) + 16 * BPG)
                act.wait_ge(S(f"nt_steps{o}"), g * NT_STEPS + 6)
                for j in range(BPG):
                    for k in range(2):
                        nc.scalar.activation(rsign[:, 0:T], rows4[:, j, 0:T], ACT.Sign, scale=-1.0, bias=nt_f[:, 1 + k, j:j + 1],
                                             accum_out=nt_c[:, k, j:j + 1]).then_inc(S(f"nt_counted{o}"), 1)
                        act.wait_ge(S(f"nt_counted{o}"), g * (2 * BPG) + 2 * j + k + 1)

        def payload_in(sp, c):
            sp.wait_ge(S("attr_free"), c + 1)
            r0 = c * (P * KE)
            if isinstance(c, int) and c == NPAY - 1:
                left = E - c * P * KE
                w = left // KE
                parts = [(0, w // 16 * 16, KE), (w // 16 * 16, w, KE), (w, w + 1, left - w * KE)]
            else:
                parts = [(0, P, KE)]
            for j, (a, z, k) in enumerate(parts):
                done = S("attr_in") if j == len(parts) - 1 else S("attr_part")
                if j and j == len(parts) - 1:
                    sp.wait_ge(S("attr_part"), 16 * 3 * j)
                r, n = r0 + a * KE, (z - a) * k
                sp.dma_start(attr[a:z, 0:k, :], A["edge_attr_64"][bass.ds(r, n), :].rearrange("(p t) w -> p t w", t=k)).then_inc(done, 16)
                sp.dma_start(pcol_i[a:z, 0:k], A["src"][bass.ds(r, n)].rearrange("(p t) -> p t", t=k)).then_inc(done, 16)
                sp.dma_start(pcol_f[a:z, 0:k], A["edge_weight"][bass.ds(r, n)].rearrange("(p t) -> p t", t=k)).then_inc(done, 16)

        def payload_out(sp, c):
            sp.wait_ge(S("pay_made"), c + 1)
            sp.dma_start(pay_dram[bass.ds(c * (P * KE), P * KE), :].rearrange("(p t) w -> p t w", t=KE), pay0[:, :, :]).then_inc(S("pay_out"), 16)

        def payload_pe(pe):
            with pe.Fori(0, NPAY) as c:
                pe.wait_ge(S("attr_in"), c * 48 + 48)
                for u in range(KE // 2):
                    ins = nc.tensor.transpose(psB[:, u // 4, (u % 4) * P:(u % 4 + 1) * P],
                                              attr[:, 2 * u:2 * u + 2, :].rearrange("p a w -> p (a w)"), ident[:, :])
                ins.then_inc(S("attr_tr"), 1)
                pe.wait_ge(S("attrT_in"), c + 1)
                for u in range(KE // 2):
                    nc.tensor.matmul(psD[:, u * 16:(u + 1) * 16], attrT[:, u, :], we2[:, :], start=True, stop=False)
                    ins = nc.tensor.matmul(psD[:, u * 16:(u + 1) * 16], ones[0:1, :], be2[:, :], start=False, stop=True)
                ins.then_inc(S("pay_mm"), 1)

        def payload_act(act, c):
            act.wait_ge(S("attr_tr"), c + 1)
            nc.scalar.copy(attrT[:, :, :].rearrange("p a b -> p (a b)"), psB[:, :, :].rearrange("p a b -> p (a b)")[:, 0:KE // 2 * P])\
              .then_inc(S("attrT_in"), 1)
            act.wait_ge(S("pay_out"), c * 16 + 16)
            nc.scalar.copy(pay0[:, :, 0:1].rearrange("p t w -> p (t w)"), pcol_i[:, :]).then_inc(S("pay_cols"), 1)
            nc.scalar.copy(pay0[:, :, 1:2].rearrange("p t w -> p (t w)"), pcol_f[:, :]).then_inc(S("pay_cols"), 1)
            act.wait_ge(S("pay_cols"), c * 2 + 2)
            act.sem_inc(S("attr_free"), 1)
            act.wait_ge(S("pay_mm"), c + 1)
            nc.scalar.copy(pay0[:, :, 2:10], psD[:, 0:KE // 2 * 16].rearrange("p (t w) -> p t w", w=8)).then_inc(S("pay_made"), 1)

        def paysort_pool(g_):
            g_.wait_ge(S("ix_ready"), 2)
            g_.wait_ge(S("pay_out"), 16 * NPAY + 16)
            with g_.Fori(0, IT // 2) as i:
                for b in range(2):
                    g_.wait_ge(S(f"paya_out{b}"), i * 16 + 16)
                    g_.wait_ge(S(f"paya_cols{b}"), i * 2 + 1)
                    g_.sem_inc(S("pool_go"), 1)
                    g_.tensor_copy(ix_s[b][:, :], eid_a[:, bass.ds(i * (2 * K) + b * K, K)]).then_inc(S(f"paya_ix{b}"), 1)
                    g_.wait_ge(S(f"paya_ix{b}"), i + 1)
                    g_.sem_inc(S("pool_go"), 1)
                    for k in range(K):
                        g_.indirect_dma_start(pay[b][:, k, :], None, pay_dram, bass.IndirectOffsetOnAxis(ap=ix_s[b][:, k:k + 1], axis=0))\
                          .then_inc(S(f"paya_in{b}"), 16)

        def paysort_dve(v):
            for b in range(2):
                v.sem_inc(S(f"paya_cols{b}"), 1)
            with v.Fori(0, IT // 2) as i:
                for b in range(2):
                    v.wait_ge(S(f"paya_in{b}"), i * (16 * K) + 16 * K)
                    cols = bass.ds(i * (2 * K) + b * K, K)
                    nc.vector.tensor_copy(oth_i[:, cols], pay[b][:, :, 0]).then_inc(S(f"paya_cols{b}"), 1)
                    nc.vector.tensor_copy(ew[:, cols], pay[b][:, :, 1]).then_inc(S(f"paya_cols{b}"), 1)
            for b in range(2):
                v.wait_ge(S(f"paya_cols{b}"), IT + 1)
            v.sem_inc(S("ix_ready"), 1)

        def paysort_sp(sp):
            for b in range(2):
                sp.sem_inc(S(f"paya_out{b}"), 16)
            with sp.Fori(0, IT // 2) as i:
                for b in range(2):
                    sp.wait_ge(S(f"paya_in{b}"), i * (16 * K) + 16 * K)
                    sp.dma_start(paya_dram.rearrange("(p t) w -> p t w", t=T)[:, bass.ds(i * (2 * K) + b * K, K), :],
                                 pay[b][:, :, :]).then_inc(S(f"paya_out{b}"), 16)

        def pass_pool(g_, q):
            both = q.tabd is not None
            far, near = oth_i, seg_i
            fars, neard = q.tabs, q.tabd
            wd_s = fars.shape[1]
            for nm in q.needs:
                g_.wait_ge(S(nm[0]), nm[1])
            with g_.Fori(0, IT // 2) as i:
                for b in range(2):
                    g_.wait_ge(*q.on(f"free{b}", i + 1))
                    g_.sem_inc(S("pool_go"), 1)
                    cols = bass.ds(i * (2 * K) + b * K, K)
                    g_.tensor_copy(ix_s[b][:, :], far[:, cols]).then_inc(q.s(f"ix{b}"), 1)
                    g_.tensor_copy(ix_d[b][:, :], near[:, cols]).then_inc(q.s(f"ix{b}"), 1)
                    g_.wait_ge(*q.on(f"ix{b}", i * 2 + 2))
                    g_.sem_inc(S("pool_go"), 1)
                    for k in range(K):
                        g_.indirect_dma_start(rows_s[b][:, k, 0:wd_s], None, fars, bass.IndirectOffsetOnAxis(ap=ix_s[b][:, k:k + 1], axis=0))\
                          .then_inc(q.own(f"rows{b}"), 16)
                        if both:
                            g_.indirect_dma_start(rows_d[b][:, k, 0:neard.shape[1]], None, neard,
                                                  bass.IndirectOffsetOnAxis(ap=ix_d[b][:, k:k + 1], axis=0)).then_inc(q.own(f"rows{b}"), 16)

        def heads(t, q):
            return t[:, 0:q.H, :]

        def pass_dve(v, q):
            H, dh, F = q.H, q.dh, q.F
            nrow = 2 if q.tabd is not None else 1
            for b in range(2):
                v.sem_inc(q.s(f"free{b}"), 1)
            f2 = lambda a: a.rearrange("p h t -> p (h t)")
            stv = st[:, 0:F * (K + 1)].rearrange("p (f t) -> p f t", t=K + 1)
            bvv = bv[:, 0:F * (K + 1)].rearrange("p (f t) -> p f t", t=K + 1)
            bvh = bvv.rearrange("p (h j) t -> p h j t", h=H)
            p0 = Seq(v, q.s("prep"), q.base("prep"))
            p0.did(nc.vector.memset(stv, 0.0))
            p0.do(nc.vector.memset(m_ext[:, :, :], -BIG))
            with v.Fori(0, IT // 2) as i:
                for b in range(2):
                    c = Seq(v, q.s("steps"), q.base("steps") + b * q.steps, i, 2 * q.steps)
                    t0 = i * (2 * K) + b * K
                    cols = bass.ds(t0, K)
                    rs, rd = rows_s[b], rows_d[b]
                    s = heads(s_ext, q)[:, :, 1:K + 1]
                    v.wait_ge(q.own(f"rows{b}"), i * (16 * K * nrow) + 16 * K * nrow)
                    if q in (PB, PA, P1):
                        c.do(nc.vector.tensor_tensor(rd[:, :, :], rs[:, :, 0:D], rd[:, :, :], ALU.mult))
                        c.did(nc.vector.tensor_reduce(s.rearrange("p h t -> p t h"), rd[:, :, :].rearrange("p t (h d) -> p t h d", h=H), AX.X, ALU.add))
                    if q is PB:
                        c.wait()
                        v.sem_inc(q.s(f"free{b}"), 1)
                    if q is PA:
                        c.wait()
                        c.did(nc.vector.tensor_tensor(heads(ww, q), s, rs[:, :, 2 * D:2 * D + H].rearrange("p t h -> p h t"), ALU.subtract))
                    if q is P1:
                        v.wait_ge(S(f"bias_in{b}"), i * 16 + 16)
                        c.wait()
                        c.do(nc.vector.scalar_tensor_tensor(out=s, in0=s, scalar=float(dh) ** -0.5, in1=pay[b][:, :, 2:2 + H].rearrange("p t h -> p h t"),
                                                            op0=ALU.mult, op1=ALU.add))
                        v.sem_inc(S(f"bias_used{b}"), 1)
                    if q is P2:
                        c.do(nc.vector.tensor_tensor(s, rs[:, :, D:D + H].rearrange("p t h -> p h t"), rd[:, :, 0:H].rearrange("p t h -> p h t"), ALU.add))
                        c.do(nc.vector.scalar_tensor_tensor(out=s, in0=s, scalar=0.2, in1=s, op0=ALU.mult, op1=ALU.max))
                    if q.soft:
                        smx = heads(s_max, q) if q is P2 else heads(s_ext, q)
                        if q is P2:
                            c.did(nc.vector.tensor_scalar(smx[:, :, 1:K + 1], s, 0.0, None, ALU.max))
                        rsh, mx = heads(rst, q), heads(m_ext, q)
                        c.did(nc.vector.tensor_copy(smx[:, :, 0:1], mx[:, :, K:K + 1]))
                        c.did(nc.vector.tensor_copy(rsh[:, :, 1:K + 1], restart[:, cols].unsqueeze(1).to_broadcast([P, H, K])))
                        v.wait_ge(*q.on("laid", i * 2 + b + 1))
                        c.wait()
                        c.do(nc.vector.tensor_tensor_scan(f2(mx), f2(rsh), f2(smx), -BIG, ALU.add, ALU.max))
                        c.did(nc.vector.tensor_tensor(heads(dtmp, q), mx[:, :, 0:K], mx[:, :, 1:K + 1], ALU.subtract))
                        c.did(nc.vector.tensor_tensor(heads(ww, q), s, mx[:, :, 1:K + 1], ALU.subtract))
                        c.wait()
                        c.did(nc.vector.tensor_tensor(heads(dd, q)[:, :, 1:K + 1], heads(dtmp, q), rsh[:, :, 1:K + 1], ALU.add))
                    else:
                        c.did(nc.vector.tensor_copy(dd[:, 0, 1:K + 1], restart[:, cols]))
                    c.wait()
                    v.sem_inc(q.s("arg"), 1)
                    if q is P3:
                        c.did(nc.vector.tensor_tensor(bvv[:, :, 1:K + 1], rs[:, :, 0:D].rearrange("p t f -> p f t"),
                                                      ew[:, cols].unsqueeze(1).to_broadcast([P, D, K]), ALU.mult))
                    elif q is PA:
                        v.wait_ge(*q.on("expw", i * 2 + b + 1))
                        c.did(nc.vector.tensor_tensor(bvh[:, :, :, 1:K + 1], rs[:, :, D:2 * D].rearrange("p t (h j) -> p h j t", h=H),
                                                      heads(ww, q).unsqueeze(2).to_broadcast([P, H, 32, K]), ALU.mult))
                    elif dh:
                        v.wait_ge(*q.on("expw", i * 2 + b + 1))
                        off = D if q is P1 else 0
                        c.did(nc.vector.tensor_tensor(bvh[:, :, 0:dh, 1:K + 1], rs[:, :, off:off + D].rearrange("p t (h j) -> p h j t", h=H),
                                                      bvh[:, :, dh:dh + 1, 1:K + 1].to_broadcast([P, H, dh, K]), ALU.mult))
                    c.did(nc.vector.tensor_copy(bvv[:, :, 0:1], stv[:, :, K:K + 1]))
                    c.wait()
                    if q is not PB:
                        v.sem_inc(q.s(f"free{b}"), 1)
                    v.wait_ge(*q.on("decay", i * 2 + b + 1))
                    if not q.soft:
                        v.wait_ge(*q.on("laid", i * 2 + b + 1))
                    c.do(nc.vector.tensor_tensor_scan(st[:, 0:F * (K + 1)], abig[:, 0:F * (K + 1)], bv[:, 0:F * (K + 1)], 0.0, ALU.mult, ALU.add))
                    v.sem_inc(q.s("scanned"), 1)
                    assert c.k == q.steps, (q.name, c.k, q.steps)

        def pass_act(act, q):
            H, dh, F, W = q.H, q.dh, q.F, q.W
            act.sem_inc(q.s("laid"), 1)
            bvh = bv[:, 0:F * (K + 1)].rearrange("p (h j t) -> p h j t", h=H, t=K + 1)
            stv = st[:, 0:F * (K + 1)].rearrange("p (f t) -> p f t", t=K + 1)
            with act.Fori(0, IT // 2) as i:
                if q is PB:
                    payload_act(act, i)
                for b in range(2):
                    act.wait_ge(*q.on("arg", i * 2 + b + 1))
                    if q.soft:
                        nc.scalar.activation(bvh[:, :, dh, 1:K + 1], heads(ww, q), ACT.Exp).then_inc(q.s("expw"), 1)
                        nc.scalar.activation(abig[:, 0:F * (K + 1)].rearrange("p (h j t) -> p h j t", h=H, t=K + 1),
                                             heads(dd, q).unsqueeze(2).to_broadcast([P, H, dh + 1, K + 1]), ACT.Exp).then_inc(q.s("decay"), 1)
                    else:
                        if q is PA:
                            nc.scalar.activation(heads(ww, q), heads(ww, q), ACT.Exp).then_inc(q.s("expw"), 1)
                        nc.scalar.activation(abig[:, 0:F * (K + 1)].rearrange("p (f t) -> p f t", t=K + 1),
                                             dd[:, 0:1, :].to_broadcast([P, F, K + 1]), ACT.Exp).then_inc(q.s("decay"), 1)
                    act.wait_ge(*q.on("scanned", i * 2 + b + 1))
                    act.wait_ge(*q.on(f"sent{b}", i * 16 + 16))
                    pr = psrow[b][:, 0:K * W].rearrange("p (t w) -> p t w", w=W)
                    ins = nc.scalar.copy(pr[:, :, 0:F], stv[:, :, 1:K + 1].rearrange("p f t -> p t f"))
                    if q.soft:
                        ins = nc.scalar.copy(pr[:, :, F:F + H], heads(m_ext, q)[:, :, 1:K + 1].rearrange("p h t -> p t h"))
                    if q is PB:
                        ins = nc.scalar.copy(pr[:, :, F + H:F + H + 1].rearrange("p t w -> p (t w)"), cnt[:, bass.ds(i * (2 * K) + b * K, K)])
                    ins.then_inc(q.s("laid"), 1)
                    act.wait_ge(*q.on("laid", i * 2 + b + 2))
                    act.sem_inc(q.s(f"laid{b}"), 1)

        def pass_store(sp, q, i, b):
            sp.wait_ge(*q.on(f"laid{b}", i + 1))
            sp.dma_start(q.ps[0:EP, :].rearrange("(p t) w -> p t w", t=T)[:, bass.ds(i * (2 * K) + b * K, K), :],
                         psrow[b][:, 0:K * q.W].rearrange("p (t w) -> p t w", w=q.W)).then_inc(q.s(f"sent{b}"), 16)

        def bias_load(sp, n, b):
            sp.dma_start(pay[b][:, :, :], paya_dram.rearrange("(p t) w -> p t w", t=T)[:, bass.ds(n * (2 * K) + b * K, K), :])\
              .then_inc(S(f"bias_in{b}"), 16)

        def pass_sp(sp, q):
            for b in range(2):
                sp.sem_inc(q.s(f"sent{b}"), 16)
            if q is PB:
                sp.sem_inc(S("pay_out"), 16)
                with sp.Fori(0, NPAY - 1) as i:
                    payload_in(sp, i)
                    for b in range(2):
                        pass_store(sp, q, i, b)
                    payload_out(sp, i)
                payload_in(sp, NPAY - 1)
                for b in range(2):
                    pass_store(sp, q, NPAY - 1, b)
                payload_out(sp, NPAY - 1)
                return
            if q is P1:
                for b in range(2):
                    sp.wait_ge(S(f"paya_out{b}"), 16 * (IT // 2) + 16)
                    bias_load(sp, 0, b)
                with sp.Fori(0, IT // 2 - 1) as i:
                    for b in range(2):
                        sp.wait_ge(S(f"bias_used{b}"), i + 1)
                        bias_load(sp, i + 1, b)
                        pass_store(sp, q, i, b)
                for b in range(2):
                    pass_store(sp, q, IT // 2 - 1, b)
                return
            with sp.Fori(0, IT // 2) as i:
                for b in range(2):
                    pass_store(sp, q, i, b)

        def carry_dve(v, q):
            H, dh, F = q.H, q.dh, q.F
            c = Seq(v, q.own("carry_steps"))
            stv = st[:, 0:F * (K + 1)].rearrange("p (f t) -> p f t", t=K + 1)
            v.wait_ge(*q.on("laid", IT + 1))
            c.do(nc.vector.tensor_copy(cst[:, 0:F].unsqueeze(2), stv[:, :, K:K + 1]))
            if q is PB:
                c.do(nc.vector.tensor_copy(cst[:, F:F + 1], cnt[:, T - 1:T]))
            if q.soft:
                dw = dwide[:, 0:H * P].rearrange("p (h r) -> p h r", h=H)
                c.do(nc.vector.tensor_tensor(dw, ident[:, :].unsqueeze(1).to_broadcast([P, H, P]),
                                             heads(m_ext, q)[:, :, K:K + 1].to_broadcast([P, H, P]), ALU.mult))
                v.sem_inc(q.s("tails"), 1)
                v.wait_ge(*q.on("maxrows", 1))
                pm = psC[:, 0:H * P].rearrange("p (h r) -> p h r", h=H)
                c.do(nc.vector.tensor_tensor(dw, pm, bias2[:, :].unsqueeze(1).to_broadcast([P, H, P]), ALU.add))
                c.do(nc.vector.tensor_reduce(mcar[:, 0:H], dw, AX.X, ALU.max))
                c.do(nc.vector.tensor_tensor(dw, dw, mcar[:, 0:H].unsqueeze(2).to_broadcast([P, H, P]), ALU.subtract))
                v.sem_inc(q.s("cw_arg"), 1)
                c.did(nc.vector.tensor_copy(ctst[:, F:F + H], mcar[:, 0:H]))
            else:
                v.sem_inc(q.s("tails"), 1)
            if q is PB:
                c.did(nc.vector.memset(ctst[:, F + H + 1:q.W], 0.0))
            v.wait_ge(*q.on("carried", 1))
            if q is PB:
                c.did(nc.vector.tensor_copy(ctst[:, F + H:F + H + 1], psD[:, F:F + 1]))
            c.did(nc.vector.tensor_copy(ctst[:, 0:F], psD[:, 0:F]))
            c.wait()
            v.sem_inc(q.s("carry_made"), 1)

        def carry_pe(pe, q):
            H, dh, F = q.H, q.dh, q.F
            pe.wait_ge(*q.on("tails", 1))
            if not q.soft:
                nc.tensor.matmul(psD[:, 0:F], contT[:, :], cst[:, 0:F], start=True, stop=True).then_inc(q.s("carried"), 1)
                return
            for a in range(0, H * P, 512):
                ins = nc.tensor.matmul(psC[:, a:a + 512], ones[:, :], dwide[:, a:a + 512], start=True, stop=True)
            ins.then_inc(q.s("maxrows"), 1)
            pe.wait_ge(*q.on("cw", 1))
            for h in range(H):
                ins = nc.tensor.transpose(psB[:, h // 4, (h % 4) * P:(h % 4 + 1) * P], wwide[:, h * P:(h + 1) * P], ident[:, :])
            ins.then_inc(q.s("cwT"), 1)
            pe.wait_ge(*q.on("cwT_in", 1))
            for h in range(H):
                f = slice(h * (dh + 1), (h + 1) * (dh + 1))
                ins = nc.tensor.matmul(psD[:, f], dwide[:, h * P:(h + 1) * P], cst[:, f], start=True, stop=True)
            if q is PB:
                ins = nc.tensor.matmul(psD[:, F:F + 1], contT[:, :], cst[:, F:F + 1], start=True, stop=True)
            ins.then_inc(q.s("carried"), 1)

        def carry_act(act, q):
            if not q.soft:
                return
            n = q.H * P
            act.wait_ge(*q.on("cw_arg", 1))
            nc.scalar.activation(wwide[:, 0:n], dwide[:, 0:n], ACT.Exp).then_inc(q.s("cw"), 1)
            act.wait_ge(*q.on("cwT", 1))
            nc.scalar.copy(dwide[:, 0:n], psB[:, :, :].rearrange("p a b -> p (a b)")[:, 0:n]).then_inc(q.s("cwT_in"), 1)

        def carry_sp(sp, q):
            sp.wait_ge(*q.on("carry_made", 1))
            sp.dma_start(q.ct[0:P, :], ctst[:, 0:q.W]).then_inc(q.s("carry_out"), 16)

        NN = -(-N // P)

        def ends_pool(g_, q):
            for b in range(2):
                g_.wait_ge(*q.on(f"sent{b}", 16 * (IT // 2) + 16))
            g_.wait_ge(*q.on("carry_out", 16))
            g_.wait_ge(S("dummy_rows"), 16 * NDUMMY)
            g_.wait_ge(S("nodes_ready"), 1 if q is PB else 2)
            with g_.Fori(0, NG) as g:
                g_.wait_ge(*q.on("ends_free", g + 1))
                g_.sem_inc(S("pool_go"), 1)
                g_.tensor_copy(fe_i[:, :], endix[:, bass.ds(g * BPG, BPG)]).then_inc(q.s("fix"), 1)
                g_.tensor_copy(fc_i[:, :], carix[:, bass.ds(g * BPG, BPG)]).then_inc(q.s("fix"), 1)
                g_.wait_ge(*q.on("fix", g * 2 + 2))
                g_.sem_inc(S("pool_go"), 1)
                for j in range(BPG):
                    g_.indirect_dma_start(end4[:, j, 0:q.W], None, q.ps, bass.IndirectOffsetOnAxis(ap=fe_i[:, j:j + 1], axis=0)).then_inc(q.s("ends_in"), 16)
                    g_.indirect_dma_start(car4[:, j, 0:q.W], None, q.ct, bass.IndirectOffsetOnAxis(ap=fc_i[:, j:j + 1], axis=0)).then_inc(q.s("ends_in"), 16)

        MERGE = {True: 7, False: 1}

        def merge_dve(v, q, g, c):
            H, dh, F = q.H, q.dh, q.F
            v.wait_ge(*q.on("ends_in", g * (32 * BPG) + 32 * BPG))
            if q.soft:
                e, r = (t[:, :, 0:F].rearrange("p j (h d) -> p j h d", h=H) for t in (end4, car4))
                me, mr = end4[:, :, F:F + H], car4[:, :, F:F + H]
                m = mx4[:, :, :, 0:H]
                wide = lambda k: m[:, k].unsqueeze(3).to_broadcast([P, BPG, H, dh + 1])
                c.do(nc.vector.tensor_tensor(m[:, 0], me, mr, ALU.max))
                c.did(nc.vector.tensor_tensor(m[:, 1], me, m[:, 0], ALU.subtract))
                c.did(nc.vector.tensor_tensor(m[:, 2], mr, m[:, 0], ALU.subtract))
                c.wait()
                v.sem_inc(q.s("mg_arg"), 1)
                v.wait_ge(*q.on("mg_exp", g * 2 + 2))
                c.did(nc.vector.tensor_tensor(e, e, wide(1), ALU.mult))
                c.do(nc.vector.tensor_tensor(r, r, wide(2), ALU.mult))
                c.do(nc.vector.tensor_tensor(e, e, r, ALU.add))
                c.do(nc.vector.tensor_scalar(m[:, 1], end4[:, :, 0:F].rearrange("p j (h d) -> p j h d", h=H)[:, :, :, dh],
                                             1e-10, None, ALU.max if q is PB else ALU.add))
            else:
                c.do(nc.vector.tensor_tensor(end4[:, :, 0:F], end4[:, :, 0:F], car4[:, :, 0:F], ALU.add))

        def merge_act(act, q, g):
            if q.soft:
                act.wait_ge(*q.on("mg_arg", g + 1))
                for k in (1, 2):
                    nc.scalar.activation(mx4[:, k, :, 0:q.H], mx4[:, k, :, 0:q.H], ACT.Exp).then_inc(q.s("mg_exp"), 1)

        def stats_dve(v):
            q = PB
            v.sem_inc(q.s("ends_free"), 1)
            per = MERGE[True] + 4
            with v.Fori(0, NG) as g:
                c = Seq(v, S("stats_steps"), 0, g, per)
                merge_dve(v, q, g, c)
                n = q.F + q.H
                c.did(nc.vector.tensor_tensor(mx4[:, 2, :, 0:1], end4[:, :, n:n + 1], car4[:, :, n:n + 1], ALU.add))
                c.do(nc.vector.reciprocal(mx4[:, 1, :, 0:H0], mx4[:, 1, :, 0:H0]))
                c.do(nc.vector.tensor_tensor(mx4[:, 1, :, 0:H0], mx4[:, 1, :, 0:H0], mx4[:, 2, :, 0:1].to_broadcast([P, BPG, H0]), ALU.mult))
                v.wait_ge(S("qm_in"), g * 32 + 32)
                hv = hst2[:, :, :].rearrange("p j (h d) -> p j h d", h=H0)
                c.do(nc.vector.tensor_tensor(hv, hv, mx4[:, 1, :, 0:H0].unsqueeze(3).to_broadcast([P, BPG, H0, D // H0]), ALU.mult))
                assert c.k == per
                v.sem_inc(S("qm_made"), 1)
                v.sem_inc(q.s("ends_free"), 1)
                v.wait_ge(S("qm_free"), g + 2)
            v.sem_inc(S("stats_done"), 1)

        def stats_act(act):
            with act.Fori(0, NG) as g:
                merge_act(act, PB, g)

        def stats_sp(sp):
            sp.sem_inc(S("qm_free"), 1)
            sp.wait_ge(S("j0_out"), 16 * 3 * NG)
            with sp.Fori(0, NG) as g:
                sp.wait_ge(S("qm_free"), g + 1)
                sp.dma_start(hst[:, :, :], grows(q0_t, g)).then_inc(S("qm_in"), 16)
                sp.dma_start(hst2[:, :, :], grows(m0_t, g)).then_inc(S("qm_in"), 16)
                sp.wait_ge(S("qm_made"), g + 1)
                sp.dma_start(grows(qm0_t, g)[:, :, 0:D], hst[:, :, :]).then_inc(S("qm_out"), 16)
                sp.dma_start(grows(qm0_t, g)[:, :, D:2 * D], hst2[:, :, :]).then_inc(S("qm_out"), 16)
                sp.dma_start(grows(qm0_t, g)[:, :, 2 * D:2 * D + H0], mx4[:, 0, :, 0:H0]).then_inc(S("qm_out"), 16)
                sp.wait_ge(S("qm_out"), g * 48 + 48)
                sp.sem_inc(S("qm_free"), 1)

        def end0_dve(v):
            q = PA
            v.sem_inc(q.s("ends_free"), 1)
            with v.Fori(0, NG) as g:
                c = Seq(v, S("e0_steps"), 0, g, 2)
                merge_dve(v, q, g, c)
                v.wait_ge(S("e0_tr"), g + 1)
                c.do(nc.vector.tensor_copy(hst[:, :, :], end4[:, :, 0:D]))
                v.sem_inc(q.s("ends_free"), 1)
            c = Seq(v, S("bn_steps"))
            v.wait_ge(S("e0_hid"), NG)
            hid = hT_all[:, 0:N]
            c.do(nc.vector.tensor_reduce(bncol[:, 3:4], hid, AX.X, ALU.add))
            c.do(nc.vector.tensor_scalar(bncol[:, 3:4], bncol[:, 3:4], -1.0 / N, None, ALU.mult))
            c.do(nc.vector.tensor_scalar(hT_all[:, :], hT_all[:, :], bncol[:, 3:4], None, ALU.add))
            v.sem_inc(S("bn_centred"), 1)
            v.wait_ge(S("bn_squares"), 1)
            c.do(nc.vector.tensor_scalar(bncol[:, 4:5], bncol[:, 4:5], 1.0 / N, EPS, ALU.mult, ALU.add))
            v.sem_inc(S("bn_var"), 1)
            v.wait_ge(S("bn_sqrt"), 1)
            c.do(nc.vector.reciprocal(bncol[:, 5:6], bncol[:, 5:6]))
            c.do(nc.vector.tensor_tensor(bncol[:, 5:6], bncol[:, 5:6], bncol[:, 1:2], ALU.mult))
            v.sem_inc(S("bn_scale"), 1)
            with v.Fori(0, NG) as g:
                v.wait_ge(S("e0_mm"), g + 1)
                xg = xsb[:, bass.ds(g * BPG, BPG), :]
                nc.vector.tensor_tensor(xg, xg, psB[:, 0, :].rearrange("p (j d) -> p j d", j=BPG), ALU.add).then_inc(S("e0_added"), 1)
                v.wait_ge(S("e0_added"), g + 2)

        def end0_pe(pe):
            pe.sem_inc(S("e0_tr"), 1)
            with pe.Fori(0, NG) as g:
                pe.wait_ge(S("e0_steps"), g * 2 + 2)
                pe.wait_ge(S("e0_at"), g + 1)
                for j in range(BPG):
                    ins = nc.tensor.transpose(psA[:, j * P:(j + 1) * P], hst[:, j, :], ident[:, :])
                ins.then_inc(S("e0_tr"), 1)
                pe.wait_ge(S("e0_at"), g + 2)
                pe.wait_ge(S("e0_hid0"), g + 1)
                nc.tensor.matmul(psD[:, :], w1_0[:, :], hT[:, 0, :], start=True, stop=True).then_inc(S("e0_w1"), 1)
            with pe.Fori(0, NG) as g:
                pe.wait_ge(S("e0_relu"), g + 1)
                pe.wait_ge(S("e0_added"), g + 1)
                for j in range(BPG):
                    nc.tensor.matmul(psB[:, 0, j * P:(j + 1) * P], hT[:, 1, j * P:(j + 1) * P], w2_0[:, :], start=True, stop=False)
                    ins = nc.tensor.matmul(psB[:, 0, j * P:(j + 1) * P], ones[0:1, :], b2_0[:, :], start=False, stop=True)
                ins.then_inc(S("e0_mm"), 1)

        def end0_act(act):
            act.sem_inc(S("e0_at"), 1)
            act.sem_inc(S("e0_hid0"), 1)
            act.sem_inc(S("e0_added"), 1)
            with act.Fori(0, NG) as g:
                act.wait_ge(S("e0_tr"), g + 2)
                nc.scalar.copy(hT[:, 0, :], psA[:, :]).then_inc(S("e0_at"), 1)
                act.wait_ge(S("e0_w1"), g + 1)
                nc.scalar.activation(hT_all[:, bass.ds(g * GN, GN)], psD[:, :], ACT.Identity, bias=bncol[:, 0:1]).then_inc(S("e0_hid"), 1)
                act.wait_ge(S("e0_hid"), g + 1)
                act.sem_inc(S("e0_hid0"), 1)
            act.wait_ge(S("bn_centred"), 1)
            nc.scalar.activation(work[:, 0:N], hT_all[:, 0:N], ACT.Square, accum_out=bncol[:, 4:5]).then_inc(S("bn_squares"), 1)
            act.wait_ge(S("bn_var"), 1)
            nc.scalar.activation(bncol[:, 5:6], bncol[:, 4:5], ACT.Sqrt).then_inc(S("bn_sqrt"), 1)
            act.wait_ge(S("bn_scale"), 1)
            with act.Fori(0, NG) as g:
                act.wait_ge(S("e0_added"), g + 1)
                nc.scalar.activation(hT[:, 1, :], hT_all[:, bass.ds(g * GN, GN)], ACT.Relu, bias=bncol[:, 2:3], scale=bncol[:, 5:6])\
                  .then_inc(S("e0_relu"), 1)

        def end12_dve(v, q):
            v.sem_inc(q.s("ends_free"), 1)
            per = MERGE[True] + 2
            with v.Fori(0, NG) as g:
                c = Seq(v, q.own("end_steps"), 0, g, per)
                merge_dve(v, q, g, c)
                c.do(nc.vector.reciprocal(mx4[:, 1, :, 0:q.H], mx4[:, 1, :, 0:q.H]))
                if q is P1:
                    v.wait_ge(S("e1_tr"), g + 1)
                c.do(nc.vector.tensor_tensor(hst[:, :, :].rearrange("p j (h d) -> p j h d", h=q.H),
                                             end4[:, :, 0:q.F].rearrange("p j (h d) -> p j h d", h=q.H)[:, :, :, 0:q.dh],
                                             mx4[:, 1, :, 0:q.H].unsqueeze(3).to_broadcast([P, BPG, q.H, q.dh]), ALU.mult))
                v.sem_inc(q.s("ends_free"), 1)
                assert c.k == per, c.k
                xg = xsb[:, bass.ds(g * BPG, BPG), :]
                if q is P1:
                    v.wait_ge(S("e1_mm"), g + 1)
                    nc.vector.tensor_tensor(xg, xg, psB[:, 0, :].rearrange("p (j d) -> p j d", j=BPG), ALU.add).then_inc(S("e1_added"), 1)
                    v.wait_ge(S("e1_added"), g + 1)
                else:
                    nc.vector.tensor_tensor(xg, xg, hst[:, :, :], ALU.add).then_inc(S("e2_added"), 1)
                    v.wait_ge(S("e2_added"), g + 1)

        def end1_pe(pe):
            pe.sem_inc(S("e1_tr"), 1)
            per = MERGE[True] + 2
            with pe.Fori(0, NG) as g:
                pe.wait_ge(P1.own("end_steps"), g * per + per)
                for j in range(BPG):
                    ins = nc.tensor.transpose(psA[:, j * P:(j + 1) * P], hst[:, j, :], ident[:, :])
                ins.then_inc(S("e1_tr"), 1)
                pe.wait_ge(S("e1_at"), g + 1)
                for j in range(BPG):
                    nc.tensor.matmul(psB[:, 0, j * P:(j + 1) * P], hT[:, 0, j * P:(j + 1) * P], wo_1[:, :], start=True, stop=False)
                    ins = nc.tensor.matmul(psB[:, 0, j * P:(j + 1) * P], ones[0:1, :], bo_1[:, :], start=False, stop=True)
                ins.then_inc(S("e1_mm"), 1)

        def end12_act(act, q):
            with act.Fori(0, NG) as g:
                merge_act(act, q, g)
                if q is P1:
                    act.wait_ge(S("e1_tr"), g + 2)
                    nc.scalar.copy(hT[:, 0, :], psA[:, :]).then_inc(S("e1_at"), 1)

        def weights3_pe(pe):
            pe.wait_ge(S("loaded"), 16 * NLOADS)
            pe.wait_ge(S("consts"), CONSTS)
            for j in range(2):
                ins = nc.tensor.transpose(psA[:, j * P:(j + 1) * P], w3raw[:, j, :], ident[:, :])
            ins.then_inc(S("w3_tr"), 1)
            pe.wait_ge(S("w3_in"), 1)

        def weights3_act(act):
            act.wait_ge(S("w3_tr"), 1)
            nc.scalar.copy(w3t[:, :, :].rearrange("p a b -> p (a b)"), psA[:, 0:2 * P]).then_inc(S("w3_in"), 1)

        E3 = 6

        def end3_dve(v):
            q = P3
            v.sem_inc(q.s("ends_free"), 1)
            with v.Fori(0, NG) as g:
                c = Seq(v, S("e3_steps"), 0, g, E3)
                merge_dve(v, q, g, c)
                v.wait_ge(S("h3_in"), g * 16 + 16)
                v.wait_ge(S("y_out"), g * 16 + 16)
                c.did(nc.vector.tensor_tensor(hst[:, :, :], end4[:, :, 0:D], hst2[:, :, :], ALU.add))
                c.do(nc.vector.tensor_tensor(end4[:, :, 0:D], end4[:, :, 0:D], hst2[:, :, :], ALU.mult))
                v.sem_inc(S("h3_free"), 1)
                v.wait_ge(S("e3_mm"), g + 1)
                c.do(nc.vector.tensor_copy(hst[:, :, :], psB[:, 2, :].rearrange("p (j d) -> p j d", j=BPG)))
                v.sem_inc(q.s("ends_free"), 1)
                c.do(nc.vector.scalar_tensor_tensor(out=hst[:, :, :], in0=hst[:, :, :], scalar=0.2, in1=hst[:, :, :], op0=ALU.mult, op1=ALU.max))
                c.do(nc.vector.tensor_tensor(hst[:, :, :], hst[:, :, :], xsb[:, bass.ds(g * BPG, BPG), :], ALU.add))
                assert c.k == E3, c.k

        def end3_pe(pe):
            with pe.Fori(0, NG) as g:
                pe.wait_ge(S("e3_steps"), g * E3 + 3)
                for u, t in ((0, hst), (1, end4)):
                    for j in range(BPG):
                        ins = nc.tensor.transpose(psB[:, u, j * P:(j + 1) * P], t[:, j, 0:D], ident[:, :])
                ins.then_inc(S("e3_tr"), 1)
                pe.wait_ge(S("e3_at"), g + 1)
                for j in range(BPG):
                    o = psB[:, 2, j * P:(j + 1) * P]
                    for u in range(2):
                        nc.tensor.matmul(o, hT[:, u, j * P:(j + 1) * P], w3t[:, u, :], start=(u == 0), stop=False)
                        ins = nc.tensor.matmul(o, ones[0:1, :], b3[:, u, :], start=False, stop=(u == 1))
                ins.then_inc(S("e3_mm"), 1)

        def end3_act(act):
            with act.Fori(0, NG) as g:
                act.wait_ge(S("e3_tr"), g + 1)
                nc.scalar.copy(hT[:, :, :], psB[:, 0:2, :]).then_inc(S("e3_at"), 1)

        def end3_sp(sp):
            sp.sem_inc(S("h3_free"), 1)
            sp.sem_inc(S("y_out"), 16)
            sp.wait_ge(S("j3_out"), 16 * NG)

            def group(g):
                sp.wait_ge(S("h3_free"), g + 1)
                sp.dma_start(hst2[:, :, :], grows(x3_t, g)).then_inc(S("h3_in"), 16)
                sp.wait_ge(S("e3_steps"), (g + 1) * E3)

            with sp.Fori(0, NG - 1) as g:
                group(g)
                sp.dma_start(grows(out, g), hst[:, :, :]).then_inc(S("y_out"), 16)
            group(NG - 1)
            r0 = (NG - 1) * GN
            whole, rest = (N - r0) // P, (N - r0) % P
            if whole:
                sp.dma_start(out[r0:r0 + whole * P, :].rearrange("(j p) w -> p j w", p=P), hst[:, 0:whole, :]).then_inc(S("y_out"), 16)
            sp.dma_start(out[r0 + whole * P:N, :], hst[0:rest, whole, :]).then_inc(S("y_out"), 16)
            sp.wait_ge(S("y_out"), 16 * NG + 16 * (2 if whole else 1))

        block = ctx.enter_context(nc.Block())

        @block.sync
        def _(sp):
            loads_sp(sp)
            keys_sp(sp)
            proj_sp(sp, "j0", [(q0_t, 0, D), (k0_t, D, 2 * D), (m0_t, 2 * D, 3 * D)])
            sort_sp(sp)
            order_sp(sp, 0)
            pass_sp(sp, PB)
            carry_sp(sp, PB)
            stats_sp(sp)
            order_sp(sp, 1)
            paysort_sp(sp)
            pass_sp(sp, PA)
            carry_sp(sp, PA)
            proj_sp(sp, "j1", [(q1_t, 0, D), (kv1_t, D, 3 * D)])
            pass_sp(sp, P1)
            carry_sp(sp, P1)
            proj_sp(sp, "j2", [(h2_t, 0, D + 4), (ed2_t, D + 4, D + 8)])
            pass_sp(sp, P2)
            carry_sp(sp, P2)
            proj_sp(sp, "j3", [(x3_t, 0, D)])
            pass_sp(sp, P3)
            carry_sp(sp, P3)
            end3_sp(sp)

        @block.gpsimd
        def _(g_):
            constants_pool(g_)
            pass_pool(g_, PB)
            nodes_pool(g_, 0)
            ends_pool(g_, PB)
            paysort_pool(g_)
            nodes_pool(g_, 1)
            pass_pool(g_, PA)
            ends_pool(g_, PA)
            pass_pool(g_, P1)
            ends_pool(g_, P1)
            pass_pool(g_, P2)
            ends_pool(g_, P2)
            pass_pool(g_, P3)
            ends_pool(g_, P3)

        @block.vector
        def _(v):
            padding_dve(v)
            keys_dve(v)
            proj_dve(v, "j0", 3 * D)
            sort_dve(v)
            order_dve(v, 0)
            pass_dve(v, PB)
            carry_dve(v, PB)
            nodes_dve(v, 0)
            stats_dve(v)
            order_dve(v, 1)
            paysort_dve(v)
            nodes_dve(v, 1)
            pass_dve(v, PA)
            carry_dve(v, PA)
            end0_dve(v)
            proj_dve(v, "j1", 3 * D)
            pass_dve(v, P1)
            carry_dve(v, P1)
            end12_dve(v, P1)
            proj_dve(v, "j2", D)
            pass_dve(v, P2)
            carry_dve(v, P2)
            end12_dve(v, P2)
            proj_dve(v, "j3", 0)
            pass_dve(v, P3)
            carry_dve(v, P3)
            end3_dve(v)

        @block.scalar
        def _(act):
            act.sem_inc(S("attr_free"), 1)
            weights3_act(act)
            proj_act(act, "j0", 3 * D)
            sort_act(act)
            pass_act(act, PB)
            carry_act(act, PB)
            nodes_act(act, 0)
            stats_act(act)
            nodes_act(act, 1)
            pass_act(act, PA)
            carry_act(act, PA)
            end0_act(act)
            proj_act(act, "j1", 3 * D)
            pass_act(act, P1)
            carry_act(act, P1)
            end12_act(act, P1)
            proj_act(act, "j2", D)
            pass_act(act, P2)
            carry_act(act, P2)
            end12_act(act, P2)
            proj_act(act, "j3", 0)
            pass_act(act, P3)
            carry_act(act, P3)
            end3_act(act)

        @block.tensor
        def _(pe):
            weights3_pe(pe)
            proj_pe(pe, "j0", wcat0[:, :], bcat0[:, :], 3 * D)
            sort_pe(pe)
            order_pe(pe, 0)
            payload_pe(pe)
            carry_pe(pe, PB)
            order_pe(pe, 1)
            carry_pe(pe, PA)
            end0_pe(pe)
            proj_pe(pe, "j1", wcat1[:, :], bcat1[:, :], 3 * D)
            carry_pe(pe, P1)
            end1_pe(pe)
            proj_pe(pe, "j2", w_2[:, :], None, D)
            carry_pe(pe, P2)
            carry_pe(pe, P3)
            end3_pe(pe)


_INS = ["x", "src", "dst", "edge_attr_64", "edge_weight",
        "L0_gnn_Wk", "L0_gnn_bk", "L0_gnn_Wm", "L0_gnn_bm", "L0_gnn_Wq", "L0_gnn_bq", "L0_gnn_W1", "L0_gnn_b1",
        "L0_gnn_gamma", "L0_gnn_beta", "L0_gnn_W2", "L0_gnn_b2",
        "L1_gnn_Wq", "L1_gnn_bq", "L1_gnn_Wk", "L1_gnn_bk", "L1_gnn_Wv", "L1_gnn_bv", "L1_gnn_We", "L1_gnn_be", "L1_gnn_Wo", "L1_gnn_bo",
        "L2_gnn_W", "L2_gnn_a_src", "L2_gnn_a_dst", "L3_gnn_W1", "L3_gnn_b1", "L3_gnn_W2", "L3_gnn_b2"]


def kernel(**inputs):
    import numpy as _np
    import concourse.bacc as _bacc
    from concourse import mybir as _mybir
    from concourse.bass_utils import run_bass_kernel_spmd as _run

    nc = _bacc.Bacc("TRN2", target_bir_lowering=False, num_devices=1)
    arrays, args = {}, {}
    for name in _INS:
        a = _np.ascontiguousarray(inputs[name])
        arrays[f"in_{name}_dram"] = a
        args[name] = nc.dram_tensor(f"in_{name}_dram", a.shape, _mybir.dt.from_np(a.dtype), kind="ExternalInput").ap()
    out = nc.dram_tensor("out_0_dram", (N, D), F32, kind="ExternalOutput").ap()
    graph_layers_kernel(nc, args, out)
    r = _run(nc, [arrays], core_ids=[0])
    return r.results[0]["out_0_dram"]
```

```python
from contextlib import ExitStack

import concourse.bass as bass
from concourse import mybir

F32 = mybir.dt.float32
I32 = mybir.dt.int32
ALU = mybir.AluOpType
ACT = mybir.ActivationFunctionType
AX = mybir.AxisListType

P = 128
N, D, E = 6250, 128, 206250
EF = 64
BPG = 4
NG = -(-N // (P * BPG))
NB = NG * BPG
NPAD = NB * P
GN = BPG * P
T = 1612
EP = P * T
K = 13
IT = T // K
assert EP >= E and T % (2 * K) == 0
PADN = 6271
assert N <= PADN < NPAD
KW = 1616
C = 2048
LOGC, LOGP = 11, 7
KE = 2 * K
NPAY = EP // (P * KE)
PW = 16
BIG = 1.0e30
H0, H1, H2 = 4, 8, 4
EPS = 1e-5


class Seq:

    def __init__(self, eng, sem, base=0, i=None, per=0):
        self.eng, self.sem, self.base, self.i, self.per, self.k = eng, sem, base, i, per, 0

    def did(self, ins):
        self.k += 1
        ins.then_inc(self.sem, 1)

    def value(self, k):
        return self.base + k if self.i is None else self.i * self.per + (self.base + k)

    def wait(self):
        self.eng.wait_ge(self.sem, self.value(self.k))

    def do(self, ins):
        self.did(ins)
        self.wait()


class Line(Seq):

    def __init__(self, eng, sem, total):
        super().__init__(eng, sem, total[0])
        self.total = total

    def did(self, ins):
        super().did(ins)
        self.total[0] += 1


def graph_layers_kernel(nc, A, out):
    with ExitStack() as ctx:
        def sb(name, shape, dt=F32):
            return ctx.enter_context(nc.sbuf_tensor(name, shape, dt))

        sems = {}

        def S(name):
            if name not in sems:
                sems[name] = ctx.enter_context(nc.semaphore(name))
            return sems[name]

        line_total = [0]

        def line(v):
            return Line(v, S("line_steps"), line_total)

        def dram(name, shape, dt=F32):
            return nc.dram_tensor(name, shape, dt).ap()

        psA = ctx.enter_context(nc.psum_tensor("psA", [P, 512], F32))
        psB = ctx.enter_context(nc.psum_tensor("psB", [P, 4, 512], F32))
        psC = ctx.enter_context(nc.psum_tensor("psC", [P, 1024], F32))
        psD = ctx.enter_context(nc.psum_tensor("psD", [P, 512], F32))

        xsb = sb("xsb", [P, NB, D])
        ident = sb("ident", [P, P])
        ones = sb("ones", [P, P])
        before = sb("before", [P, P])
        after = sb("after", [P, P])
        nid = sb("nid", [P, NB])
        sgn = sb("sgn", [P, 8])
        wcat0 = sb("wcat0", [P, 3 * D])
        bcat0 = sb("bcat0", [1, 3 * D])
        wcat1 = sb("wcat1", [P, 3 * D])
        bcat1 = sb("bcat1", [1, 3 * D])
        w1_0 = sb("w1_0", [P, D])
        w2_0 = sb("w2_0", [P, D])
        b2_0 = sb("b2_0", [1, D])
        bncol = sb("bncol", [P, 8])
        we2 = sb("we2", [P, 16])
        be2 = sb("be2", [1, 16])
        wo_1 = sb("wo_1", [P, D])
        bo_1 = sb("bo_1", [1, D])
        w_2 = sb("w_2", [P, D])
        avec = sb("avec", [P, 2, D])
        w3raw = sb("w3raw", [P, 2, D])
        w3t = sb("w3t", [P, 2, D])
        b3 = sb("b3", [1, 2, D])

        oth_i = sb("oth_i", [P, T + 2 * K], I32)
        restart = sb("restart", [P, T])
        ew = sb("ew", [P, T])
        endix = sb("endix", [P, NB], I32)
        spos = sb("spos", [P, NB], I32)
        head_i = sb("head_i", [P, 1], I32)
        patch_i = sb("patch_i", [P, 1], I32)
        head = sb("head", [P, D])
        bias2 = sb("bias2", [P, P])
        contT = sb("contT", [P, P])

        WS = 260
        region = sb("region", [P, 2 * K * (WS + D)])
        rows_s = [region[:, b * K * WS:(b + 1) * K * WS].rearrange("p (t w) -> p t w", w=WS) for b in range(2)]
        rows_d = [region[:, 2 * K * WS + b * K * D:2 * K * WS + (b + 1) * K * D].rearrange("p (t w) -> p t w", w=D) for b in range(2)]
        ix_s = [sb(f"ix_s{b}", [P, K], I32) for b in range(2)]
        pay = [sb(f"pay{b}", [P, K, PW]) for b in range(2)]
        s_ext = sb("s_ext", [P, 8, K + 1])
        s_max = sb("s_max", [P, 8, K + 1])
        m_ext = sb("m_ext", [P, 8, K + 1])
        rst = sb("rst", [P, 8, K + 1])
        dd = sb("dd", [P, 8, K + 1])
        ww = sb("ww", [P, 8, K])
        dtmp = sb("dtmp", [P, 8, K])

        WORK = 14900
        work = sb("work", [P, WORK])
        at = [0]

        def w_view(n):
            a = work[:, at[0]:at[0] + n]
            at[0] += n
            assert at[0] <= WORK
            return a

        FM = 136
        bv = w_view(FM * (K + 1))
        abig = w_view(FM * (K + 1))
        st = w_view(FM * (K + 1))
        psrow = [w_view(K * 144) for _ in range(2)]
        zt = w_view(D * (K + 1))
        nsb = w_view(D * (K + 1))
        hold = w_view(D * (K + 1))
        falls = work[:, 2 * C:3 * C]
        keyin = [work[:, i * C:(i + 1) * C] for i in range(2)]
        rows4 = [work[:, b * 2 * KW:(b + 1) * 2 * KW].rearrange("p (j w) -> p j w", w=KW) for b in range(2)]
        rsign = work[:, 4 * KW:5 * KW]
        cmp_n = work[:, 0:NB * P].rearrange("p (j r) -> p j r", r=P)

        attr = work[:, 100:100 + KE * EF].rearrange("p (t w) -> p t w", w=EF)
        attrT = work[:, 2000:2000 + KE // 2 * P].rearrange("p (u r) -> p u r", r=P)
        pay0 = sb("payrow", [P, KE, PW])
        pcol_i = sb("pcol_i", [P, KE], I32)
        pcol_f = sb("pcol_f", [P, KE])

        X = region[:, 0:C]
        Y = region[:, C:2 * C]
        eid_i = region[:, 2 * C:3 * C].bitcast(I32)
        raw = region[:, 2 * C:2 * C + T].bitcast(I32)
        seg_i = region[:, 3 * C:3 * C + T].bitcast(I32)
        same = region[:, 4 * C:4 * C + T]
        eid_a = Y[:, 0:T].bitcast(I32)
        cnt_tmp = work[:, 4000:4000 + T]
        nid_i = sb("nid_i", [P, NB], I32)
        part_i = sb("part_i", [P, 8], I32)
        diag2 = sb("diag2", [P, 2, P])
        firstrow = sb("firstrow", [P, P])
        down1 = sb("down1", [P, P])
        wrap1 = sb("wrap1", [P, P])
        nt_c = sb("nt_c", [P, NB + 1])
        nt_q = sb("nt_q", [P, NB])
        nt_b = sb("nt_b", [P, NB])
        zero_t = sb("zero_t", [P, 4 * D])
        segf = X[:, 0:KW]
        hT_all = region[:, 0:NPAD]

        hst = sb("hst", [P, BPG, D])
        hst2 = sb("hst2", [P, BPG, D])
        hT = sb("hT", [P, 2, GN])
        tab = sb("tab", [P, BPG, 3 * D])
        ln_s = sb("ln_s", [P, 4, BPG])
        nt_f = sb("nt_f", [P, 2, NB])
        nt_i = sb("nt_i", [P, NB], I32)
        fe_i = sb("fe_i", [P, BPG], I32)
        half_i = [sb(f"half_i{b}", [P, 2], I32) for b in range(2)]
        end4 = sb("end4", [P, BPG, 144])
        prow = sb("prow", [P, 144])
        pmx = sb("pmx", [P, 3, 8])
        mx4 = sb("mx4", [P, 3, BPG, 8])
        cst = sb("cst", [P, 144])
        ctz = sb("ctz", [1, 144])
        next_i = sb("next_i", [P, 1], I32)
        flag_f = sb("flag_f", [P, 2])
        flag_i = sb("flag_i", [P, 1], I32)
        mcar = sb("mcar", [P, 8])
        dwide = work[:, 0:1024]
        wwide = work[:, 1024:2048]

        keys_dram = dram("keys_in", [2, P, C])
        sorted_dram = dram("keys_sorted", [2, P * C])
        pay_dram = dram("payload", [EP, PW])
        paya_dram = dram("payload_by_dst", [EP, PW])
        q0_t = dram("q0", [NPAD, D])
        k0_t = dram("k0", [NPAD, D])
        m0_t = dram("m0", [NPAD, D])
        qm0_t = dram("qm0", [NPAD, 260])
        q1_t = dram("q1", [NPAD, D])
        kv1_t = dram("kv1", [NPAD, 2 * D])
        h2_t = dram("h2", [NPAD, D + 4])
        ed2_t = dram("ed2", [NPAD, 4])
        x3_t = dram("x3", [NPAD, D])
        keyrow_t = [dram(f"keyrow{o}", [P, KW]) for o in range(2)]
        qxb_t = dram("start_rows_by_src", [EP + NPAD, D])
        qxa_t = dram("start_rows_by_dst", [EP + NPAD, D])
        edx_t = dram("start_ed2", [EP + NPAD, 4])

        class Pass:
            def __init__(self, name, H, dh, soft, tabs, tabd, near, W):
                self.name, self.H, self.dh, self.soft = name, H, dh, soft
                self.tabs, self.tabd, self.near, self.W = tabs, tabd, near, W
                self.HF = near.shape[1] if near is not None else D
                self.made = 2 if near is not None else 1
                self.F = H * (dh + 1) if soft else D
                self.ps = dram(f"state_{name}", [EP + 1, W])

            def s(self, what):
                return S(f"pass_{what}")

            def own(self, what):
                return S(f"{self.name}_{what}")

            def total(self, what):
                half = IT // 2
                exps = IT if self.soft or self is PA else 0
                hold = self.near is not None
                return {"free0": 1 + half, "free1": 1 + half, "prep": 4 + hold, "steps": self.steps * IT,
                        "near_in0": 16 * half * hold, "near_in1": 16 * half * hold, "made": self.made * IT, "held": IT * hold,
                        "laid": 1 + IT, "laid0": half, "laid1": half, "arg": exps, "expw": exps, "decay": IT * self.soft, "scanned": IT,
                        "sent0": 16 + 16 * half, "sent1": 16 + 16 * half, "ends_free": 1 + NG, "fix": NG,
                        "ends_in": 16 * BPG * NG,
                        "carry_dve": 3 if self.soft else 1, "carry_pe": 3 if self.soft else 1, "carry_act": 4 * self.soft,
                        "head_in": 16 * hold, "prow_in": 16, "patched": 1,
                        "prow_out": 16}[what]

            def base(self, what):
                return sum(q.total(what) for q in passes[:passes.index(self)])

            def on(self, what, value):
                return self.s(what), value + self.base(what)

        PB = Pass("pB", H0, 0, True, k0_t, q0_t, qxb_t, 12)
        PA = Pass("pA", H0, 32, False, qm0_t, k0_t, qxa_t, D)
        P1 = Pass("p1", H1, 16, True, kv1_t, q1_t, qxa_t, 144)
        P2 = Pass("p2", H2, 32, True, h2_t, ed2_t, edx_t, 136)
        P3 = Pass("p3", 1, D, False, x3_t, None, None, D)
        passes = [PB, PA, P1, P2, P3]
        SCATTER = 16 * BPG * NG
        PB.steps, PB.needs = 13, [("order_ready", 1), ("j0_out", 16 * 3 * NG)]
        PA.steps, PA.needs = 9, [("edges_ready", 1), ("qm_out", 48 * NG)]
        P1.steps, P1.needs = 15, [("j1_out", 32 * NG)]
        P2.steps, P2.needs = 15, [("j2_out", 32 * NG)]
        P3.steps, P3.needs = 4, [("j3_out", 16 * NG)]
        PB.started = [("spread_out0", 32 * NG), ("spread_out1", 32 * NG)]
        PA.started = [("spread_out0", 64 * NG), ("spread_out1", 64 * NG)]
        P1.started = [("scat_out", SCATTER)]
        P2.started = [("scat_out", 2 * SCATTER)]

        cnt = ew

        def grows(t, g):
            return t[bass.ds(g * GN, GN), :].rearrange("(j p) w -> p j w", p=P)

        def constants_pool(g):
            g.memset(ident[:, :], 0.0).then_inc(S("c_fill"), 1)
            g.memset(before[:, :], 1.0).then_inc(S("c_fill"), 1)
            g.memset(after[:, :], 1.0).then_inc(S("c_fill"), 1)
            g.memset(ones[:, :], 1.0).then_inc(S("consts"), 1)
            g.memset(down1[:, :], 0.0).then_inc(S("c_fill"), 1)
            g.memset(wrap1[:, :], 0.0).then_inc(S("c_fill"), 1)
            g.memset(zero_t[:, :], 0.0).then_inc(S("consts"), 1)
            g.iota(nid_i[:, :], [[P, NB]], base=0, channel_multiplier=1).then_inc(S("consts"), 1)
            g.iota(eid_i, [[1, C]], base=0, channel_multiplier=C).then_inc(S("consts"), 1)
            g.iota(part_i[:, :], [[0, 8]], base=0, channel_multiplier=1).then_inc(S("consts"), 1)
            g.wait_ge(S("c_fill"), 5)
            g.affine_select(out=ident[:, :], in_=ident[:, :], compare_op=ALU.not_equal, fill=1.0, base=0,
                            pattern=[[-1, P]], channel_multiplier=1).then_inc(S("consts"), 1)
            g.affine_select(out=before[:, :], in_=before[:, :], compare_op=ALU.is_gt, fill=0.0, base=0,
                            pattern=[[-1, P]], channel_multiplier=1).then_inc(S("consts"), 1)
            g.affine_select(out=after[:, :], in_=after[:, :], compare_op=ALU.is_gt, fill=0.0, base=0,
                            pattern=[[1, P]], channel_multiplier=-1).then_inc(S("consts"), 1)
            g.affine_select(out=down1[:, :], in_=down1[:, :], compare_op=ALU.not_equal, fill=1.0, base=1,
                            pattern=[[-1, P]], channel_multiplier=1).then_inc(S("consts"), 1)
            g.affine_select(out=wrap1[:, :], in_=wrap1[:, :], compare_op=ALU.not_equal, fill=1.0, base=1 - P,
                            pattern=[[-1, P]], channel_multiplier=1).then_inc(S("consts"), 1)

        CONSTS = 10

        def zeros_sp(sp):
            n = EP // (4 * P)
            sp.dma_start(qxb_t[0:EP, :].rearrange("(p r c) w -> p r (c w)", p=P, c=4),
                         zero_t[:, :].unsqueeze(1).to_broadcast([P, n, 4 * D])).then_inc(S("zeroed"), 16)
            c = T // 13
            sp.dma_start(edx_t[0:EP, :].rearrange("(p r c) w -> p r (c w)", p=P, c=c),
                         zero_t[:, 0:4 * c].unsqueeze(1).to_broadcast([P, 13, 4 * c])).then_inc(S("zeroed"), 16)

        def zeros_chunk_sp(sp, i):
            c = 2 * K // 2
            sp.dma_start(qxa_t[0:EP, :].rearrange("(p r) w -> p (r w)", p=P)[:, bass.ds(i * (2 * K * D), 2 * K * D)].rearrange("p (r w) -> p r w", w=2 * D),
                         zero_t[:, 0:2 * D].unsqueeze(1).to_broadcast([P, c, 2 * D])).then_inc(S("zeroed_a"), 16)

        def padding_dve(v):
            nc.vector.memset(X.bitcast(I32), PADN).then_inc(S("padded"), 1)
            nc.vector.memset(Y.bitcast(I32), PADN).then_inc(S("padded"), 1)
            nc.vector.memset(xsb[:, N // P:NB, :], 0.0).then_inc(S("padded"), 1)
            nc.vector.memset(next_i[:, :], PADN).then_inc(S("padded"), 1)
            nc.vector.memset(ctz[:, :], 0.0).then_inc(S("dummies"), 1)
            nc.vector.memset(oth_i[:, T:T + 2 * K], 0).then_inc(S("dummies"), 1)
            nc.vector.memset(nt_c[:, 0:1], 0.0).then_inc(S("dummies"), 1)
            nc.vector.memset(we2[:, :], 0.0).then_inc(S("dummies"), 1)
            nc.vector.memset(pay0[:, :, :], 0.0).then_inc(S("dummies"), 1)
            nc.vector.memset(attr[:, :, :], 0.0).then_inc(S("dummies"), 1)
            nc.vector.memset(pcol_i[:, :], 0).then_inc(S("dummies"), 1)
            nc.vector.memset(pcol_f[:, :], 0.0).then_inc(S("dummies"), 1)
            nc.vector.memset(rst[:, :, :], -BIG).then_inc(S("dummies"), 1)
            nc.vector.memset(dd[:, :, :], -BIG).then_inc(S("dummies"), 1)
            for b in range(2):
                nc.vector.memset(psrow[b], 0.0).then_inc(S("dummies"), 1)
            v.wait_ge(S("consts"), CONSTS)
            q = line(v)
            for k in range(8):
                q.did(nc.vector.tensor_scalar(part_i[:, k:k + 1], part_i[:, k:k + 1], k, 1, ALU.logical_shift_right, ALU.bitwise_and))
            q.did(nc.vector.tensor_copy(nid[:, :], nid_i[:, :]))
            q.wait()
            q.do(nc.vector.tensor_scalar(sgn[:, :], part_i[:, :], -2.0, 1.0, ALU.mult, ALU.add))

        DUMMIES = 12

        def loads_sp(sp):
            n = [0]

            def load(dst, src):
                n[0] += 1
                sp.dma_start(dst, src).then_inc(S("loaded"), 16)

            def row(name):
                return A[name].rearrange("(a d) -> a d", a=1)

            sp.wait_ge(S("padded"), 4)
            full, rest = E // C, E % C
            with nc.allow_non_contiguous_dma(reason="the edge after each partition's run"):
                sp.dma_start(next_i[0:full - 1, :], A["dst"][0:full * C].rearrange("(p c) -> p c", c=C)[1:full, 0:1]).then_inc(S("ends_in"), 16)
                sp.dma_start(next_i[full - 1:full, :], A["dst"][full * C:full * C + 1].rearrange("(p c) -> p c", p=1)).then_inc(S("ends_in"), 16)
            for name, dst in (("src", X), ("dst", Y)):
                d = dst.bitcast(I32)
                sp.dma_start(d[0:full, :], A[name][0:full * C].rearrange("(p c) -> p c", c=C)).then_inc(S("ends_in"), 16)
                sp.dma_start(d[full:full + 1, 0:rest], A[name][full * C:E].rearrange("(p c) -> p c", p=1)).then_inc(S("ends_in"), 16)
            whole = N // P
            load(xsb[:, 0:whole, :], A["x"][0:whole * P, :].rearrange("(j p) w -> p j w", p=P))
            load(xsb[0:N - whole * P, whole, :], A["x"][whole * P:N, :])
            for j, nm in enumerate("qkm"):
                load(wcat0[:, j * D:(j + 1) * D], A["L0_gnn_W" + nm])
                load(bcat0[:, j * D:(j + 1) * D], row("L0_gnn_b" + nm))
            for j, nm in enumerate("qkv"):
                load(wcat1[:, j * D:(j + 1) * D], A["L1_gnn_W" + nm])
                load(bcat1[:, j * D:(j + 1) * D], row("L1_gnn_b" + nm))
            load(w1_0[:, :], A["L0_gnn_W1"])
            load(w2_0[:, :], A["L0_gnn_W2"])
            load(b2_0[:, :], row("L0_gnn_b2"))
            with nc.allow_non_contiguous_dma(reason="a column of 128 values"):
                for j, nm in enumerate(("b1", "gamma", "beta")):
                    load(bncol[:, j:j + 1], A["L0_gnn_" + nm].rearrange("(p a) -> p a", a=1))
            sp.wait_ge(S("dummies"), DUMMIES)
            for j in range(2):
                load(we2[j * EF:(j + 1) * EF, j * 8:(j + 1) * 8], A["L1_gnn_We"])
                load(be2[:, j * 8:(j + 1) * 8], row("L1_gnn_be"))
            load(wo_1[:, :], A["L1_gnn_Wo"])
            load(bo_1[:, :], row("L1_gnn_bo"))
            load(w_2[:, :].rearrange("i (h o) -> i h o", h=H2), A["L2_gnn_W"].rearrange("h i o -> i h o"))
            for j, nm in enumerate(("src", "dst")):
                load(avec[:, j, :], A["L2_gnn_a_" + nm].rearrange("(a h) o b -> a (h o b)", a=1).to_broadcast([P, D]))
                load(w3raw[:, j, :], A[f"L3_gnn_W{j + 1}"])
                load(b3[:, j, :], row(f"L3_gnn_b{j + 1}"))
            assert n[0] == NLOADS, n[0]
            for q in passes:
                sp.dma_start(q.ps[EP:EP + 1, :], ctz[:, 0:q.W]).then_inc(S("dummy_rows"), 16)

        NLOADS = 2 + 6 + 6 + 3 + 3 + 4 + 2 + 1 + 6
        NDUMMY = 5

        def keys_dve(v):
            v.wait_ge(S("ends_in"), 96)
            v.wait_ge(S("consts"), CONSTS)
            q = line(v)
            srcs, dsts = X.bitcast(I32), Y.bitcast(I32)
            kb, ka = keyin[0].bitcast(I32), keyin[1].bitcast(I32)
            q.did(nc.vector.tensor_scalar(kb, srcs, 13, 1 << 30, ALU.logical_shift_left, ALU.bitwise_or))
            q.do(nc.vector.tensor_scalar(ka, dsts, 32.0, None, ALU.add))
            q.did(nc.vector.tensor_tensor(kb, kb, dsts, ALU.bitwise_or))
            q.do(nc.vector.tensor_scalar(ka, ka, 18, 0, ALU.logical_shift_left, ALU.bitwise_or))
            q.did(nc.vector.tensor_tensor(ka, ka, eid_i, ALU.bitwise_or))
            q.wait()
            v.sem_inc(S("keys_made"), 1)
            q.did(nc.vector.tensor_tensor(falls[:, 0:C - 1], dsts[:, 1:C], dsts[:, 0:C - 1], ALU.is_lt))
            q.did(nc.vector.tensor_tensor(falls[:, C - 1:C], next_i[:, :], dsts[:, C - 1:C], ALU.is_lt))
            q.wait()
            q.do(nc.vector.tensor_reduce(flag_f[:, 0:1], falls, AX.X, ALU.add))
            v.sem_inc(S("falls_made"), 1)

        def flag_pe(pe):
            pe.wait_ge(S("falls_made"), 1)
            nc.tensor.matmul(psC[:, 0:1], ones[:, :], flag_f[:, 0:1], start=True, stop=True).then_inc(S("falls_sum"), 1)

        def flag_dve(v):
            q = line(v)
            v.wait_ge(S("falls_sum"), 1)
            q.do(nc.vector.tensor_scalar(flag_f[:, 1:2], psC[:, 0:1], 1.0, None, ALU.min))
            q.do(nc.vector.tensor_copy(flag_i[:, :], flag_f[:, 1:2]))
            v.sem_inc(S("flag_made"), 1)

        def unsorted(eng):
            eng.wait_ge(S("flag_made"), 1)
            return eng.value_load(flag_i[0:1, 0:1], min_val=0, max_val=1)

        def keys_sp(sp):
            sp.wait_ge(S("keys_made"), 1)
            for o in range(2):
                sp.dma_start(keys_dram[o], keyin[o]).then_inc(S("keys_out"), 16)
            sp.wait_ge(S("keys_out"), 32)

        SORT_STEPS = sum(4 * k for k in range(1, LOGC)) + 2 * LOGC * (LOGP + 1) + sum(4 * q for q in range(1, LOGP)) + 2 * LOGP
        SORT_TURNS = 2 * LOGP
        SORT_SIGNS = 2 * LOGP + 1

        class Sort:

            def __init__(self):
                self.cur, self.oth = X, Y

            def swap(self):
                self.cur, self.oth = self.oth, self.cur

        def stage_views(a, j, k, directed):
            s = 1 << j
            if directed:
                w = a.rearrange("p (g d n h s) -> p d h g n s", d=2, n=1 << (k - 1 - j), h=2, s=s)
                return [(w[:, d, 0], w[:, d, 1]) for d in range(2)]
            w = a.rearrange("p (n h s) -> p h n s", h=2, s=s)
            return [(w[:, 0], w[:, 1])]

        def sort_dve(v, o):
            q = Seq(v, S("sort_steps"), o * SORT_STEPS)
            b = Sort()
            turn, sign = [0], [0]

            def stage(j, k, directed):
                for d, ((lo, hi), (lo2, hi2)) in enumerate(zip(stage_views(b.cur, j, k, directed), stage_views(b.oth, j, k, directed))):
                    q.did(nc.vector.tensor_tensor(lo2, lo, hi, ALU.max if d else ALU.min))
                    q.did(nc.vector.tensor_tensor(hi2, lo, hi, ALU.min if d else ALU.max))
                b.swap()
                q.wait()

            def signed():
                sign[0] += 1
                v.wait_ge(S("sort_signs"), o * SORT_SIGNS + sign[0])
                b.swap()

            v.wait_ge(S("sort_in"), o * 16 + 16)
            for k in range(1, LOGC):
                for j in reversed(range(k)):
                    stage(j, k, True)
            for k in range(LOGC, LOGC + LOGP + 1):
                if k > LOGC:
                    signed()
                    turn[0] += 1
                    v.wait_ge(S("sort_turns"), o * SORT_TURNS + turn[0])
                    nc.vector.tensor_copy(b.oth, psB[:, :, :].rearrange("p a b -> p (a b)")).then_inc(S("sort_evacs"), 1)
                    b.swap()
                    v.wait_ge(S("sort_evacs"), o * LOGP + turn[0] // 2 + 1)
                    lp = k - LOGC
                    for j in reversed(range(lp)):
                        stage(j, lp, k < LOGC + LOGP)
                    turn[0] += 1
                signed()
                for j in reversed(range(LOGC)):
                    stage(j, LOGC, False)
            assert q.k == SORT_STEPS, (q.k, SORT_STEPS)
            assert b.cur is sorted_at(), "the sorted keys' buffer"

        def sorted_at():
            n = sum(range(1, LOGC)) + LOGC * (LOGP + 1) + sum(range(1, LOGP + 1)) + SORT_SIGNS + LOGP
            return Y if n % 2 else X

        def sort_act(act, o):
            b = Sort()
            steps = sum(4 * k for k in range(1, LOGC))
            for _ in range(sum(range(1, LOGC))):
                b.swap()
            turn = 0
            for k in range(LOGC, LOGC + LOGP + 1):
                lp = k - LOGC
                if lp:
                    act.wait_ge(S("sort_steps"), o * SORT_STEPS + steps)
                    nc.scalar.mul(b.oth, b.cur, sgn[:, lp - 1:lp]).then_inc(S("sort_signs"), 1)
                    b.swap()
                    b.swap()
                    steps += (4 if lp < LOGP else 2) * lp
                    for _ in range(lp):
                        b.swap()
                    turn += 2
                    act.wait_ge(S("sort_turns"), o * SORT_TURNS + turn)
                    nc.scalar.mul(b.oth, psB[:, :, :].rearrange("p a b -> p (a b)"),
                                  sgn[:, lp:lp + 1]).then_inc(S("sort_signs"), 1)
                else:
                    act.wait_ge(S("sort_steps"), o * SORT_STEPS + steps)
                    nc.scalar.mul(b.oth, b.cur, sgn[:, 0:1]).then_inc(S("sort_signs"), 1)
                b.swap()
                steps += 2 * LOGC
                for _ in range(LOGC):
                    b.swap()

        def sort_pe(pe, o):
            b = Sort()
            steps = sum(4 * k for k in range(1, LOGC)) + 2 * LOGC
            for _ in range(sum(range(1, LOGC)) + 1 + LOGC):
                b.swap()

            def turn_all():
                for c in range(C // P):
                    ins = nc.tensor.transpose(psB[:, c // 4, (c % 4) * P:(c % 4 + 1) * P], b.cur[:, c * P:(c + 1) * P], ident[:, :])
                ins.then_inc(S("sort_turns"), 1)

            sign = 1
            for lp in range(1, LOGP + 1):
                b.swap()
                sign += 1
                pe.wait_ge(S("sort_signs"), o * SORT_SIGNS + sign)
                turn_all()
                b.swap()
                for _ in range(lp):
                    b.swap()
                steps += (4 if lp < LOGP else 2) * lp
                pe.wait_ge(S("sort_evacs"), o * LOGP + lp)
                pe.wait_ge(S("sort_steps"), o * SORT_STEPS + steps)
                turn_all()
                b.swap()
                sign += 1
                steps += 2 * LOGC
                for _ in range(LOGC):
                    b.swap()

        def sort_sp(sp, o):
            sp.dma_start(X, keys_dram[o]).then_inc(S("sort_in"), 16)
            if o == 0:
                zeros_sp(sp)
            sp.wait_ge(S("sort_steps"), (o + 1) * SORT_STEPS)
            sp.dma_start(sorted_dram[o, :].rearrange("(p c) -> p c", c=C), sorted_at()).then_inc(S("sort_out"), 16)
            sp.wait_ge(S("sort_out"), o * 16 + 16)

        LN_STEPS = 8

        def proj_on(nm, what, value):
            before = "j0 j1 j2 j3".split().index(nm)
            return S("proj_" + what), value + before * (NG + (what in ("tr", "ht", "psfree", "tabfree")))

        def norm_group(v, nm, g, q, first_write):
            xg = xsb[:, bass.ds(g * BPG, BPG), :]
            bc = lambda k: ln_s[:, k, :].unsqueeze(2).to_broadcast([P, BPG, D])
            q.do(nc.vector.tensor_reduce(ln_s[:, 0, :], xg, AX.X, ALU.add))
            q.do(nc.vector.tensor_scalar(ln_s[:, 1, :], ln_s[:, 0, :], -1.0 / D, None, ALU.mult))
            first_write()
            q.do(nc.vector.tensor_tensor(hst[:, :, :], xg, bc(1), ALU.add))
            q.do(nc.vector.tensor_tensor(hst2[:, :, :], hst[:, :, :], hst[:, :, :], ALU.mult))
            q.do(nc.vector.tensor_reduce(ln_s[:, 0, :], hst2[:, :, :], AX.X, ALU.add))
            q.did(nc.vector.tensor_scalar(ln_s[:, 2, :], ln_s[:, 0, :], 1.0 / D, EPS, ALU.mult, ALU.add))
            v.wait_ge(*proj_on(nm, "sqrt", g + 1))
            q.do(nc.vector.reciprocal(ln_s[:, 1, :], ln_s[:, 3, :]))
            q.do(nc.vector.tensor_tensor(hst[:, :, :], hst[:, :, :], bc(1), ALU.mult))

        def proj_dve(v, nm, ncol):
            steps = LN_STEPS + 1 + (4 if nm == "j2" else 0)
            if nm == "j0":
                v.wait_ge(S("loaded"), 16 * NLOADS)
            with v.Fori(0, NG) as g:
                q = Seq(v, S(nm + "_steps"), 0, g, steps)
                left = "tr" if ncol else "tabfree"
                norm_group(v, nm, g, q, lambda: v.wait_ge(*proj_on(nm, left, g + 1)))
                q.did(nc.vector.tensor_scalar(hst[:, :, :], hst[:, :, :], 0.0, None, ALU.max))
                if nm == "j2":
                    v.wait_ge(*proj_on(nm, "tab", g + 1))
                    for j in range(2):
                        q.do(nc.vector.tensor_tensor(hst2[:, :, :], tab[:, :, 0:D],
                                                     avec[:, j, :].unsqueeze(1).to_broadcast([P, BPG, D]), ALU.mult))
                        q.do(nc.vector.tensor_reduce(tab[:, :, D + 4 * j:D + 4 * j + 4],
                                                     hst2[:, :, :].rearrange("p j (h o) -> p j h o", h=H2), AX.X, ALU.add))
                assert q.k == steps, (q.k, steps)

        def proj_pe(pe, nm, w, brow, ncol):
            pe.sem_inc(S("proj_tr"), 1)
            steps = LN_STEPS + 1 + (4 if nm == "j2" else 0)
            with pe.Fori(0, NG) as g:
                pe.wait_ge(S(nm + "_steps"), g * steps + LN_STEPS + 1)
                pe.wait_ge(*proj_on(nm, "ht", g + 1))
                for j in range(BPG):
                    ins = nc.tensor.transpose(psA[:, j * P:(j + 1) * P], hst[:, j, :], ident[:, :])
                ins.then_inc(S("proj_tr"), 1)
                pe.wait_ge(*proj_on(nm, "ht", g + 2))
                pe.wait_ge(*proj_on(nm, "psfree", g + 1))
                for j in range(BPG):
                    ins = nc.tensor.matmul(psB[:, j, 0:ncol], hT[:, 0, j * P:(j + 1) * P], w, start=True, stop=brow is None)
                    if brow is not None:
                        ins = nc.tensor.matmul(psB[:, j, 0:ncol], ones[0:1, :], brow, start=False, stop=True)
                ins.then_inc(S("proj_mm"), 1)

        def proj_act(act, nm, ncol):
            steps = LN_STEPS + 1 + (4 if nm == "j2" else 0)
            if ncol:
                act.sem_inc(S("proj_ht"), 1)
                act.sem_inc(S("proj_psfree"), 1)
            with act.Fori(0, NG) as g:
                act.wait_ge(S(nm + "_steps"), g * steps + 6)
                nc.scalar.activation(ln_s[:, 3, :], ln_s[:, 2, :], ACT.Sqrt).then_inc(S("proj_sqrt"), 1)
                if ncol:
                    act.wait_ge(*proj_on(nm, "tr", g + 2))
                    nc.scalar.copy(hT[:, 0, :], psA[:, :]).then_inc(S("proj_ht"), 1)
                    act.wait_ge(*proj_on(nm, "mm", g + 1))
                    act.wait_ge(*proj_on(nm, "tabfree", g + 1))
                    if nm == "j0":
                        nc.scalar.mul(tab[:, :, 0:D], psB[:, :, 0:D], 1.0 / (32 ** 0.5)).then_inc(S(nm + "_q"), 1)
                        ins = nc.scalar.copy(tab[:, :, D:ncol], psB[:, :, D:ncol])
                    else:
                        ins = nc.scalar.copy(tab[:, :, 0:ncol], psB[:, :, 0:ncol])
                    ins.then_inc(S("proj_tab"), 1)
                    act.wait_ge(*proj_on(nm, "tab", g + 1))
                    act.sem_inc(S("proj_psfree"), 1)

        def proj_sp(sp, nm, tabs):
            sp.sem_inc(S("proj_tabfree"), 1)
            steps = LN_STEPS + 1 + (4 if nm == "j2" else 0)
            with sp.Fori(0, NG) as g:
                if nm in ("j2", "j3"):
                    sp.wait_ge(S(nm + "_steps"), (g + 1) * steps)
                else:
                    sp.wait_ge(*proj_on(nm, "tab", g + 1))
                if nm == "j0":
                    sp.wait_ge(S("j0_q"), g + 1)
                for t, a, z in tabs:
                    src = hst if nm == "j3" else tab
                    sp.dma_start(grows(t, g), src[:, :, a:z]).then_inc(S(nm + "_out"), 16)
                sp.wait_ge(S(nm + "_out"), g * (16 * len(tabs)) + 16 * len(tabs))
                if nm in SCATTERED:
                    sp.wait_ge(S("scat_out"), g * (16 * BPG) + (SCATTERED.index(nm) * SCATTER + 16 * BPG))
                sp.sem_inc(S("proj_tabfree"), 1)

        SCATTERED = ["j1", "j2"]

        def scatter_pool(g_, nm, a, z, t):
            o = SCATTERED.index(nm)
            steps = LN_STEPS + 1 + (4 if nm == "j2" else 0)
            with g_.Fori(0, NG) as g:
                if nm == "j2":
                    g_.wait_ge(S(nm + "_steps"), (g + 1) * steps)
                else:
                    g_.wait_ge(*proj_on(nm, "tab", g + 1))
                g_.sem_inc(S("pool_go"), 1)
                g_.tensor_copy(fe_i[:, :], spos[:, bass.ds(g * BPG, BPG)]).then_inc(S("scat_ix"), 1)
                g_.wait_ge(S("scat_ix"), g + (1 + o * NG))
                g_.sem_inc(S("pool_go"), 1)
                for j in range(BPG):
                    g_.indirect_dma_start(t, bass.IndirectOffsetOnAxis(ap=fe_i[:, j:j + 1], axis=0), tab[:, j, a:z], None)\
                      .then_inc(S("scat_out"), 16)

        def order_sp(sp, o):
            def sorted_keys():
                sp.dma_start(raw, sorted_dram[o, 0:EP].bitcast(I32).rearrange("(p t) -> p t", t=T)).then_inc(S("raw_in"), 16)

            if o == 0:
                sorted_keys()
            else:
                sp.wait_ge(S("stats_done"), 1)
                with sp.If(unsorted(sp) > 0):
                    sorted_keys()
                with sp.If(unsorted(sp) < 1):
                    sp.wait_ge(S("edges_padded"), 3)
                    full, rest = E // T, E % T
                    for name, dst in (("dst", seg_i), ("src", oth_i), ("edge_weight", ew)):
                        sp.dma_start(dst[0:full, 0:T], A[name][0:full * T].rearrange("(p t) -> p t", t=T)).then_inc(S("edges_in"), 16)
                        sp.dma_start(dst[full:full + 1, 0:rest], A[name][full * T:E].rearrange("(p t) -> p t", p=1)).then_inc(S("edges_in"), 16)
            sp.wait_ge(S("keyrow_made"), o + 1)
            sp.dma_start(keyrow_t[o], segf).then_inc(S("keyrow_out"), 16)

        def order_dve(v, o):
            if o == 0:
                q = line(v)
                v.wait_ge(S("raw_in"), 16)
                q.did(nc.vector.tensor_scalar(seg_i[:, :], raw, 13, 0x1FFF, ALU.logical_shift_right, ALU.bitwise_and))
                q.do(nc.vector.tensor_scalar(oth_i[:, 0:T], raw, 0x1FFF, 0, ALU.bitwise_and, ALU.bitwise_or))
            else:
                with v.If(unsorted(v) > 0):
                    q = Seq(v, S("decode_steps"))
                    v.wait_ge(S("raw_in"), 32)
                    q.did(nc.vector.tensor_scalar(seg_i[:, :], raw, 18, 0x1FFF, ALU.logical_shift_right, ALU.bitwise_and))
                    q.do(nc.vector.tensor_scalar(eid_a, raw, 0x3FFFF, 0, ALU.bitwise_and, ALU.bitwise_or))
                    q.do(nc.vector.tensor_scalar(seg_i[:, :], seg_i[:, :], 32.0, None, ALU.subtract))
                    v.sem_inc(S("eid_ready"), 1)
                with v.If(unsorted(v) < 1):
                    r0, p0 = E % T, E // T // 32 * 32
                    nc.vector.memset(seg_i[p0:P, r0:T], PADN).then_inc(S("edges_padded"), 1)
                    nc.vector.memset(oth_i[p0:P, r0:T], PADN).then_inc(S("edges_padded"), 1)
                    nc.vector.memset(ew[p0:P, r0:T], 0.0).then_inc(S("edges_padded"), 1)
                    v.wait_ge(S("edges_in"), 96)
                q = line(v)
            q.did(nc.vector.memset(segf[:, T:KW], 0.0))
            q.did(nc.vector.tensor_copy(head_i[:, :], seg_i[:, 0:1]))
            q.do(nc.vector.tensor_copy(segf[:, 0:T], seg_i[:, :]))
            q.do(nc.vector.tensor_scalar(same, segf[:, 0:T], segf[:, 0:1], None, ALU.is_equal))
            q.do(nc.vector.tensor_reduce(mcar[:, 0:1], same, AX.X, ALU.add))
            q.do(nc.vector.scalar_tensor_tensor(out=mcar[:, 1:2], in0=nid[:, 0:1], scalar=float(T), in1=mcar[:, 0:1], op0=ALU.mult, op1=ALU.add))
            q.did(nc.vector.tensor_scalar(patch_i[:, :], mcar[:, 1:2], -1.0, None, ALU.add))
            q.do(nc.vector.tensor_tensor(restart[:, 1:T], segf[:, 1:T], segf[:, 0:T - 1], ALU.is_equal))
            q.did(nc.vector.tensor_scalar(restart[:, 1:T], restart[:, 1:T], BIG, -BIG, ALU.mult, ALU.add))
            q.did(nc.vector.tensor_scalar(diag2[:, 0, :], ident[:, :], segf[:, 0:1], None, ALU.mult))
            q.do(nc.vector.tensor_scalar(diag2[:, 1, :], ident[:, :], segf[:, T - 1:T], None, ALU.mult))
            v.sem_inc(S("ends_made"), 1)
            v.wait_ge(S("ends_rows"), o + 1)
            q.do(nc.vector.tensor_copy(firstrow[:, :], psC[:, 0:P]))
            q.did(nc.vector.scalar_tensor_tensor(out=contT[:, :], in0=firstrow[:, :], scalar=segf[:, T - 1:T], in1=after[:, :],
                                                 op0=ALU.is_equal, op1=ALU.mult))
            q.do(nc.vector.scalar_tensor_tensor(out=bias2[:, :], in0=psC[:, P:2 * P], scalar=segf[:, 0:1], in1=before[:, :],
                                                op0=ALU.is_equal, op1=ALU.mult))
            v.sem_inc(S("keyrow_made"), 1)
            q.do(nc.vector.tensor_reduce(mcar[:, 0:1], bias2[:, :], AX.X, ALU.max))
            q.do(nc.vector.tensor_scalar(restart[:, 0:1], mcar[:, 0:1], BIG, -BIG, ALU.mult, ALU.add))
            q.do(nc.vector.tensor_scalar(bias2[:, :], bias2[:, :], BIG, -BIG, ALU.mult, ALU.add))
            if o == 0:
                q.do(nc.vector.tensor_scalar(cnt_tmp, restart[:, :], 1.0 / BIG, 1.0, ALU.mult, ALU.add))
                q.do(nc.vector.tensor_tensor_scan(cnt[:, :], cnt_tmp, ones[:, 0:1].to_broadcast([P, T]), 0.0, ALU.mult, ALU.add))
            v.sem_inc(S("order_ready"), 1)

        def order_pe(pe, o):
            pe.wait_ge(S("ends_made"), o + 1)
            nc.tensor.matmul(psC[:, 0:2 * P], ones[:, :], diag2[:, :, :].rearrange("p a b -> p (a b)"), start=True, stop=True).then_inc(S("ends_rows"), 1)

        def nodes_dve(v, o):
            q = line(v)
            q.did(nc.vector.tensor_scalar(nt_b[:, :], nid[:, :], 0.5, None, ALU.add))
            q.do(nc.vector.tensor_tensor(cmp_n, firstrow[:, :].unsqueeze(1).to_broadcast([P, NB, P]),
                                         nid[:, :].unsqueeze(2).to_broadcast([P, NB, P]), ALU.is_le))
            q.do(nc.vector.tensor_reduce(nt_q[:, :], cmp_n, AX.X, ALU.add))
            q.do(nc.vector.tensor_scalar(nt_q[:, :], nt_q[:, :], -1.0, 0.0, ALU.add, ALU.max))
            q.do(nc.vector.tensor_copy(nt_i[:, :], nt_q[:, :]))
            v.sem_inc(S("nt_made"), 1)
            v.wait_ge(S("nt_counted"), (o + 1) * NB)
            cum = nt_c[:, 1:NB + 1]
            q.do(nc.vector.tensor_scalar(cum, cum, 0.5, T / 2, ALU.mult, ALU.add))
            q.do(nc.vector.scalar_tensor_tensor(out=cum, in0=nt_q[:, :], scalar=float(T), in1=cum, op0=ALU.mult, op1=ALU.add))
            v.sem_inc(S("nt_made"), 1)
            v.wait_ge(S("nt_prev"), o + 1)
            has, prev = nt_f[:, 0, :], nt_f[:, 1, :]
            q.do(nc.vector.tensor_copy(prev, psD[:, 0:NB]))
            q.do(nc.vector.tensor_tensor(has, cum, prev, ALU.is_gt))
            q.do(nc.vector.scalar_tensor_tensor(out=cum, in0=cum, scalar=-float(EP + 1), in1=has, op0=ALU.add, op1=ALU.mult))
            q.did(nc.vector.tensor_scalar(endix[:, :], cum, float(EP), None, ALU.add))
            q.do(nc.vector.tensor_scalar(nt_b[:, :], nid[:, :], float(EP), None, ALU.add))
            q.do(nc.vector.tensor_tensor(prev, prev, nt_b[:, :], ALU.subtract))
            q.do(nc.vector.tensor_tensor(prev, prev, has, ALU.mult))
            q.do(nc.vector.tensor_tensor(spos[:, :], prev, nt_b[:, :], ALU.add))
            v.sem_inc(S("nodes_ready"), 1)

        def nodes_pool(g_, o):
            g_.wait_ge(S("keyrow_out"), 16 * (o + 1))
            g_.wait_ge(S("nt_made"), 2 * o + 1)
            if o == 0:
                g_.sem_inc(S("nt_counted0"), 2)
                g_.sem_inc(S("nt_counted1"), 2)
            with g_.Fori(0, NG) as g:
                for b in range(2):
                    g_.wait_ge(S(f"nt_counted{b}"), g * 2 + (2 + o * 2 * NG))
                    g_.sem_inc(S("pool_go"), 1)
                    g_.tensor_copy(half_i[b][:, :], nt_i[:, bass.ds(g * BPG + 2 * b, 2)]).then_inc(S("nt_ix"), 1)
                    g_.wait_ge(S("nt_ix"), g * 2 + (o * 2 * NG + b + 1))
                    g_.sem_inc(S("pool_go"), 1)
                    for j in range(2):
                        g_.indirect_dma_start(rows4[b][:, j, :], None, keyrow_t[o], bass.IndirectOffsetOnAxis(ap=half_i[b][:, j:j + 1], axis=0))\
                          .then_inc(S(f"nt_in{b}"), 16)

        def nodes_act(act, o):
            act.wait_ge(S("nt_made"), 2 * o + 1)
            act.wait_ge(S("dummies"), DUMMIES)
            with act.Fori(0, NG) as g:
                for b in range(2):
                    act.wait_ge(S(f"nt_in{b}"), g * 32 + (o * 32 * NG + 32))
                    for j in range(2):
                        n = g * BPG + (2 * b + j)
                        nc.scalar.activation(rsign[:, 0:T], rows4[b][:, j, 0:T], ACT.Sign, scale=-1.0, bias=nt_b[:, bass.ds(n, 1)],
                                             accum_out=nt_c[:, bass.ds(n + 1, 1)]).then_inc(S("nt_counted"), 1)
                        act.wait_ge(S("nt_counted"), n + (o * NB + 1))
                    act.sem_inc(S(f"nt_counted{b}"), 2)

        def nodes_pe(pe, o):
            pe.wait_ge(S("nt_made"), 2 * o + 2)
            nc.tensor.matmul(psD[:, 0:NB], down1[:, :], nt_c[:, 1:NB + 1], start=True, stop=False)
            nc.tensor.matmul(psD[:, 0:NB], wrap1[:, :], nt_c[:, 0:NB], start=False, stop=True).then_inc(S("nt_prev"), 1)

        def spread_sp(sp, o, t):
            sp.wait_ge(S("j0_out"), 16 * 3 * NG)

            def load(g, b):
                sp.dma_start(hst[:, 2 * b:2 * b + 2, :], grows(t, g)[:, 2 * b:2 * b + 2, :]).then_inc(S(f"spread_in{b}"), 16)

            load(0, 0)
            load(0, 1)
            with sp.Fori(1, NG) as g:
                for b in range(2):
                    sp.wait_ge(S(f"spread_out{b}"), g * 32 + o * 32 * NG)
                    load(g, b)

        def spread_pool(g_, o, t):
            g_.wait_ge(S("nodes_ready"), o + 1)
            g_.wait_ge(S("zeroed"), 32)
            if o:
                g_.wait_ge(S("zeroed_a"), 16 * (IT // 2))
            with g_.Fori(0, NG) as g:
                for b in range(2):
                    g_.wait_ge(S(f"spread_in{b}"), g * 16 + (o * 16 * NG + 16))
                    g_.sem_inc(S("pool_go"), 1)
                    g_.tensor_copy(half_i[b][:, :], spos[:, bass.ds(g * BPG + 2 * b, 2)]).then_inc(S("spread_ix"), 1)
                    g_.wait_ge(S("spread_ix"), g * 2 + (o * 2 * NG + b + 1))
                    g_.sem_inc(S("pool_go"), 1)
                    for j in range(2):
                        g_.indirect_dma_start(t, bass.IndirectOffsetOnAxis(ap=half_i[b][:, j:j + 1], axis=0), hst[:, 2 * b + j, :], None)\
                          .then_inc(S(f"spread_out{b}"), 16)

        def payload_in(sp, c):
            sp.wait_ge(S("attr_free"), c + 1)
            r0 = c * (P * KE)
            if isinstance(c, int) and c == NPAY - 1:
                left = E - c * P * KE
                w = left // KE
                parts = [(0, w // 16 * 16, KE), (w // 16 * 16, w, KE), (w, w + 1, left - w * KE)]
            else:
                parts = [(0, P, KE)]
            for j, (a, z, k) in enumerate(parts):
                done = S("attr_in") if j == len(parts) - 1 else S("attr_part")
                if j and j == len(parts) - 1:
                    sp.wait_ge(S("attr_part"), 16 * 3 * j)
                r, n = r0 + a * KE, (z - a) * k
                sp.dma_start(attr[a:z, 0:k, :], A["edge_attr_64"][bass.ds(r, n), :].rearrange("(p t) w -> p t w", t=k)).then_inc(done, 16)
                sp.dma_start(pcol_i[a:z, 0:k], A["src"][bass.ds(r, n)].rearrange("(p t) -> p t", t=k)).then_inc(done, 16)
                sp.dma_start(pcol_f[a:z, 0:k], A["edge_weight"][bass.ds(r, n)].rearrange("(p t) -> p t", t=k)).then_inc(done, 16)

        def payload_out(sp, c):
            sp.wait_ge(S("pay_made"), c + 1)
            for t in (pay_dram, paya_dram):
                sp.dma_start(t[bass.ds(c * (P * KE), P * KE), :].rearrange("(p t) w -> p t w", t=KE), pay0[:, :, :]).then_inc(S("pay_out"), 16)

        def payload_pe(pe):
            with pe.Fori(0, NPAY) as c:
                pe.wait_ge(S("attr_in"), c * 48 + 48)
                for u in range(KE // 2):
                    ins = nc.tensor.transpose(psB[:, u // 4, (u % 4) * P:(u % 4 + 1) * P],
                                              attr[:, 2 * u:2 * u + 2, :].rearrange("p a w -> p (a w)"), ident[:, :])
                ins.then_inc(S("attr_tr"), 1)
                pe.wait_ge(S("attrT_in"), c + 1)
                for u in range(KE // 2):
                    nc.tensor.matmul(psD[:, u * 16:(u + 1) * 16], attrT[:, u, :], we2[:, :], start=True, stop=False)
                    ins = nc.tensor.matmul(psD[:, u * 16:(u + 1) * 16], ones[0:1, :], be2[:, :], start=False, stop=True)
                ins.then_inc(S("pay_mm"), 1)

        def payload_act(act, c):
            act.wait_ge(S("attr_tr"), c + 1)
            nc.scalar.copy(attrT[:, :, :].rearrange("p a b -> p (a b)"), psB[:, :, :].rearrange("p a b -> p (a b)")[:, 0:KE // 2 * P])\
              .then_inc(S("attrT_in"), 1)
            act.wait_ge(S("pay_out"), c * 32 + 32)
            nc.scalar.copy(pay0[:, :, 0:1].rearrange("p t w -> p (t w)"), pcol_i[:, :]).then_inc(S("pay_cols"), 1)
            nc.scalar.copy(pay0[:, :, 1:2].rearrange("p t w -> p (t w)"), pcol_f[:, :]).then_inc(S("pay_cols"), 1)
            act.wait_ge(S("pay_cols"), c * 2 + 2)
            act.sem_inc(S("attr_free"), 1)
            act.wait_ge(S("pay_mm"), c + 1)
            nc.scalar.copy(pay0[:, :, 2:10], psD[:, 0:KE // 2 * 16].rearrange("p (t w) -> p t w", w=8)).then_inc(S("pay_made"), 1)

        def paysort_pool(g_):
            g_.wait_ge(S("eid_ready"), 1)
            g_.wait_ge(S("pay_out"), 32 * NPAY + 32)
            with g_.Fori(0, IT // 2) as i:
                for b in range(2):
                    g_.wait_ge(S(f"paya_out{b}"), i * 16 + 16)
                    g_.wait_ge(S(f"paya_cols{b}"), i * 2 + 1)
                    g_.sem_inc(S("pool_go"), 1)
                    g_.tensor_copy(ix_s[b][:, :], eid_a[:, bass.ds(i * (2 * K) + b * K, K)]).then_inc(S(f"paya_ix{b}"), 1)
                    g_.wait_ge(S(f"paya_ix{b}"), i + 1)
                    g_.sem_inc(S("pool_go"), 1)
                    for k in range(K):
                        g_.indirect_dma_start(pay[b][:, k, :], None, pay_dram, bass.IndirectOffsetOnAxis(ap=ix_s[b][:, k:k + 1], axis=0))\
                          .then_inc(S(f"paya_in{b}"), 16)

        def paysort_dve(v):
            for b in range(2):
                v.sem_inc(S(f"paya_cols{b}"), 1)
            with v.Fori(0, IT // 2) as i:
                for b in range(2):
                    v.wait_ge(S(f"paya_in{b}"), i * (16 * K) + 16 * K)
                    cols = bass.ds(i * (2 * K) + b * K, K)
                    nc.vector.tensor_copy(oth_i[:, cols], pay[b][:, :, 0]).then_inc(S(f"paya_cols{b}"), 1)
                    nc.vector.tensor_copy(ew[:, cols], pay[b][:, :, 1]).then_inc(S(f"paya_cols{b}"), 1)
            for b in range(2):
                v.wait_ge(S(f"paya_cols{b}"), IT + 1)

        def paysort_sp(sp):
            for b in range(2):
                sp.sem_inc(S(f"paya_out{b}"), 16)
            with sp.Fori(0, IT // 2) as i:
                for b in range(2):
                    sp.wait_ge(S(f"paya_in{b}"), i * (16 * K) + 16 * K)
                    sp.dma_start(paya_dram.rearrange("(p t) w -> p t w", t=T)[:, bass.ds(i * (2 * K) + b * K, K), :],
                                 pay[b][:, :, :]).then_inc(S(f"paya_out{b}"), 16)

            for b in range(2):
                sp.wait_ge(S(f"paya_out{b}"), 16 * (IT // 2) + 16)

        def pass_pool(g_, q):
            wd_s = q.tabs.shape[1]
            for nm in q.needs:
                g_.wait_ge(S(nm[0]), nm[1])
            if q.near is not None:
                g_.indirect_dma_start(head[:, 0:q.HF], None, q.tabd, bass.IndirectOffsetOnAxis(ap=head_i[:, 0:1], axis=0)).then_inc(q.s("head_in"), 16)
            with g_.Fori(0, IT // 2) as i:
                for b in range(2):
                    g_.wait_ge(*q.on(f"free{b}", i + 1))
                    g_.sem_inc(S("pool_go"), 1)
                    for k in range(K):
                        g_.indirect_dma_start(rows_s[b][:, k, 0:wd_s], None, q.tabs, bass.IndirectOffsetOnAxis(ap=ix_s[b][:, k:k + 1], axis=0))\
                          .then_inc(q.own(f"rows{b}"), 16)

        def heads(t, q):
            return t[:, 0:q.H, :]

        def pass_dve(v, q):
            H, dh, F, HF = q.H, q.dh, q.F, q.HF
            f2 = lambda a: a.rearrange("p h t -> p (h t)")
            by_t = lambda a, f: a[:, 0:f * (K + 1)].rearrange("p (f t) -> p f t", t=K + 1)
            stv, bvv, ztv, hv = by_t(st, F), by_t(bv, F), by_t(zt, HF), by_t(hold, HF)
            bvh = bvv.rearrange("p (h j) t -> p h j t", h=H)
            p0 = Seq(v, q.s("prep"), q.base("prep"))
            p0.did(nc.vector.memset(stv, 0.0))
            p0.did(nc.vector.memset(m_ext[:, :, :], -BIG))
            p0.did(nc.vector.memset(by_t(nsb, D)[:, :, 0:1], 0.0))
            p0.did(nc.vector.memset(by_t(abig, D)[:, :, 0:1], 0.0))
            p0.wait()
            if q is PA:
                v.wait_ge(S("edges_ready"), 1)
            for b in range(2):
                nc.vector.tensor_copy(ix_s[b][:, :], oth_i[:, b * K:(b + 1) * K]).then_inc(q.s(f"free{b}"), 1)
            if q.near is not None:
                v.wait_ge(*q.on("head_in", 16))
                p0.do(nc.vector.tensor_copy(hv[:, :, K:K + 1], head[:, 0:HF].unsqueeze(2)))
            with v.Fori(0, IT // 2) as i:
                for b in range(2):
                    c = Seq(v, q.s("steps"), q.base("steps") + b * q.steps, i, 2 * q.steps)
                    t0 = i * (2 * K) + b * K
                    cols = bass.ds(t0, K)
                    rs, rd = rows_s[b], rows_d[b]
                    s = heads(s_ext, q)[:, :, 1:K + 1]
                    decay = abig if q.soft or b else nsb

                    def leave():
                        c.did(nc.vector.tensor_copy(ix_s[b][:, :], oth_i[:, bass.ds(t0 + 2 * K, K)]))
                        c.wait()
                        v.sem_inc(q.s(f"free{b}"), 1)

                    if q.near is not None:
                        c.did(nc.vector.tensor_copy(ztv[:, :, 0:1], hv[:, :, K:K + 1]))
                        v.wait_ge(*q.on("made", i * (2 * q.made) + (b + 1) * q.made))
                        c.wait()
                        n = HF * (K + 1)
                        c.do(nc.vector.tensor_tensor_scan(hold[:, 0:n], (nsb if q.soft or not b else abig)[:, 0:n], zt[:, 0:n], 0.0, ALU.mult, ALU.add))
                        v.sem_inc(q.s("held"), 1)
                    v.wait_ge(q.own(f"rows{b}"), i * (16 * K) + 16 * K)
                    if q in (PB, PA, P1):
                        c.do(nc.vector.tensor_tensor(rd[:, :, :], rs[:, :, 0:D], hv[:, :, 1:K + 1].rearrange("p f t -> p t f"), ALU.mult))
                        c.did(nc.vector.tensor_reduce(s.rearrange("p h t -> p t h"), rd[:, :, :].rearrange("p t (h d) -> p t h d", h=H), AX.X, ALU.add))
                    if q is PB:
                        leave()
                    if q is PA:
                        c.wait()
                        c.did(nc.vector.tensor_tensor(heads(ww, q), s, rs[:, :, 2 * D:2 * D + H].rearrange("p t h -> p h t"), ALU.subtract))
                    if q is P1:
                        v.wait_ge(S(f"bias_in{b}"), i * 16 + 16)
                        c.wait()
                        c.do(nc.vector.scalar_tensor_tensor(out=s, in0=s, scalar=float(dh) ** -0.5, in1=pay[b][:, :, 2:2 + H].rearrange("p t h -> p h t"),
                                                            op0=ALU.mult, op1=ALU.add))
                        v.sem_inc(S(f"bias_used{b}"), 1)
                    if q is P2:
                        c.do(nc.vector.tensor_tensor(s, rs[:, :, D:D + H].rearrange("p t h -> p h t"), hv[:, :, 1:K + 1], ALU.add))
                        c.do(nc.vector.scalar_tensor_tensor(out=s, in0=s, scalar=0.2, in1=s, op0=ALU.mult, op1=ALU.max))
                    if q.soft:
                        smx = heads(s_max, q) if q is P2 else heads(s_ext, q)
                        if q is P2:
                            c.did(nc.vector.tensor_scalar(smx[:, :, 1:K + 1], s, 0.0, None, ALU.max))
                        rsh, mx = heads(rst, q), heads(m_ext, q)
                        c.did(nc.vector.tensor_copy(smx[:, :, 0:1], mx[:, :, K:K + 1]))
                        c.did(nc.vector.tensor_copy(rsh[:, :, 1:K + 1], restart[:, cols].unsqueeze(1).to_broadcast([P, H, K])))
                        v.wait_ge(*q.on("laid", i * 2 + b + 1))
                        c.wait()
                        c.do(nc.vector.tensor_tensor_scan(f2(mx), f2(rsh), f2(smx), -BIG, ALU.add, ALU.max))
                        c.did(nc.vector.tensor_tensor(heads(dtmp, q), mx[:, :, 0:K], mx[:, :, 1:K + 1], ALU.subtract))
                        c.did(nc.vector.tensor_tensor(heads(ww, q), s, mx[:, :, 1:K + 1], ALU.subtract))
                        c.wait()
                        c.did(nc.vector.tensor_tensor(heads(dd, q)[:, :, 1:K + 1], heads(dtmp, q), rsh[:, :, 1:K + 1], ALU.add))
                    if q.soft or q is PA:
                        c.wait()
                        v.sem_inc(q.s("arg"), 1)
                    if q is P3:
                        c.did(nc.vector.tensor_tensor(bvv[:, :, 1:K + 1], rs[:, :, 0:D].rearrange("p t f -> p f t"),
                                                      ew[:, cols].unsqueeze(1).to_broadcast([P, D, K]), ALU.mult))
                    elif q is PA:
                        v.wait_ge(*q.on("expw", i * 2 + b + 1))
                        c.did(nc.vector.tensor_tensor(bvh[:, :, :, 1:K + 1], rs[:, :, D:2 * D].rearrange("p t (h j) -> p h j t", h=H),
                                                      heads(ww, q).unsqueeze(2).to_broadcast([P, H, 32, K]), ALU.mult))
                    elif dh:
                        v.wait_ge(*q.on("expw", i * 2 + b + 1))
                        off = D if q is P1 else 0
                        c.did(nc.vector.tensor_tensor(bvh[:, :, 0:dh, 1:K + 1], rs[:, :, off:off + D].rearrange("p t (h j) -> p h j t", h=H),
                                                      bvh[:, :, dh:dh + 1, 1:K + 1].to_broadcast([P, H, dh, K]), ALU.mult))
                    c.did(nc.vector.tensor_copy(bvv[:, :, 0:1], stv[:, :, K:K + 1]))
                    if q is not PB:
                        leave()
                    c.wait()
                    if q.soft:
                        v.wait_ge(*q.on("decay", i * 2 + b + 1))
                    else:
                        v.wait_ge(*q.on("made", i * (2 * q.made) + (b + 1) * q.made))
                        v.wait_ge(*q.on("laid", i * 2 + b + 1))
                    c.do(nc.vector.tensor_tensor_scan(st[:, 0:F * (K + 1)], decay[:, 0:F * (K + 1)], bv[:, 0:F * (K + 1)], 0.0, ALU.mult, ALU.add))
                    v.sem_inc(q.s("scanned"), 1)
                    assert c.k == q.steps, (q.name, c.k, q.steps)

        def near_act(act, q, i, b):
            by_t = lambda a: a[:, 0:q.HF * (K + 1)].rearrange("p (f t) -> p f t", t=K + 1)[:, :, 1:K + 1]
            first = isinstance(i, int) and i == 0
            if q.near is not None:
                act.wait_ge(*q.on(f"near_in{b}", i * 16 + 16))
                if not (first and b == 0):
                    act.wait_ge(*q.on("held", i * 2 + b))
                nc.scalar.copy(by_t(zt), rows_d[b][:, :, :].rearrange("p t w -> p (t w)")[:, 0:K * q.HF].rearrange("p (t f) -> p f t", f=q.HF))\
                  .then_inc(q.s("made"), 1)
            nc.scalar.activation(by_t(nsb if q.soft or not b else abig), restart[:, bass.ds(i * (2 * K) + b * K, K)].unsqueeze(1).to_broadcast([P, q.HF, K]),
                                 ACT.Exp).then_inc(q.s("made"), 1)

        def pass_act(act, q):
            H, dh, F, W = q.H, q.dh, q.F, q.W
            act.sem_inc(q.s("laid"), 1)
            act.wait_ge(*q.on("prep", 4))
            bvh = bv[:, 0:F * (K + 1)].rearrange("p (h j t) -> p h j t", h=H, t=K + 1)
            stv = st[:, 0:F * (K + 1)].rearrange("p (f t) -> p f t", t=K + 1)

            def two(i, last):
                if q is PB:
                    payload_act(act, i)
                for b in range(2):
                    if q.soft or q is PA:
                        act.wait_ge(*q.on("arg", i * 2 + b + 1))
                    if q.soft:
                        nc.scalar.activation(bvh[:, :, dh, 1:K + 1], heads(ww, q), ACT.Exp).then_inc(q.s("expw"), 1)
                        nc.scalar.activation(abig[:, 0:F * (K + 1)].rearrange("p (h j t) -> p h j t", h=H, t=K + 1),
                                             heads(dd, q).unsqueeze(2).to_broadcast([P, H, dh + 1, K + 1]), ACT.Exp).then_inc(q.s("decay"), 1)
                    elif q is PA:
                        nc.scalar.activation(heads(ww, q), heads(ww, q), ACT.Exp).then_inc(q.s("expw"), 1)
                    if not (last and b):
                        near_act(act, q, i + b, 1 - b)
                    act.wait_ge(*q.on("scanned", i * 2 + b + 1))
                    act.wait_ge(*q.on(f"sent{b}", i * 16 + 16))
                    pr = psrow[b][:, 0:K * W].rearrange("p (t w) -> p t w", w=W)
                    ins = nc.scalar.copy(pr[:, :, 0:F], stv[:, :, 1:K + 1].rearrange("p f t -> p t f"))
                    if q.soft:
                        ins = nc.scalar.copy(pr[:, :, F:F + H], heads(m_ext, q)[:, :, 1:K + 1].rearrange("p h t -> p t h"))
                    if q is PB:
                        ins = nc.scalar.copy(pr[:, :, F + H:F + H + 1].rearrange("p t w -> p (t w)"), cnt[:, bass.ds(i * (2 * K) + b * K, K)])
                    ins.then_inc(q.s("laid"), 1)
                    act.wait_ge(*q.on("laid", i * 2 + b + 2))
                    act.sem_inc(q.s(f"laid{b}"), 1)

            near_act(act, q, 0, 0)
            with act.Fori(0, IT // 2 - 1) as i:
                two(i, False)
            two(IT // 2 - 1, True)

        def pass_store(sp, q, i, b):
            sp.wait_ge(*q.on(f"laid{b}", i + 1))
            sp.dma_start(q.ps[0:EP, :].rearrange("(p t) w -> p t w", t=T)[:, bass.ds(i * (2 * K) + b * K, K), :],
                         psrow[b][:, 0:K * q.W].rearrange("p (t w) -> p t w", w=q.W)).then_inc(q.s(f"sent{b}"), 16)

        def bias_load(sp, n, b):
            sp.dma_start(pay[b][:, :, :], paya_dram.rearrange("(p t) w -> p t w", t=T)[:, bass.ds(n * (2 * K) + b * K, K), :])\
              .then_inc(S(f"bias_in{b}"), 16)

        def near_load(sp, q, i, b):
            sp.dma_start(rows_d[b][:, :, :].rearrange("p t w -> p (t w)")[:, 0:K * q.HF].rearrange("p (t w) -> p t w", w=q.HF),
                         q.near[0:EP, :].rearrange("(p t) w -> p t w", t=T)[:, bass.ds(i * (2 * K) + b * K, K), :]).then_inc(q.s(f"near_in{b}"), 16)

        def pass_sp(sp, q):
            for b in range(2):
                sp.sem_inc(q.s(f"sent{b}"), 16)
            if q is PB:
                sp.sem_inc(S("pay_out"), 32)
            if q.near is not None:
                for nm in q.started:
                    sp.wait_ge(S(nm[0]), nm[1])
            for b in range(2):
                if q.near is not None:
                    near_load(sp, q, 0, b)
                if q is P1:
                    bias_load(sp, 0, b)

            def two(i, last):
                if q is PB:
                    payload_in(sp, i)
                    zeros_chunk_sp(sp, i)
                for b in range(2):
                    if not last and q.near is not None:
                        sp.wait_ge(*q.on(f"free{b}", i + 2))
                        near_load(sp, q, i + 1, b)
                    if not last and q is P1:
                        sp.wait_ge(S(f"bias_used{b}"), i + 1)
                        bias_load(sp, i + 1, b)
                    pass_store(sp, q, i, b)
                if q is PB:
                    payload_out(sp, i)

            with sp.Fori(0, IT // 2 - 1) as i:
                two(i, False)
            two(IT // 2 - 1, True)

        def carry_dve(v, q):
            H, dh, F = q.H, q.dh, q.F
            c = line(v)
            stv = st[:, 0:F * (K + 1)].rearrange("p (f t) -> p f t", t=K + 1)
            v.wait_ge(*q.on("laid", IT + 1))
            c.do(nc.vector.tensor_copy(cst[:, 0:F].unsqueeze(2), stv[:, :, K:K + 1]))
            if q is PB:
                c.do(nc.vector.tensor_copy(cst[:, F:F + 1], cnt[:, T - 1:T]))
            if q.soft:
                dw = dwide[:, 0:H * P].rearrange("p (h r) -> p h r", h=H)
                c.do(nc.vector.tensor_tensor(dw, ident[:, :].unsqueeze(1).to_broadcast([P, H, P]),
                                             heads(m_ext, q)[:, :, K:K + 1].to_broadcast([P, H, P]), ALU.mult))
                v.sem_inc(q.s("carry_dve"), 1)
                v.wait_ge(*q.on("carry_pe", 1))
                pm = psC[:, 0:H * P].rearrange("p (h r) -> p h r", h=H)
                c.do(nc.vector.tensor_tensor(dw, pm, bias2[:, :].unsqueeze(1).to_broadcast([P, H, P]), ALU.add))
                c.do(nc.vector.tensor_reduce(mcar[:, 0:H], dw, AX.X, ALU.max))
                c.do(nc.vector.tensor_tensor(dw, dw, mcar[:, 0:H].unsqueeze(2).to_broadcast([P, H, P]), ALU.subtract))
                v.sem_inc(q.s("carry_dve"), 1)
            else:
                v.sem_inc(q.s("carry_dve"), 1)
            v.wait_ge(*q.on("prow_in", 16))
            if q.soft:
                m = pmx[:, :, 0:H]
                pm = prow[:, F:F + H]
                c.do(nc.vector.tensor_tensor(m[:, 0], pm, mcar[:, 0:H], ALU.max))
                c.did(nc.vector.tensor_tensor(m[:, 1], pm, m[:, 0], ALU.subtract))
                c.did(nc.vector.tensor_tensor(m[:, 2], mcar[:, 0:H], m[:, 0], ALU.subtract))
                c.wait()
                v.sem_inc(q.s("carry_dve"), 1)
                v.wait_ge(*q.on("carry_act", 4))
                by_h = lambda a: a.rearrange("p (h d) -> p h d", h=H)
                wide = lambda k: m[:, k].unsqueeze(2).to_broadcast([P, H, dh + 1])
                v.wait_ge(*q.on("carry_pe", 3))
                c.did(nc.vector.tensor_tensor(by_h(prow[:, 0:F]), by_h(prow[:, 0:F]), wide(1), ALU.mult))
                c.did(nc.vector.tensor_tensor(by_h(cst[:, 0:F]), by_h(psD[:, 0:F]), wide(2), ALU.mult))
                c.did(nc.vector.tensor_copy(pm, m[:, 0]))
                c.wait()
                c.did(nc.vector.tensor_tensor(prow[:, 0:F], prow[:, 0:F], cst[:, 0:F], ALU.add))
                if q is PB:
                    c.did(nc.vector.tensor_tensor(prow[:, F + H:F + H + 1], prow[:, F + H:F + H + 1], psD[:, F:F + 1], ALU.add))
            else:
                v.wait_ge(*q.on("carry_pe", 1))
                c.did(nc.vector.tensor_tensor(prow[:, 0:F], prow[:, 0:F], psD[:, 0:F], ALU.add))
            c.wait()
            v.sem_inc(q.s("patched"), 1)

        def carry_pool(g_, q):
            for b in range(2):
                g_.wait_ge(*q.on(f"sent{b}", 16 * (IT // 2) + 16))
            at = bass.IndirectOffsetOnAxis(ap=patch_i[:, 0:1], axis=0)
            g_.indirect_dma_start(prow[:, 0:q.W], None, q.ps, at).then_inc(q.s("prow_in"), 16)
            g_.wait_ge(*q.on("patched", 1))
            g_.indirect_dma_start(q.ps, at, prow[:, 0:q.W], None).then_inc(q.s("prow_out"), 16)

        def carry_pe(pe, q):
            H, dh, F = q.H, q.dh, q.F
            pe.wait_ge(*q.on("carry_dve", 1))
            if not q.soft:
                nc.tensor.matmul(psD[:, 0:F], contT[:, :], cst[:, 0:F], start=True, stop=True).then_inc(q.s("carry_pe"), 1)
                return
            for a in range(0, H * P, 512):
                ins = nc.tensor.matmul(psC[:, a:a + 512], ones[:, :], dwide[:, a:a + 512], start=True, stop=True)
            ins.then_inc(q.s("carry_pe"), 1)
            pe.wait_ge(*q.on("carry_act", 1))
            for h in range(H):
                ins = nc.tensor.transpose(psB[:, h // 4, (h % 4) * P:(h % 4 + 1) * P], wwide[:, h * P:(h + 1) * P], ident[:, :])
            ins.then_inc(q.s("carry_pe"), 1)
            pe.wait_ge(*q.on("carry_act", 2))
            for h in range(H):
                f = slice(h * (dh + 1), (h + 1) * (dh + 1))
                ins = nc.tensor.matmul(psD[:, f], dwide[:, h * P:(h + 1) * P], cst[:, f], start=True, stop=True)
            if q is PB:
                ins = nc.tensor.matmul(psD[:, F:F + 1], contT[:, :], cst[:, F:F + 1], start=True, stop=True)
            ins.then_inc(q.s("carry_pe"), 1)

        def carry_act(act, q):
            if not q.soft:
                return
            n = q.H * P
            act.wait_ge(*q.on("carry_dve", 2))
            nc.scalar.activation(wwide[:, 0:n], dwide[:, 0:n], ACT.Exp).then_inc(q.s("carry_act"), 1)
            act.wait_ge(*q.on("carry_pe", 2))
            nc.scalar.copy(dwide[:, 0:n], psB[:, :, :].rearrange("p a b -> p (a b)")[:, 0:n]).then_inc(q.s("carry_act"), 1)
            act.wait_ge(*q.on("carry_dve", 3))
            for k in (1, 2):
                nc.scalar.activation(pmx[:, k, 0:q.H], pmx[:, k, 0:q.H], ACT.Exp).then_inc(q.s("carry_act"), 1)

        def ends_pool(g_, q):
            g_.wait_ge(*q.on("prow_out", 16))
            g_.wait_ge(S("dummy_rows"), 16 * NDUMMY)
            with g_.Fori(0, NG) as g:
                g_.wait_ge(*q.on("ends_free", g + 1))
                g_.sem_inc(S("pool_go"), 1)
                g_.tensor_copy(fe_i[:, :], endix[:, bass.ds(g * BPG, BPG)]).then_inc(q.s("fix"), 1)
                g_.wait_ge(*q.on("fix", g + 1))
                g_.sem_inc(S("pool_go"), 1)
                for j in range(BPG):
                    g_.indirect_dma_start(end4[:, j, 0:q.W], None, q.ps, bass.IndirectOffsetOnAxis(ap=fe_i[:, j:j + 1], axis=0)).then_inc(q.s("ends_in"), 16)

        MERGE = {True: 1, False: 0}

        def merge_dve(v, q, g, c):
            v.wait_ge(*q.on("ends_in", g * (16 * BPG) + 16 * BPG))
            if q.soft:
                c.do(nc.vector.tensor_scalar(mx4[:, 1, :, 0:q.H], end4[:, :, 0:q.F].rearrange("p j (h d) -> p j h d", h=q.H)[:, :, :, q.dh],
                                             1e-10, None, ALU.max if q is PB else ALU.add))

        def stats_dve(v):
            q = PB
            v.sem_inc(q.s("ends_free"), 1)
            per = MERGE[True] + 4
            with v.Fori(0, NG) as g:
                c = Seq(v, S("stats_steps"), 0, g, per)
                merge_dve(v, q, g, c)
                n = q.F + q.H
                c.did(nc.vector.tensor_copy(mx4[:, 0, :, 0:H0], end4[:, :, q.F:n]))
                c.do(nc.vector.reciprocal(mx4[:, 1, :, 0:H0], mx4[:, 1, :, 0:H0]))
                c.do(nc.vector.tensor_tensor(mx4[:, 1, :, 0:H0], mx4[:, 1, :, 0:H0], end4[:, :, n:n + 1].to_broadcast([P, BPG, H0]), ALU.mult))
                v.wait_ge(S("qm_in"), g * 32 + 32)
                hv = hst2[:, :, :].rearrange("p j (h d) -> p j h d", h=H0)
                c.do(nc.vector.tensor_tensor(hv, hv, mx4[:, 1, :, 0:H0].unsqueeze(3).to_broadcast([P, BPG, H0, D // H0]), ALU.mult))
                assert c.k == per
                v.sem_inc(S("qm_made"), 1)
                v.sem_inc(q.s("ends_free"), 1)
                v.wait_ge(S("qm_free"), g + 2)
            v.sem_inc(S("stats_done"), 1)

        def stats_sp(sp):
            sp.sem_inc(S("qm_free"), 1)
            sp.wait_ge(S("j0_out"), 16 * 3 * NG)
            with sp.Fori(0, NG) as g:
                sp.wait_ge(S("qm_free"), g + 1)
                sp.dma_start(hst[:, :, :], grows(q0_t, g)).then_inc(S("qm_in"), 16)
                sp.dma_start(hst2[:, :, :], grows(m0_t, g)).then_inc(S("qm_in"), 16)
                sp.wait_ge(S("qm_made"), g + 1)
                sp.dma_start(grows(qm0_t, g)[:, :, 0:D], hst[:, :, :]).then_inc(S("qm_out"), 16)
                sp.dma_start(grows(qm0_t, g)[:, :, D:2 * D], hst2[:, :, :]).then_inc(S("qm_out"), 16)
                sp.dma_start(grows(qm0_t, g)[:, :, 2 * D:2 * D + H0], mx4[:, 0, :, 0:H0]).then_inc(S("qm_out"), 16)
                sp.wait_ge(S("qm_out"), g * 48 + 48)
                sp.sem_inc(S("qm_free"), 1)

        def end0_dve(v):
            q = PA
            v.sem_inc(q.s("ends_free"), 1)
            with v.Fori(0, NG) as g:
                c = Seq(v, S("e0_steps"), 0, g, 1)
                merge_dve(v, q, g, c)
                v.wait_ge(S("e0_tr"), g + 1)
                c.do(nc.vector.tensor_copy(hst[:, :, :], end4[:, :, 0:D]))
                v.sem_inc(q.s("ends_free"), 1)
            c = line(v)
            v.wait_ge(S("e0_hid"), NG)
            hid = hT_all[:, 0:N]
            c.do(nc.vector.tensor_reduce(bncol[:, 3:4], hid, AX.X, ALU.add))
            c.do(nc.vector.tensor_scalar(bncol[:, 3:4], bncol[:, 3:4], -1.0 / N, None, ALU.mult))
            c.do(nc.vector.tensor_scalar(hT_all[:, :], hT_all[:, :], bncol[:, 3:4], None, ALU.add))
            v.sem_inc(S("bn_by_dve"), 1)
            v.wait_ge(S("bn_by_act"), 1)
            c.do(nc.vector.tensor_scalar(bncol[:, 4:5], bncol[:, 4:5], 1.0 / N, EPS, ALU.mult, ALU.add))
            v.sem_inc(S("bn_by_dve"), 1)
            v.wait_ge(S("bn_by_act"), 2)
            c.do(nc.vector.reciprocal(bncol[:, 5:6], bncol[:, 5:6]))
            c.do(nc.vector.tensor_tensor(bncol[:, 5:6], bncol[:, 5:6], bncol[:, 1:2], ALU.mult))
            v.sem_inc(S("bn_by_dve"), 1)
            with v.Fori(0, NG) as g:
                v.wait_ge(S("e0_mm"), g + 1)
                xg = xsb[:, bass.ds(g * BPG, BPG), :]
                nc.vector.tensor_tensor(xg, xg, psB[:, 0, :].rearrange("p (j d) -> p j d", j=BPG), ALU.add).then_inc(S("e0_added"), 1)
                v.wait_ge(S("e0_added"), g + 2)

        def end0_pe(pe):
            pe.sem_inc(S("e0_tr"), 1)
            with pe.Fori(0, NG) as g:
                pe.wait_ge(S("e0_steps"), g + 1)
                pe.wait_ge(S("e0_at"), g + 1)
                for j in range(BPG):
                    ins = nc.tensor.transpose(psA[:, j * P:(j + 1) * P], hst[:, j, :], ident[:, :])
                ins.then_inc(S("e0_tr"), 1)
                pe.wait_ge(S("e0_at"), g + 2)
                pe.wait_ge(S("e0_hid0"), g + 1)
                nc.tensor.matmul(psD[:, :], w1_0[:, :], hT[:, 0, :], start=True, stop=True).then_inc(S("e0_w1"), 1)
            with pe.Fori(0, NG) as g:
                pe.wait_ge(S("e0_relu"), g + 1)
                pe.wait_ge(S("e0_added"), g + 1)
                for j in range(BPG):
                    nc.tensor.matmul(psB[:, 0, j * P:(j + 1) * P], hT[:, 1, j * P:(j + 1) * P], w2_0[:, :], start=True, stop=False)
                    ins = nc.tensor.matmul(psB[:, 0, j * P:(j + 1) * P], ones[0:1, :], b2_0[:, :], start=False, stop=True)
                ins.then_inc(S("e0_mm"), 1)

        def end0_act(act):
            act.sem_inc(S("e0_at"), 1)
            act.sem_inc(S("e0_hid0"), 1)
            act.sem_inc(S("e0_added"), 1)
            with act.Fori(0, NG) as g:
                act.wait_ge(S("e0_tr"), g + 2)
                nc.scalar.copy(hT[:, 0, :], psA[:, :]).then_inc(S("e0_at"), 1)
                act.wait_ge(S("e0_w1"), g + 1)
                nc.scalar.activation(hT_all[:, bass.ds(g * GN, GN)], psD[:, :], ACT.Identity, bias=bncol[:, 0:1]).then_inc(S("e0_hid"), 1)
                act.wait_ge(S("e0_hid"), g + 1)
                act.sem_inc(S("e0_hid0"), 1)
            act.wait_ge(S("bn_by_dve"), 1)
            nc.scalar.activation(work[:, 0:N], hT_all[:, 0:N], ACT.Square, accum_out=bncol[:, 4:5]).then_inc(S("bn_by_act"), 1)
            act.wait_ge(S("bn_by_dve"), 2)
            nc.scalar.activation(bncol[:, 5:6], bncol[:, 4:5], ACT.Sqrt).then_inc(S("bn_by_act"), 1)
            act.wait_ge(S("bn_by_dve"), 3)
            with act.Fori(0, NG) as g:
                act.wait_ge(S("e0_added"), g + 1)
                nc.scalar.activation(hT[:, 1, :], hT_all[:, bass.ds(g * GN, GN)], ACT.Relu, bias=bncol[:, 2:3], scale=bncol[:, 5:6])\
                  .then_inc(S("e0_relu"), 1)

        def end12_dve(v, q):
            v.sem_inc(q.s("ends_free"), 1)
            per = MERGE[True] + 2
            with v.Fori(0, NG) as g:
                c = Seq(v, q.own("end_steps"), 0, g, per)
                merge_dve(v, q, g, c)
                c.do(nc.vector.reciprocal(mx4[:, 1, :, 0:q.H], mx4[:, 1, :, 0:q.H]))
                if q is P1:
                    v.wait_ge(S("e1_tr"), g + 1)
                c.do(nc.vector.tensor_tensor(hst[:, :, :].rearrange("p j (h d) -> p j h d", h=q.H),
                                             end4[:, :, 0:q.F].rearrange("p j (h d) -> p j h d", h=q.H)[:, :, :, 0:q.dh],
                                             mx4[:, 1, :, 0:q.H].unsqueeze(3).to_broadcast([P, BPG, q.H, q.dh]), ALU.mult))
                v.sem_inc(q.s("ends_free"), 1)
                assert c.k == per, c.k
                xg = xsb[:, bass.ds(g * BPG, BPG), :]
                if q is P1:
                    v.wait_ge(S("e1_mm"), g + 1)
                    nc.vector.tensor_tensor(xg, xg, psB[:, 0, :].rearrange("p (j d) -> p j d", j=BPG), ALU.add).then_inc(S("e1_added"), 1)
                    v.wait_ge(S("e1_added"), g + 1)
                else:
                    nc.vector.tensor_tensor(xg, xg, hst[:, :, :], ALU.add).then_inc(S("e2_added"), 1)
                    v.wait_ge(S("e2_added"), g + 1)

        def end1_pe(pe):
            pe.sem_inc(S("e1_tr"), 1)
            per = MERGE[True] + 2
            with pe.Fori(0, NG) as g:
                pe.wait_ge(P1.own("end_steps"), g * per + per)
                for j in range(BPG):
                    ins = nc.tensor.transpose(psA[:, j * P:(j + 1) * P], hst[:, j, :], ident[:, :])
                ins.then_inc(S("e1_tr"), 1)
                pe.wait_ge(S("e1_at"), g + 1)
                for j in range(BPG):
                    nc.tensor.matmul(psB[:, 0, j * P:(j + 1) * P], hT[:, 0, j * P:(j + 1) * P], wo_1[:, :], start=True, stop=False)
                    ins = nc.tensor.matmul(psB[:, 0, j * P:(j + 1) * P], ones[0:1, :], bo_1[:, :], start=False, stop=True)
                ins.then_inc(S("e1_mm"), 1)

        def end1_act(act):
            with act.Fori(0, NG) as g:
                act.wait_ge(S("e1_tr"), g + 2)
                nc.scalar.copy(hT[:, 0, :], psA[:, :]).then_inc(S("e1_at"), 1)

        def weights3_pe(pe):
            pe.wait_ge(S("loaded"), 16 * NLOADS)
            pe.wait_ge(S("consts"), CONSTS)
            for j in range(2):
                ins = nc.tensor.transpose(psA[:, j * P:(j + 1) * P], w3raw[:, j, :], ident[:, :])
            ins.then_inc(S("w3_tr"), 1)
            pe.wait_ge(S("w3_in"), 1)

        def weights3_act(act):
            act.wait_ge(S("w3_tr"), 1)
            nc.scalar.copy(w3t[:, :, :].rearrange("p a b -> p (a b)"), psA[:, 0:2 * P]).then_inc(S("w3_in"), 1)

        E3 = 5

        def end3_dve(v):
            q = P3
            v.sem_inc(q.s("ends_free"), 1)
            with v.Fori(0, NG) as g:
                c = Seq(v, S("e3_steps"), 0, g, E3)
                merge_dve(v, q, g, c)
                v.wait_ge(S("h3_in"), g * 16 + 16)
                v.wait_ge(S("y_out"), g * 16 + 16)
                c.did(nc.vector.tensor_tensor(hst[:, :, :], end4[:, :, 0:D], hst2[:, :, :], ALU.add))
                c.do(nc.vector.tensor_tensor(end4[:, :, 0:D], end4[:, :, 0:D], hst2[:, :, :], ALU.mult))
                v.sem_inc(S("h3_free"), 1)
                v.wait_ge(S("e3_mm"), g + 1)
                c.do(nc.vector.tensor_copy(hst[:, :, :], psB[:, 2, :].rearrange("p (j d) -> p j d", j=BPG)))
                v.sem_inc(q.s("ends_free"), 1)
                c.do(nc.vector.scalar_tensor_tensor(out=hst[:, :, :], in0=hst[:, :, :], scalar=0.2, in1=hst[:, :, :], op0=ALU.mult, op1=ALU.max))
                c.do(nc.vector.tensor_tensor(hst[:, :, :], hst[:, :, :], xsb[:, bass.ds(g * BPG, BPG), :], ALU.add))
                assert c.k == E3, c.k

        def end3_pe(pe):
            with pe.Fori(0, NG) as g:
                pe.wait_ge(S("e3_steps"), g * E3 + 2)
                for u, t in ((0, hst), (1, end4)):
                    for j in range(BPG):
                        ins = nc.tensor.transpose(psB[:, u, j * P:(j + 1) * P], t[:, j, 0:D], ident[:, :])
                ins.then_inc(S("e3_tr"), 1)
                pe.wait_ge(S("e3_at"), g + 1)
                for j in range(BPG):
                    o = psB[:, 2, j * P:(j + 1) * P]
                    for u in range(2):
                        nc.tensor.matmul(o, hT[:, u, j * P:(j + 1) * P], w3t[:, u, :], start=(u == 0), stop=False)
                        ins = nc.tensor.matmul(o, ones[0:1, :], b3[:, u, :], start=False, stop=(u == 1))
                ins.then_inc(S("e3_mm"), 1)

        def end3_act(act):
            with act.Fori(0, NG) as g:
                act.wait_ge(S("e3_tr"), g + 1)
                nc.scalar.copy(hT[:, :, :], psB[:, 0:2, :]).then_inc(S("e3_at"), 1)

        def end3_sp(sp):
            sp.sem_inc(S("h3_free"), 1)
            sp.sem_inc(S("y_out"), 16)
            sp.wait_ge(S("j3_out"), 16 * NG)

            def group(g):
                sp.wait_ge(S("h3_free"), g + 1)
                sp.dma_start(hst2[:, :, :], grows(x3_t, g)).then_inc(S("h3_in"), 16)
                sp.wait_ge(S("e3_steps"), (g + 1) * E3)

            with sp.Fori(0, NG - 1) as g:
                group(g)
                sp.dma_start(grows(out, g), hst[:, :, :]).then_inc(S("y_out"), 16)
            group(NG - 1)
            r0 = (NG - 1) * GN
            whole, rest = (N - r0) // P, (N - r0) % P
            if whole:
                sp.dma_start(out[r0:r0 + whole * P, :].rearrange("(j p) w -> p j w", p=P), hst[:, 0:whole, :]).then_inc(S("y_out"), 16)
            sp.dma_start(out[r0 + whole * P:N, :], hst[0:rest, whole, :]).then_inc(S("y_out"), 16)
            sp.wait_ge(S("y_out"), 16 * NG + 16 * (2 if whole else 1))

        block = ctx.enter_context(nc.Block())

        @block.sync
        def _(sp):
            loads_sp(sp)
            keys_sp(sp)
            proj_sp(sp, "j0", [(q0_t, 0, D), (k0_t, D, 2 * D), (m0_t, 2 * D, 3 * D)])
            sort_sp(sp, 0)
            with sp.If(unsorted(sp) > 0):
                sort_sp(sp, 1)
            order_sp(sp, 0)
            spread_sp(sp, 0, q0_t)
            pass_sp(sp, PB)
            stats_sp(sp)
            order_sp(sp, 1)
            sp.wait_ge(S("pay_out"), 32 * NPAY + 32)
            with sp.If(unsorted(sp) > 0):
                paysort_sp(sp)
            spread_sp(sp, 1, k0_t)
            pass_sp(sp, PA)
            proj_sp(sp, "j1", [(q1_t, 0, D), (kv1_t, D, 3 * D)])
            pass_sp(sp, P1)
            proj_sp(sp, "j2", [(h2_t, 0, D + 4), (ed2_t, D + 4, D + 8)])
            pass_sp(sp, P2)
            proj_sp(sp, "j3", [(x3_t, 0, D)])
            pass_sp(sp, P3)
            end3_sp(sp)

        @block.gpsimd
        def _(g_):
            constants_pool(g_)
            nodes_pool(g_, 0)
            spread_pool(g_, 0, qxb_t)
            pass_pool(g_, PB)
            carry_pool(g_, PB)
            ends_pool(g_, PB)
            with g_.If(unsorted(g_) > 0):
                paysort_pool(g_)
            nodes_pool(g_, 1)
            spread_pool(g_, 1, qxa_t)
            pass_pool(g_, PA)
            carry_pool(g_, PA)
            ends_pool(g_, PA)
            scatter_pool(g_, "j1", 0, D, qxa_t)
            pass_pool(g_, P1)
            carry_pool(g_, P1)
            ends_pool(g_, P1)
            scatter_pool(g_, "j2", D + 4, D + 8, edx_t)
            pass_pool(g_, P2)
            carry_pool(g_, P2)
            ends_pool(g_, P2)
            pass_pool(g_, P3)
            carry_pool(g_, P3)
            ends_pool(g_, P3)

        @block.vector
        def _(v):
            padding_dve(v)
            keys_dve(v)
            proj_dve(v, "j0", 3 * D)
            flag_dve(v)
            sort_dve(v, 0)
            with v.If(unsorted(v) > 0):
                sort_dve(v, 1)
            order_dve(v, 0)
            nodes_dve(v, 0)
            pass_dve(v, PB)
            carry_dve(v, PB)
            stats_dve(v)
            order_dve(v, 1)
            with v.If(unsorted(v) > 0):
                paysort_dve(v)
            v.sem_inc(S("edges_ready"), 1)
            nodes_dve(v, 1)
            pass_dve(v, PA)
            carry_dve(v, PA)
            end0_dve(v)
            proj_dve(v, "j1", 3 * D)
            pass_dve(v, P1)
            carry_dve(v, P1)
            end12_dve(v, P1)
            proj_dve(v, "j2", D)
            pass_dve(v, P2)
            carry_dve(v, P2)
            end12_dve(v, P2)
            proj_dve(v, "j3", 0)
            pass_dve(v, P3)
            carry_dve(v, P3)
            end3_dve(v)

        @block.scalar
        def _(act):
            act.sem_inc(S("attr_free"), 1)
            weights3_act(act)
            proj_act(act, "j0", 3 * D)
            sort_act(act, 0)
            with act.If(unsorted(act) > 0):
                sort_act(act, 1)
            nodes_act(act, 0)
            pass_act(act, PB)
            carry_act(act, PB)
            nodes_act(act, 1)
            pass_act(act, PA)
            carry_act(act, PA)
            end0_act(act)
            proj_act(act, "j1", 3 * D)
            pass_act(act, P1)
            carry_act(act, P1)
            end1_act(act)
            proj_act(act, "j2", D)
            pass_act(act, P2)
            carry_act(act, P2)
            proj_act(act, "j3", 0)
            pass_act(act, P3)
            carry_act(act, P3)
            end3_act(act)

        @block.tensor
        def _(pe):
            weights3_pe(pe)
            flag_pe(pe)
            proj_pe(pe, "j0", wcat0[:, :], bcat0[:, :], 3 * D)
            sort_pe(pe, 0)
            with pe.If(unsorted(pe) > 0):
                sort_pe(pe, 1)
            order_pe(pe, 0)
            nodes_pe(pe, 0)
            payload_pe(pe)
            carry_pe(pe, PB)
            order_pe(pe, 1)
            nodes_pe(pe, 1)
            carry_pe(pe, PA)
            end0_pe(pe)
            proj_pe(pe, "j1", wcat1[:, :], bcat1[:, :], 3 * D)
            carry_pe(pe, P1)
            end1_pe(pe)
            proj_pe(pe, "j2", w_2[:, :], None, D)
            carry_pe(pe, P2)
            carry_pe(pe, P3)
            end3_pe(pe)


_INS = ["x", "src", "dst", "edge_attr_64", "edge_weight",
        "L0_gnn_Wk", "L0_gnn_bk", "L0_gnn_Wm", "L0_gnn_bm", "L0_gnn_Wq", "L0_gnn_bq", "L0_gnn_W1", "L0_gnn_b1",
        "L0_gnn_gamma", "L0_gnn_beta", "L0_gnn_W2", "L0_gnn_b2",
        "L1_gnn_Wq", "L1_gnn_bq", "L1_gnn_Wk", "L1_gnn_bk", "L1_gnn_Wv", "L1_gnn_bv", "L1_gnn_We", "L1_gnn_be", "L1_gnn_Wo", "L1_gnn_bo",
        "L2_gnn_W", "L2_gnn_a_src", "L2_gnn_a_dst", "L3_gnn_W1", "L3_gnn_b1", "L3_gnn_W2", "L3_gnn_b2"]


def kernel(**inputs):
    import numpy as _np
    import concourse.bacc as _bacc
    from concourse import mybir as _mybir
    from concourse.bass_utils import run_bass_kernel_spmd as _run

    nc = _bacc.Bacc("TRN2", target_bir_lowering=False, num_devices=1)
    arrays, args = {}, {}
    for name in _INS:
        a = _np.ascontiguousarray(inputs[name])
        arrays[f"in_{name}_dram"] = a
        args[name] = nc.dram_tensor(f"in_{name}_dram", a.shape, _mybir.dt.from_np(a.dtype), kind="ExternalInput").ap()
    out = nc.dram_tensor("out_0_dram", (N, D), F32, kind="ExternalOutput").ap()
    graph_layers_kernel(nc, args, out)
    r = _run(nc, [arrays], core_ids=[0])
    return r.results[0]["out_0_dram"]
```

```python
from contextlib import ExitStack

import concourse.bass as bass
from concourse import mybir

F32 = mybir.dt.float32
I32 = mybir.dt.int32
I16 = mybir.dt.int16
BF16 = mybir.dt.bfloat16
ALU = mybir.AluOpType
ACT = mybir.ActivationFunctionType
AX = mybir.AxisListType

P = 128
N, D, E = 6250, 128, 206250
EF = 64
BPG = 4
NG = -(-N // (P * BPG))
NB = NG * BPG
NPAD = NB * P
GN = BPG * P
T = 1612
EP = P * T
K = 13
IT = T // K
assert EP >= E and T % (2 * K) == 0
PADN = 6271
assert N <= PADN < NPAD
C = 2048
LOGC, LOGP = 11, 7
KE = 2 * K
NPAY = EP // (P * KE)
PW = 16
BIG = 1.0e30
H0, H1, H2 = 4, 8, 4
EPS = 1e-5


class Seq:

    def __init__(self, eng, sem, base=0, i=None, per=0):
        self.eng, self.sem, self.base, self.i, self.per, self.k = eng, sem, base, i, per, 0

    def did(self, ins):
        self.k += 1
        ins.then_inc(self.sem, 1)

    def value(self, k):
        return self.base + k if self.i is None else self.i * self.per + (self.base + k)

    def wait(self):
        self.eng.wait_ge(self.sem, self.value(self.k))

    def do(self, ins):
        self.did(ins)
        self.wait()


def group_seq(eng, sem, g, per):
    return Seq(eng, sem, g * per) if isinstance(g, int) else Seq(eng, sem, 0, g, per)


class Line(Seq):

    def __init__(self, eng, sem, total):
        super().__init__(eng, sem, total[0])
        self.total = total

    def did(self, ins):
        super().did(ins)
        self.total[0] += 1


def graph_layers_kernel(nc, A, out):
    with ExitStack() as ctx:
        def sb(name, shape, dt=F32):
            return ctx.enter_context(nc.sbuf_tensor(name, shape, dt))

        sems = {}

        def S(name):
            if name not in sems:
                sems[name] = ctx.enter_context(nc.semaphore(name))
            return sems[name]

        line_total, staged_total = [0], [0]

        def staged(n):
            staged_total[0] += n
            return staged_total[0] - n

        def line(v):
            return Line(v, S("line_steps"), line_total)

        def dram(name, shape, dt=F32):
            return nc.dram_tensor(name, shape, dt).ap()

        psA = ctx.enter_context(nc.psum_tensor("psA", [P, 512], F32))
        psB = ctx.enter_context(nc.psum_tensor("psB", [P, 4, 512], F32))
        psC = ctx.enter_context(nc.psum_tensor("psC", [P, 1024], F32))
        psD = ctx.enter_context(nc.psum_tensor("psD", [P, 512], F32))

        xsb = sb("xsb", [P, NB, D])
        ident = sb("ident", [P, P])
        ones = sb("ones", [P, P])
        before = sb("before", [P, P])
        after = sb("after", [P, P])
        nid = sb("nid", [P, NB])
        sgn = sb("sgn", [P, 8])
        wcat0 = sb("wcat0", [P, 3 * D])
        bcat0 = sb("bcat0", [P, 3 * D])
        wcat1 = sb("wcat1", [P, 3 * D])
        bcat1 = sb("bcat1", [P, 3 * D])
        w1_0 = sb("w1_0", [P, D])
        w2_0 = sb("w2_0", [P, D])
        b2_0 = sb("b2_0", [P, D])
        bncol = sb("bncol", [P, 8])
        we2 = sb("we2", [P, 16])
        be2 = sb("be2", [1, 16])
        wo_1 = sb("wo_1", [P, D])
        bo_1 = sb("bo_1", [P, D])
        w_2 = sb("w_2", [P, D + 8])
        avec = sb("avec", [P, 2, D])
        w3raw = sb("w3raw", [P, 2, D])
        w3t = sb("w3t", [P, 2, D])
        b3 = sb("b3", [P, 2, D])

        oth_i = [sb(f"oth_i{o}", [P, T + 2 * K], I32) for o in range(2)]
        restart = [sb(f"restart{o}", [P, T], BF16) for o in range(2)]
        ew = sb("ew", [P, T])
        endix = [sb(f"endix{o}", [P, NB], I32) for o in range(2)]
        spos = sb("spos", [P, NB], I32)
        head_i = [sb(f"head_i{o}", [P, 1], I32) for o in range(2)]
        patch_i = [sb(f"patch_i{o}", [P, 1], I32) for o in range(2)]
        head = sb("head", [P, D])
        bias2 = [sb(f"bias2_{o}", [P, P]) for o in range(2)]
        contT = [sb(f"contT{o}", [P, P]) for o in range(2)]

        WS = 264
        region = sb("region", [P, 2 * K * (WS + D)])
        rows_s = [region[:, b * K * WS:(b + 1) * K * WS].rearrange("p (t w) -> p t w", w=WS) for b in range(2)]
        rows_d = [region[:, 2 * K * WS + b * K * D:2 * K * WS + (b + 1) * K * D].rearrange("p (t w) -> p t w", w=D) for b in range(2)]
        ix_s = [sb(f"ix_s{b}", [P, K], I32) for b in range(2)]
        pay = [sb(f"pay{b}", [P, K, PW]) for b in range(2)]
        s_ext = sb("s_ext", [P, 8, K + 1])
        s_max = sb("s_max", [P, 8, K + 1])
        m_ext = sb("m_ext", [P, 8, K + 1])
        rst = sb("rst", [P, 8, K + 1])
        dd = sb("dd", [P, 8, K + 1])
        ww = sb("ww", [P, 8, K])
        dtmp = sb("dtmp", [P, 8, K])

        WORK = 14900
        work = sb("work", [P, WORK])
        at = [0]

        def w_view(n):
            a = work[:, at[0]:at[0] + n]
            at[0] += n
            assert at[0] <= WORK
            return a

        FM = 136
        bv = w_view(FM * (K + 1))
        abig = w_view(FM * (K + 1))
        st = w_view(FM * (K + 1))
        psrow = [w_view(K * 144) for _ in range(2)]
        zt = w_view(D * (K + 1))
        nsb = w_view(D * (K + 1))
        hold = w_view(D * (K + 1))
        falls = work[:, 2 * C:3 * C]
        keyin = [work[:, i * C:(i + 1) * C] for i in range(2)]
        rows4 = [work[:, b * T:(b + 1) * T].bitcast(I16).rearrange("p (j w) -> p j w", w=T) for b in range(2)]
        rsign = work[:, 3900:3900 + T]
        row1 = work[:, 5900:5900 + T // 2].bitcast(I16)
        cmp_n = work[:, 8000:8000 + NB * P].rearrange("p (j r) -> p j r", r=P)

        attr = work[:, 100:100 + KE * EF].rearrange("p (t w) -> p t w", w=EF)
        attrT = work[:, 2000:2000 + KE // 2 * P].rearrange("p (u r) -> p u r", r=P)
        pay0 = sb("payrow", [P, KE, PW])
        pcol_i = sb("pcol_i", [P, KE], I32)
        pcol_f = sb("pcol_f", [P, KE])

        X = region[:, 0:C]
        Y = region[:, C:2 * C]
        eid_i = region[:, 2 * C:3 * C].bitcast(I32)
        raw = region[:, 2 * C:2 * C + T].bitcast(I32)
        seg_i = region[:, 3 * C:3 * C + T].bitcast(I32)
        same = region[:, 4 * C:4 * C + T]
        seg16 = region[:, 2 * C:2 * C + T // 2].bitcast(I16)
        near_all = region[:, 0:NPAD].rearrange("p (j d) -> p j d", d=D)
        h3_all = near_all
        nid_i = sb("nid_i", [P, NB], I32)
        part_i = sb("part_i", [P, 8], I32)
        diag2 = sb("diag2", [P, 2, P])
        firstrow = sb("firstrow", [P, P])
        down1 = sb("down1", [P, P])
        wrap1 = sb("wrap1", [P, P])
        NB2 = IT // 2
        assert NB2 >= NB
        nt_c = [sb(f"nt_c{o}", [P, NB2 + 1]) for o in range(2)]
        nt_q = [sb(f"nt_q{o}", [P, NB]) for o in range(2)]
        nt_i = [sb(f"nt_i{o}", [P, NB2 + 1], I32) for o in range(2)]
        nt_b = sb("nt_b", [P, NB2])
        row_i = sb("row_i", [P, 1], I32)
        zero_t = sb("zero_t", [P, 4 * D])
        segf = X[:, 0:T]
        hT_all = region[:, 0:NPAD]

        hst = sb("hst", [P, BPG, D])
        hst2 = sb("hst2", [P, BPG, D])
        hT = sb("hT", [P, 2, GN])
        tab = sb("tab", [P, BPG, 3 * D])
        ln_s = sb("ln_s", [P, 4, BPG])
        ln_a = sb("ln_a", [P, 4, NB])
        nt_f = sb("nt_f", [P, 3, NB])
        fe_i = sb("fe_i", [P, BPG], I32)
        half_i = [sb(f"half_i{b}", [P, 2], I32) for b in range(2)]
        stat = sb("stat", [P, NB, 2, H0])
        prow = sb("prow", [P, 144])
        pmx = sb("pmx", [P, 3, 8])
        mx4 = sb("mx4", [P, 3, BPG, 8])
        cst = sb("cst", [P, 144])
        ctz = sb("ctz", [1, 144])
        next_i = sb("next_i", [P, 1], I32)
        flag_f = sb("flag_f", [P, 2])
        flag_i = sb("flag_i", [P, 1], I32)
        mcar = sb("mcar", [P, 8])
        dwide = work[:, 0:1024]
        wwide = work[:, 1024:2048]

        def ends(q):
            return work[:, 2048:2048 + NB * q.W].rearrange("p (j w) -> p j w", w=q.W)

        h_all = work[:, 0:NPAD].rearrange("p (j d) -> p j d", d=D)
        sq_all = work[:, NPAD:2 * NPAD].rearrange("p (j d) -> p j d", d=D)

        keys_dram = dram("keys_in", [2, P, C])
        sorted_dram = dram("keys_sorted", [2, P * C])
        pay_dram = dram("payload", [EP, PW])
        paya_dram = dram("payload_by_dst", [EP, PW])
        q0_t = dram("q0", [NPAD, D])
        k0_t = dram("k0", [NPAD, D])
        qm0_t = dram("qm0", [NPAD, 264])
        q1_t = dram("q1", [NPAD, D])
        kv1_t = dram("kv1", [NPAD, 2 * D])
        h2_t = dram("h2", [NPAD, D + 4])
        ed2_t = dram("ed2", [NPAD, 4])
        x3_t = dram("x3", [NPAD, D])
        keyrow_t = [dram(f"keyrow{o}", [P, T], I16) for o in range(2)]
        qxb_t = dram("start_rows_by_src", [EP + NPAD, D])
        qxa_t = dram("start_rows_by_dst", [EP + NPAD, D])
        edx_t = dram("start_ed2", [EP + NPAD, 4])

        class Pass:
            def __init__(self, name, H, dh, soft, tabs, tabd, near, W):
                self.name, self.H, self.dh, self.soft = name, H, dh, soft
                self.tabs, self.tabd, self.near, self.W = tabs, tabd, near, W
                self.o = 0 if name == "pB" else 1
                self.HF = near.shape[1] if near is not None else D
                self.made = 3 if near is not None else 1
                self.F = H * (dh + 1) if soft else D
                self.ps = dram(f"state_{name}", [EP + 1, W])

            def s(self, what):
                return S(f"pass_{what}")

            def own(self, what):
                return S(f"{self.name}_{what}")

            def total(self, what):
                half = IT // 2
                exps = IT if self.soft or self is PA else 0
                hold = self.near is not None
                return {"free0": 1 + half, "free1": 1 + half, "prep": 5, "steps": self.steps * IT,
                        "near_in0": 16 * half * hold, "near_in1": 16 * half * hold, "made": self.made * IT, "held": IT * hold,
                        "laid": 1 + IT, "laid0": half, "laid1": half, "arg": exps, "expw": exps, "decay": IT * self.soft, "scanned": IT,
                        "sent0": 16 + 16 * half, "sent1": 16 + 16 * half, "ends_in0": 16 * BPG * (NG + 1 >> 1), "ends_in1": 16 * BPG * (NG >> 1), "ends_ready": NG,
                        "carry_dve": 3 if self.soft else 1, "carry_pe": 3 if self.soft else 1, "carry_act": 4 * self.soft,
                        "head_in": 16 * hold, "prow_in": 16, "patched": 1,
                        "prow_out": 16}[what]

            def base(self, what):
                return sum(q.total(what) for q in passes[:passes.index(self)])

            def on(self, what, value):
                return self.s(what), value + self.base(what)

        PB = Pass("pB", H0, 0, True, k0_t, q0_t, qxb_t, 12)
        PA = Pass("pA", H0, 32, False, qm0_t, k0_t, qxa_t, D)
        P1 = Pass("p1", H1, 16, True, kv1_t, q1_t, qxa_t, 144)
        P2 = Pass("p2", H2, 32, True, h2_t, ed2_t, edx_t, 136)
        P3 = Pass("p3", 1, D, False, x3_t, None, None, D)
        passes = [PB, PA, P1, P2, P3]
        NN = PADN // P + 1
        SCATTER = 16 * BPG * NG
        PB.steps, PB.needs = 11, [("tables_made", 8), ("j0_out", 16 * 3 * NG), ("spread_out", 16 * NN)]
        PA.steps, PA.needs = 8, [("edges_ready", 1), ("qm_out", 16 * NG), ("spread_out", 32 * NN)]
        P1.steps, P1.needs = 13, [("j1_out", 32 * NG)]
        P2.steps, P2.needs = 13, [("j2_out", 32 * NG)]
        P3.steps, P3.needs = 3, [("j3_out", 16 * NG)]
        PB.started = [("spread_out", 16 * NN)]
        PA.started = [("spread_out", 32 * NN)]
        P1.started = [("scat_out", SCATTER)]
        P2.started = [("scat_out", 2 * SCATTER)]

        cnt = ew

        def grows(t, g):
            return t[bass.ds(g * GN, GN), :].rearrange("(j p) w -> p j w", p=P)

        def constants_pool(g):
            g.memset(ident[:, :], 0.0).then_inc(S("c_fill"), 1)
            g.memset(before[:, :], 1.0).then_inc(S("c_fill"), 1)
            g.memset(after[:, :], 1.0).then_inc(S("c_fill"), 1)
            g.memset(ones[:, :], 1.0).then_inc(S("consts"), 1)
            g.memset(down1[:, :], 0.0).then_inc(S("c_fill"), 1)
            g.memset(wrap1[:, :], 0.0).then_inc(S("c_fill"), 1)
            g.memset(zero_t[:, :], 0.0).then_inc(S("consts"), 1)
            g.iota(nid_i[:, :], [[P, NB]], base=0, channel_multiplier=1).then_inc(S("consts"), 1)
            g.iota(eid_i, [[1, C]], base=0, channel_multiplier=C).then_inc(S("consts"), 1)
            g.iota(part_i[:, :], [[0, 8]], base=0, channel_multiplier=1).then_inc(S("consts"), 1)
            g.wait_ge(S("c_fill"), 5)
            g.affine_select(out=ident[:, :], in_=ident[:, :], compare_op=ALU.not_equal, fill=1.0, base=0,
                            pattern=[[-1, P]], channel_multiplier=1).then_inc(S("consts"), 1)
            g.affine_select(out=before[:, :], in_=before[:, :], compare_op=ALU.is_gt, fill=0.0, base=0,
                            pattern=[[-1, P]], channel_multiplier=1).then_inc(S("consts"), 1)
            g.affine_select(out=after[:, :], in_=after[:, :], compare_op=ALU.is_gt, fill=0.0, base=0,
                            pattern=[[1, P]], channel_multiplier=-1).then_inc(S("consts"), 1)
            g.affine_select(out=down1[:, :], in_=down1[:, :], compare_op=ALU.not_equal, fill=1.0, base=1,
                            pattern=[[-1, P]], channel_multiplier=1).then_inc(S("consts"), 1)
            g.affine_select(out=wrap1[:, :], in_=wrap1[:, :], compare_op=ALU.not_equal, fill=1.0, base=1 - P,
                            pattern=[[-1, P]], channel_multiplier=1).then_inc(S("consts"), 1)

        CONSTS = 10

        def zeros_sp(sp):
            n = EP // (4 * P)
            sp.dma_start(qxb_t[0:EP, :].rearrange("(p r c) w -> p r (c w)", p=P, c=4),
                         zero_t[:, :].unsqueeze(1).to_broadcast([P, n, 4 * D])).then_inc(S("zeroed"), 16)
            c = T // 13
            sp.dma_start(edx_t[0:EP, :].rearrange("(p r c) w -> p r (c w)", p=P, c=c),
                         zero_t[:, 0:4 * c].unsqueeze(1).to_broadcast([P, 13, 4 * c])).then_inc(S("zeroed"), 16)

        def zeros_chunk_sp(sp, i):
            c = 2 * K // 2
            sp.dma_start(qxa_t[0:EP, :].rearrange("(p r) w -> p (r w)", p=P)[:, bass.ds(i * (2 * K * D), 2 * K * D)].rearrange("p (r w) -> p r w", w=2 * D),
                         zero_t[:, 0:2 * D].unsqueeze(1).to_broadcast([P, c, 2 * D])).then_inc(S("zeroed_a"), 16)

        def padding_dve(v):
            nc.vector.memset(X.bitcast(I32), PADN).then_inc(S("padded"), 1)
            nc.vector.memset(Y.bitcast(I32), PADN).then_inc(S("padded"), 1)
            nc.vector.memset(xsb[:, N // P:NB, :], 0.0).then_inc(S("padded"), 1)
            nc.vector.memset(next_i[:, :], PADN).then_inc(S("padded"), 1)
            nc.vector.memset(ctz[:, :], 0.0).then_inc(S("dummies"), 1)
            for o in range(2):
                nc.vector.memset(oth_i[o][:, T:T + 2 * K], 0).then_inc(S("dummies"), 1)
                nc.vector.memset(nt_c[o][:, 0:1], 0.0).then_inc(S("dummies"), 1)
                nc.vector.memset(nt_i[o][:, :], 0).then_inc(S("dummies"), 1)
            nc.vector.memset(nt_b[:, :], 0.0).then_inc(S("dummies"), 1)
            nc.vector.memset(we2[:, :], 0.0).then_inc(S("dummies"), 1)
            nc.vector.memset(pay0[:, :, :], 0.0).then_inc(S("dummies"), 1)
            nc.vector.memset(attr[:, :, :], 0.0).then_inc(S("dummies"), 1)
            nc.vector.memset(pcol_i[:, :], 0).then_inc(S("dummies"), 1)
            nc.vector.memset(pcol_f[:, :], 0.0).then_inc(S("dummies"), 1)
            nc.vector.memset(rst[:, :, :], -BIG).then_inc(S("dummies"), 1)
            nc.vector.memset(dd[:, :, :], -BIG).then_inc(S("dummies"), 1)
            for b in range(2):
                nc.vector.memset(psrow[b], 0.0).then_inc(S("dummies"), 1)
            v.wait_ge(S("consts"), CONSTS)
            q = line(v)
            for k in range(8):
                q.did(nc.vector.tensor_scalar(part_i[:, k:k + 1], part_i[:, k:k + 1], k, 1, ALU.logical_shift_right, ALU.bitwise_and))
            q.did(nc.vector.tensor_copy(nid[:, :], nid_i[:, :]))
            q.wait()
            q.do(nc.vector.tensor_scalar(sgn[:, :], part_i[:, :], -2.0, 1.0, ALU.mult, ALU.add))

        DUMMIES = 17

        def loads_sp(sp):
            n = [0]

            def load(dst, src):
                n[0] += 1
                sp.dma_start(dst, src).then_inc(S("loaded"), 16)

            def row(name):
                return A[name].rearrange("(a d) -> a d", a=1)

            sp.wait_ge(S("padded"), 4)
            full, rest = E // C, E % C
            with nc.allow_non_contiguous_dma(reason="the edge after each partition's run"):
                sp.dma_start(next_i[0:full - 1, :], A["dst"][0:full * C].rearrange("(p c) -> p c", c=C)[1:full, 0:1]).then_inc(S("ends_in"), 16)
                sp.dma_start(next_i[full - 1:full, :], A["dst"][full * C:full * C + 1].rearrange("(p c) -> p c", p=1)).then_inc(S("ends_in"), 16)
            for name, dst in (("src", X), ("dst", Y)):
                d = dst.bitcast(I32)
                sp.dma_start(d[0:full, :], A[name][0:full * C].rearrange("(p c) -> p c", c=C)).then_inc(S("ends_in"), 16)
                sp.dma_start(d[full:full + 1, 0:rest], A[name][full * C:E].rearrange("(p c) -> p c", p=1)).then_inc(S("ends_in"), 16)
            whole = N // P
            load(xsb[:, 0:whole, :], A["x"][0:whole * P, :].rearrange("(j p) w -> p j w", p=P))
            load(xsb[0:N - whole * P, whole, :], A["x"][whole * P:N, :])
            for j, nm in enumerate("kqm"):
                load(wcat0[:, j * D:(j + 1) * D], A["L0_gnn_W" + nm])
                load(bcat0[:, j * D:(j + 1) * D], row("L0_gnn_b" + nm).to_broadcast([P, D]))
            for j, nm in enumerate("qkv"):
                load(wcat1[:, j * D:(j + 1) * D], A["L1_gnn_W" + nm])
                load(bcat1[:, j * D:(j + 1) * D], row("L1_gnn_b" + nm).to_broadcast([P, D]))
            load(w1_0[:, :], A["L0_gnn_W1"])
            load(w2_0[:, :], A["L0_gnn_W2"])
            load(b2_0[:, :], row("L0_gnn_b2").to_broadcast([P, D]))
            with nc.allow_non_contiguous_dma(reason="a column of 128 values"):
                for j, nm in enumerate(("b1", "gamma", "beta")):
                    load(bncol[:, j:j + 1], A["L0_gnn_" + nm].rearrange("(p a) -> p a", a=1))
            sp.wait_ge(S("dummies"), DUMMIES)
            for j in range(2):
                load(we2[j * EF:(j + 1) * EF, j * 8:(j + 1) * 8], A["L1_gnn_We"])
                load(be2[:, j * 8:(j + 1) * 8], row("L1_gnn_be"))
            load(wo_1[:, :], A["L1_gnn_Wo"])
            load(bo_1[:, :], row("L1_gnn_bo").to_broadcast([P, D]))
            load(w_2[:, 0:D].rearrange("i (h o) -> i h o", h=H2), A["L2_gnn_W"].rearrange("h i o -> i h o"))
            for j, nm in enumerate(("src", "dst")):
                load(avec[:, j, :], A["L2_gnn_a_" + nm].rearrange("(a h) o b -> a (h o b)", a=1).to_broadcast([P, D]))
                load(w3raw[:, j, :], A[f"L3_gnn_W{j + 1}"])
                load(b3[:, j, :], row(f"L3_gnn_b{j + 1}").to_broadcast([P, D]))
            assert n[0] == NLOADS, n[0]
            for q in passes:
                sp.dma_start(q.ps[EP:EP + 1, :], ctz[:, 0:q.W]).then_inc(S("dummy_rows"), 16)

        NLOADS = 2 + 6 + 6 + 3 + 3 + 4 + 2 + 1 + 6
        NDUMMY = 5

        def keys_dve(v):
            v.wait_ge(S("ends_in"), 96)
            v.wait_ge(S("consts"), CONSTS)
            q = line(v)
            srcs, dsts = X.bitcast(I32), Y.bitcast(I32)
            kb, ka = keyin[0].bitcast(I32), keyin[1].bitcast(I32)
            q.did(nc.vector.tensor_scalar(kb, srcs, 13, 1 << 30, ALU.logical_shift_left, ALU.bitwise_or))
            q.do(nc.vector.tensor_scalar(ka, dsts, 32.0, None, ALU.add))
            q.did(nc.vector.tensor_tensor(kb, kb, dsts, ALU.bitwise_or))
            q.do(nc.vector.tensor_scalar(ka, ka, 18, 0, ALU.logical_shift_left, ALU.bitwise_or))
            q.did(nc.vector.tensor_tensor(ka, ka, eid_i, ALU.bitwise_or))
            q.wait()
            v.sem_inc(S("keys_made"), 1)
            q.did(nc.vector.tensor_tensor(falls[:, 0:C - 1], dsts[:, 1:C], dsts[:, 0:C - 1], ALU.is_lt))
            q.did(nc.vector.tensor_tensor(falls[:, C - 1:C], next_i[:, :], dsts[:, C - 1:C], ALU.is_lt))
            q.wait()
            q.do(nc.vector.tensor_reduce(flag_f[:, 0:1], falls, AX.X, ALU.add))
            v.sem_inc(S("keys_made"), 1)

        def flag_pe(pe):
            pe.wait_ge(S("keys_made"), 2)
            nc.tensor.matmul(psC[:, 0:1], ones[:, :], flag_f[:, 0:1], start=True, stop=True).then_inc(S("falls_sum"), 1)

        def flag_dve(v):
            q = line(v)
            v.wait_ge(S("falls_sum"), 1)
            q.do(nc.vector.tensor_scalar(flag_f[:, 1:2], psC[:, 0:1], 1.0, None, ALU.min))
            q.do(nc.vector.tensor_copy(flag_i[:, :], flag_f[:, 1:2]))
            v.sem_inc(S("flag_made"), 1)

        def unsorted(eng):
            eng.wait_ge(S("flag_made"), 1)
            return eng.value_load(flag_i[0:1, 0:1], min_val=0, max_val=1)

        def keys_sp(sp):
            sp.wait_ge(S("keys_made"), 1)
            for o in range(2):
                sp.dma_start(keys_dram[o], keyin[o]).then_inc(S("keys_out"), 16)
            sp.wait_ge(S("keys_out"), 32)

        SORT_STEPS = sum(4 * k for k in range(1, LOGC)) + 2 * LOGC * (LOGP + 1) + sum(4 * q for q in range(1, LOGP)) + 2 * LOGP
        SORT_TURNS = 2 * LOGP
        SORT_SIGNS = 2 * LOGP + 1

        class Sort:

            def __init__(self):
                self.cur, self.oth = X, Y

            def swap(self):
                self.cur, self.oth = self.oth, self.cur

        def stage_views(a, j, k, directed):
            s = 1 << j
            if directed:
                w = a.rearrange("p (g d n h s) -> p d h g n s", d=2, n=1 << (k - 1 - j), h=2, s=s)
                return [(w[:, d, 0], w[:, d, 1]) for d in range(2)]
            w = a.rearrange("p (n h s) -> p h n s", h=2, s=s)
            return [(w[:, 0], w[:, 1])]

        def sort_dve(v, o):
            q = Seq(v, S("sort_steps"), o * SORT_STEPS)
            b = Sort()
            turn, sign = [0], [0]

            def stage(j, k, directed):
                for d, ((lo, hi), (lo2, hi2)) in enumerate(zip(stage_views(b.cur, j, k, directed), stage_views(b.oth, j, k, directed))):
                    q.did(nc.vector.tensor_tensor(lo2, lo, hi, ALU.max if d else ALU.min))
                    q.did(nc.vector.tensor_tensor(hi2, lo, hi, ALU.min if d else ALU.max))
                b.swap()
                q.wait()

            def signed():
                sign[0] += 1
                v.wait_ge(S("sort_signs"), o * SORT_SIGNS + sign[0])
                b.swap()

            v.wait_ge(S("sort_in"), o * 16 + 16)
            for k in range(1, LOGC):
                for j in reversed(range(k)):
                    stage(j, k, True)
            for k in range(LOGC, LOGC + LOGP + 1):
                if k > LOGC:
                    signed()
                    turn[0] += 1
                    v.wait_ge(S("sort_turns"), o * SORT_TURNS + turn[0])
                    nc.vector.tensor_copy(b.oth, psB[:, :, :].rearrange("p a b -> p (a b)")).then_inc(S("sort_evacs"), 1)
                    b.swap()
                    v.wait_ge(S("sort_evacs"), o * LOGP + turn[0] // 2 + 1)
                    lp = k - LOGC
                    for j in reversed(range(lp)):
                        stage(j, lp, k < LOGC + LOGP)
                    turn[0] += 1
                signed()
                for j in reversed(range(LOGC)):
                    stage(j, LOGC, False)
            assert q.k == SORT_STEPS, (q.k, SORT_STEPS)
            assert b.cur is sorted_at(), "the sorted keys' buffer"

        def sorted_at():
            n = sum(range(1, LOGC)) + LOGC * (LOGP + 1) + sum(range(1, LOGP + 1)) + SORT_SIGNS + LOGP
            return Y if n % 2 else X

        def sort_act(act, o):
            b = Sort()
            steps = sum(4 * k for k in range(1, LOGC))
            for _ in range(sum(range(1, LOGC))):
                b.swap()
            turn = 0
            for k in range(LOGC, LOGC + LOGP + 1):
                lp = k - LOGC
                if lp:
                    act.wait_ge(S("sort_steps"), o * SORT_STEPS + steps)
                    nc.scalar.mul(b.oth, b.cur, sgn[:, lp - 1:lp]).then_inc(S("sort_signs"), 1)
                    b.swap()
                    b.swap()
                    steps += (4 if lp < LOGP else 2) * lp
                    for _ in range(lp):
                        b.swap()
                    turn += 2
                    act.wait_ge(S("sort_turns"), o * SORT_TURNS + turn)
                    nc.scalar.mul(b.oth, psB[:, :, :].rearrange("p a b -> p (a b)"),
                                  sgn[:, lp:lp + 1]).then_inc(S("sort_signs"), 1)
                else:
                    act.wait_ge(S("sort_steps"), o * SORT_STEPS + steps)
                    nc.scalar.mul(b.oth, b.cur, sgn[:, 0:1]).then_inc(S("sort_signs"), 1)
                b.swap()
                steps += 2 * LOGC
                for _ in range(LOGC):
                    b.swap()

        def sort_pe(pe, o):
            b = Sort()
            steps = sum(4 * k for k in range(1, LOGC)) + 2 * LOGC
            for _ in range(sum(range(1, LOGC)) + 1 + LOGC):
                b.swap()

            def turn_all():
                for c in range(C // P):
                    ins = nc.tensor.transpose(psB[:, c // 4, (c % 4) * P:(c % 4 + 1) * P], b.cur[:, c * P:(c + 1) * P], ident[:, :])
                ins.then_inc(S("sort_turns"), 1)

            sign = 1
            for lp in range(1, LOGP + 1):
                b.swap()
                sign += 1
                pe.wait_ge(S("sort_signs"), o * SORT_SIGNS + sign)
                turn_all()
                b.swap()
                for _ in range(lp):
                    b.swap()
                steps += (4 if lp < LOGP else 2) * lp
                pe.wait_ge(S("sort_evacs"), o * LOGP + lp)
                pe.wait_ge(S("sort_steps"), o * SORT_STEPS + steps)
                turn_all()
                b.swap()
                sign += 1
                steps += 2 * LOGC
                for _ in range(LOGC):
                    b.swap()

        def sort_sp(sp, o):
            sp.dma_start(X, keys_dram[o]).then_inc(S("sort_in"), 16)
            if o == 0:
                proj0_sp(sp)
                zeros_sp(sp)
            sp.wait_ge(S("sort_steps"), (o + 1) * SORT_STEPS)
            sp.dma_start(sorted_dram[o, :].rearrange("(p c) -> p c", c=C), sorted_at()).then_inc(S("sort_out"), 16)
            sp.wait_ge(S("sort_out"), o * 16 + 16)

        LN_STEPS = 9

        def proj_on(nm, what, value):
            before = "j1 j2 j3".split().index(nm)
            return S("proj_" + what), value + before * (NG + (what in ("tr", "ht", "psfree", "tabfree")))

        def norm_group(v, nm, g, q, first_write):
            xg = xsb[:, bass.ds(g * BPG, BPG), :]
            bc = lambda k: ln_s[:, k, :].unsqueeze(2).to_broadcast([P, BPG, D])
            k0 = q.k
            q.do(nc.vector.tensor_reduce(ln_s[:, 0, :], xg, AX.X, ALU.add))
            q.do(nc.vector.tensor_scalar(ln_s[:, 1, :], ln_s[:, 0, :], -1.0 / D, None, ALU.mult))
            first_write()
            q.do(nc.vector.tensor_tensor(hst[:, :, :], xg, bc(1), ALU.add))
            q.do(nc.vector.tensor_tensor(hst2[:, :, :], hst[:, :, :], hst[:, :, :], ALU.mult))
            q.do(nc.vector.tensor_reduce(ln_s[:, 0, :], hst2[:, :, :], AX.X, ALU.add))
            nc.vector.tensor_scalar(ln_s[:, 2, :], ln_s[:, 0, :], 1.0 / D, EPS, ALU.mult, ALU.add).then_inc(S("proj_var"), 1)
            v.wait_ge(*proj_on(nm, "sqrt", g + 1))
            q.do(nc.vector.reciprocal(ln_s[:, 1, :], ln_s[:, 3, :]))
            q.do(nc.vector.tensor_tensor(hst[:, :, :], hst[:, :, :], bc(1), ALU.mult))
            q.did(nc.vector.tensor_scalar(hst[:, :, :], hst[:, :, :], 0.0, None, ALU.max))
            assert q.k == k0 + LN_STEPS - 1, q.k

        def sqrt_act(act, nm, g):
            act.wait_ge(*proj_on(nm, "var", g + 1))
            nc.scalar.activation(ln_s[:, 3, :], ln_s[:, 2, :], ACT.Sqrt).then_inc(S("proj_sqrt"), 1)

        PER = LN_STEPS - 1

        def norm_dve(v, nm, g):
            q = group_seq(v, S(nm + "_steps"), g, PER)
            norm_group(v, nm, g, q, lambda: v.wait_ge(*proj_on(nm, "tr", g + 1)))

        def take_dve(v, nm, ncol, g):
            v.wait_ge(*proj_on(nm, "mm", g + 1))
            v.wait_ge(*proj_on(nm, "tabfree", g + 1))
            if nm == "j1":
                ins = nc.vector.tensor_tensor(tab[:, :, 0:ncol], psB[:, :, 0:ncol], bcat1[:, :].unsqueeze(1).to_broadcast([P, BPG, ncol]), ALU.add)
            else:
                ins = nc.vector.tensor_copy(tab[:, :, 0:ncol], psB[:, :, 0:ncol])
            ins.then_inc(S("proj_tab"), 1)
            v.wait_ge(*proj_on(nm, "tab", g + 1))
            v.sem_inc(S("proj_psfree"), 1)

        def proj_pe(pe, nm, w, ncol, g):
            pe.wait_ge(S(nm + "_steps"), g * PER + PER)
            pe.wait_ge(*proj_on(nm, "ht", g + 1))
            for j in range(BPG):
                ins = nc.tensor.transpose(psA[:, j * P:(j + 1) * P], hst[:, j, :], ident[:, :])
            ins.then_inc(S("proj_tr"), 1)
            pe.wait_ge(*proj_on(nm, "ht", g + 2))
            pe.wait_ge(*proj_on(nm, "psfree", g + 1))
            for j in range(BPG):
                ins = nc.tensor.matmul(psB[:, j, 0:ncol], hT[:, 1, j * P:(j + 1) * P], w, start=True, stop=True)
            ins.then_inc(S("proj_mm"), 1)

        def proj_act(act, nm, g):
            sqrt_act(act, nm, g)
            act.wait_ge(*proj_on(nm, "tr", g + 2))
            nc.scalar.copy(hT[:, 1, :], psA[:, :]).then_inc(S("proj_ht"), 1)

        def proj_sp(sp, nm, tabs):
            sp.sem_inc(S("proj_tabfree"), 1)
            with sp.Fori(0, NG) as g:
                if nm == "j3":
                    sp.wait_ge(S(nm + "_steps"), (g + 1) * E2)
                else:
                    sp.wait_ge(*proj_on(nm, "tab", g + 1))
                for t, a, z in tabs:
                    src = hst if nm == "j3" else tab
                    sp.dma_start(grows(t, g), src[:, :, a:z]).then_inc(S(nm + "_out"), 16)
                sp.wait_ge(S(nm + "_out"), g * (16 * len(tabs)) + 16 * len(tabs))
                if nm in SCATTERED:
                    sp.wait_ge(S("scat_out"), g * (16 * BPG) + (SCATTERED.index(nm) * SCATTER + 16 * BPG))
                sp.sem_inc(S("proj_tabfree"), 1)

        def proj0_dve(v):
            v.wait_ge(S("loaded"), 16 * NLOADS)
            v.wait_ge(S("keys_out"), 32)
            q = line(v)
            bc = lambda k: ln_a[:, k, :].unsqueeze(2).to_broadcast([P, NB, D])
            q.do(nc.vector.tensor_reduce(ln_a[:, 0, :], xsb[:, :, :], AX.X, ALU.add))
            q.do(nc.vector.tensor_scalar(ln_a[:, 1, :], ln_a[:, 0, :], -1.0 / D, None, ALU.mult))
            q.do(nc.vector.tensor_tensor(h_all, xsb[:, :, :], bc(1), ALU.add))
            q.do(nc.vector.tensor_tensor(sq_all, h_all, h_all, ALU.mult))
            q.do(nc.vector.tensor_reduce(ln_a[:, 0, :], sq_all, AX.X, ALU.add))
            q.do(nc.vector.tensor_scalar(ln_a[:, 2, :], ln_a[:, 0, :], 1.0 / D, EPS, ALU.mult, ALU.add))
            v.sem_inc(S("ln0_by_dve"), 1)
            for j in range(2):
                q.do(nc.vector.tensor_tensor(hst2[:, 0, :], w_2[:, 0:D], avec[:, j, :], ALU.mult))
                q.do(nc.vector.tensor_reduce(w_2[:, D + 4 * j:D + 4 * j + 4], hst2[:, 0, :].rearrange("p (h o) -> p h o", h=H2), AX.X, ALU.add))
            v.wait_ge(S("sqrt0"), 1)
            q.do(nc.vector.reciprocal(ln_a[:, 1, :], ln_a[:, 3, :]))
            q.do(nc.vector.tensor_tensor(h_all, h_all, bc(1), ALU.mult))
            q.do(nc.vector.tensor_scalar(h_all, h_all, 0.0, None, ALU.max))
            v.sem_inc(S("ln0_by_dve"), 1)

        def proj0_act(act):
            act.wait_ge(S("loaded"), 16 * NLOADS)
            nc.scalar.mul(wcat0[:, D:2 * D], wcat0[:, D:2 * D], 1.0 / (32 ** 0.5)).then_inc(S("w0_scaled"), 1)
            nc.scalar.mul(bcat0[:, D:2 * D], bcat0[:, D:2 * D], 1.0 / (32 ** 0.5)).then_inc(S("w0_scaled"), 1)
            act.wait_ge(S("ln0_by_dve"), 1)
            nc.scalar.activation(ln_a[:, 3, :], ln_a[:, 2, :], ACT.Sqrt).then_inc(S("sqrt0"), 1)
            act.wait_ge(S("ln0_by_dve"), 2)

            def turned(g):
                act.wait_ge(S("tr0"), g + 1)
                nc.scalar.copy(hT[:, 0, :], psA[:, :]).then_inc(S("ht0"), 1)

            def take(g):
                act.wait_ge(S("mm0"), g + 1)
                act.wait_ge(S("tab0_free"), g + 1)
                nc.scalar.copy(tab[:, :, :], psB[:, :, 0:3 * D]).then_inc(S("raw0"), 1)

            act.sem_inc(S("raw0"), 1)
            nc.scalar.copy(hst[:, :, :], h_all[:, 0:BPG, :]).then_inc(S("h0_group"), 1)
            with act.Fori(0, NG - 1) as g:
                turned(g)
                nc.scalar.copy(hst[:, :, :], h_all[:, bass.ds((g + 1) * BPG, BPG), :]).then_inc(S("h0_group"), 1)
                take(g)
            turned(NG - 1)
            take(NG - 1)

        def proj0_pe(pe):
            pe.wait_ge(S("w0_scaled"), 2)
            with pe.Fori(0, NG) as g:
                pe.wait_ge(S("h0_group"), g + 1)
                for j in range(BPG):
                    ins = nc.tensor.transpose(psA[:, j * P:(j + 1) * P], hst[:, j, :], ident[:, :])
                ins.then_inc(S("tr0"), 1)
                pe.wait_ge(S("ht0"), g + 1)
                pe.wait_ge(S("raw0"), g + 1)
                for j in range(BPG):
                    ins = nc.tensor.matmul(psB[:, j, 0:3 * D], hT[:, 0, j * P:(j + 1) * P], wcat0[:, :], start=True, stop=True)
                ins.then_inc(S("mm0"), 1)

        def proj0_pool(g_):
            with g_.Fori(0, NG) as g:
                g_.wait_ge(S("raw0"), g + 2)
                g_.tensor_tensor(tab[:, :, :], tab[:, :, :], bcat0[:, :].unsqueeze(1).to_broadcast([P, BPG, 3 * D]), ALU.add).then_inc(S("tab0"), 1)

        def proj0_sp(sp):
            sp.sem_inc(S("tab0_free"), 1)
            with sp.Fori(0, NG) as g:
                sp.wait_ge(S("tab0"), g + 1)
                sp.dma_start(grows(k0_t, g), tab[:, :, 0:D]).then_inc(S("j0_out"), 16)
                sp.dma_start(grows(q0_t, g), tab[:, :, D:2 * D]).then_inc(S("j0_out"), 16)
                sp.dma_start(grows(qm0_t, g)[:, :, 0:2 * D], tab[:, :, D:3 * D]).then_inc(S("j0_out"), 16)
                sp.wait_ge(S("j0_out"), g * 48 + 48)
                sp.sem_inc(S("tab0_free"), 1)

        SCATTERED = ["j1", "j2"]

        def scatter_pool(g_, nm, a, z, t):
            base = staged(NG)
            with g_.Fori(0, NG) as g:
                g_.wait_ge(*proj_on(nm, "tab", g + 1))
                g_.sem_inc(S("pool_go"), 1)
                g_.tensor_copy(fe_i[:, :], spos[:, bass.ds(g * BPG, BPG)]).then_inc(S("staged"), 1)
                g_.wait_ge(S("staged"), g + (base + 1))
                g_.sem_inc(S("pool_go"), 1)
                for j in range(BPG):
                    g_.indirect_dma_start(t, bass.IndirectOffsetOnAxis(ap=fe_i[:, j:j + 1], axis=0), tab[:, j, a:z], None)\
                      .then_inc(S("scat_out"), 16)

        def table(what, o):
            return S("tables_made"), 9 + o if what == "cum" else 4 * o + ("segments", "ends", "parts", "masks").index(what) + 1

        def order_sp(sp, o):
            def sorted_keys():
                sp.dma_start(raw, sorted_dram[o, 0:EP].bitcast(I32).rearrange("(p t) -> p t", t=T)).then_inc(S("raw_in"), 16)

            if o == 0:
                sorted_keys()
            else:
                with sp.If(unsorted(sp) > 0):
                    sp.wait_ge(S("keyrow_out"), 16)
                    sorted_keys()
                with sp.If(unsorted(sp) < 1):
                    sp.wait_ge(S("edges_padded"), 2)
                    edges_in(sp, (("dst", seg_i), ("src", oth_i[1])), S("edges_in"))
            sp.wait_ge(*table("segments", o))
            sp.dma_start(keyrow_t[o], seg16).then_inc(S("keyrow_out"), 16)

        def edges_in(sp, what, sem):
            full, rest = E // T, E % T
            for name, dst in what:
                sp.dma_start(dst[0:full, 0:T], A[name][0:full * T].rearrange("(p t) -> p t", t=T)).then_inc(sem, 16)
                sp.dma_start(dst[full:full + 1, 0:rest], A[name][full * T:E].rearrange("(p t) -> p t", p=1)).then_inc(sem, 16)

        PAD_COL, PAD_ROW = E % T, E // T // 32 * 32

        def order_dve(v, o):
            if o == 0:
                q = line(v)
                v.wait_ge(S("raw_in"), 16)
                q.did(nc.vector.tensor_scalar(seg_i[:, :], raw, 13, 0x1FFF, ALU.logical_shift_right, ALU.bitwise_and))
                q.do(nc.vector.tensor_scalar(oth_i[0][:, 0:T], raw, 0x1FFF, 0, ALU.bitwise_and, ALU.bitwise_or))
            else:
                with v.If(unsorted(v) > 0):
                    q = Seq(v, S("decode_steps"))
                    v.wait_ge(S("raw_in"), 32)
                    q.did(nc.vector.tensor_scalar(seg_i[:, :], raw, 18, 0x1FFF, ALU.logical_shift_right, ALU.bitwise_and))
                    q.do(nc.vector.tensor_scalar(oth_i[1][:, 0:T], raw, 0x3FFFF, 0, ALU.bitwise_and, ALU.bitwise_or))
                    q.do(nc.vector.tensor_scalar(seg_i[:, :], seg_i[:, :], 32.0, None, ALU.subtract))
                with v.If(unsorted(v) < 1):
                    nc.vector.memset(seg_i[PAD_ROW:P, PAD_COL:T], PADN).then_inc(S("edges_padded"), 1)
                    nc.vector.memset(oth_i[1][PAD_ROW:P, PAD_COL:T], PADN).then_inc(S("edges_padded"), 1)
                    v.wait_ge(S("edges_in"), 64)
                q = line(v)
                v.wait_ge(S("keyrow_out"), 16)
            q.did(nc.vector.tensor_copy(seg16, seg_i[:, :]))
            q.did(nc.vector.tensor_copy(head_i[o][:, :], seg_i[:, 0:1]))
            q.do(nc.vector.tensor_copy(segf, seg_i[:, :]))
            v.sem_inc(S("tables_made"), 1)
            q.did(nc.vector.tensor_scalar(diag2[:, 0, :], ident[:, :], segf[:, 0:1], None, ALU.mult))
            q.do(nc.vector.tensor_scalar(diag2[:, 1, :], ident[:, :], segf[:, T - 1:T], None, ALU.mult))
            v.sem_inc(S("tables_made"), 1)
            v.wait_ge(S("ends_rows"), o + 1)
            q.do(nc.vector.tensor_copy(firstrow[:, :], psC[:, 0:P]))

        def masks_dve(v, o):
            q = line(v)
            q.do(nc.vector.tensor_scalar(same, segf, segf[:, 0:1], None, ALU.is_equal))
            q.do(nc.vector.tensor_reduce(mcar[:, 0:1], same, AX.X, ALU.add))
            q.do(nc.vector.scalar_tensor_tensor(out=mcar[:, 1:2], in0=nid[:, 0:1], scalar=float(T), in1=mcar[:, 0:1], op0=ALU.mult, op1=ALU.add))
            q.did(nc.vector.tensor_scalar(patch_i[o][:, :], mcar[:, 1:2], -1.0, None, ALU.add))
            q.do(nc.vector.tensor_tensor(same[:, 1:T], segf[:, 1:T], segf[:, 0:T - 1], ALU.is_equal))
            q.did(nc.vector.scalar_tensor_tensor(out=contT[o][:, :], in0=firstrow[:, :], scalar=segf[:, T - 1:T], in1=after[:, :],
                                                 op0=ALU.is_equal, op1=ALU.mult))
            q.do(nc.vector.scalar_tensor_tensor(out=bias2[o][:, :], in0=psC[:, P:2 * P], scalar=segf[:, 0:1], in1=before[:, :],
                                                op0=ALU.is_equal, op1=ALU.mult))
            q.do(nc.vector.tensor_reduce(same[:, 0:1], bias2[o][:, :], AX.X, ALU.max))
            q.did(nc.vector.tensor_scalar(restart[o][:, :], same, BIG, -BIG, ALU.mult, ALU.add))
            q.do(nc.vector.tensor_scalar(bias2[o][:, :], bias2[o][:, :], BIG, -BIG, ALU.mult, ALU.add))
            if o == 0:
                q.do(nc.vector.tensor_tensor_scan(cnt[:, :], same, ones[:, 0:1].to_broadcast([P, T]), 0.0, ALU.mult, ALU.add))
            v.sem_inc(S("tables_made"), 1)

        def order_pe(pe, o):
            pe.wait_ge(*table("ends", o))
            nc.tensor.matmul(psC[:, 0:2 * P], ones[:, :], diag2[:, :, :].rearrange("p a b -> p (a b)"), start=True, stop=True).then_inc(S("ends_rows"), 1)

        def node_parts_dve(v, o):
            q = line(v)
            if o == 0:
                q.did(nc.vector.tensor_scalar(nt_b[:, 0:NB], nid[:, :], 0.5, None, ALU.add))
            q.do(nc.vector.tensor_tensor(cmp_n, firstrow[:, :].unsqueeze(1).to_broadcast([P, NB, P]),
                                         nid[:, :].unsqueeze(2).to_broadcast([P, NB, P]), ALU.is_le))
            q.do(nc.vector.tensor_reduce(nt_q[o][:, :], cmp_n, AX.X, ALU.add))
            q.do(nc.vector.tensor_scalar(nt_q[o][:, :], nt_q[o][:, :], -1.0, 0.0, ALU.add, ALU.max))
            q.do(nc.vector.tensor_copy(nt_i[o][:, 0:NB], nt_q[o][:, :]))
            v.sem_inc(S("tables_made"), 1)

        def node_ends_dve(v, o):
            q = line(v)
            v.wait_ge(S("nt_counted"), (NB, NB + NB2)[o])
            cum = nt_c[o][:, 1:NB + 1]
            q.do(nc.vector.tensor_scalar(cum, cum, 0.5, T / 2, ALU.mult, ALU.add))
            q.do(nc.vector.scalar_tensor_tensor(out=cum, in0=nt_q[o][:, :], scalar=float(T), in1=cum, op0=ALU.mult, op1=ALU.add))
            v.sem_inc(S("tables_made"), 1)
            v.wait_ge(S("nt_prev"), o + 1)
            has, prev, none = nt_f[:, 0, :], nt_f[:, 1, :], nt_f[:, 2, :]
            q.do(nc.vector.tensor_copy(prev, psD[:, 0:NB]))
            q.do(nc.vector.tensor_tensor(has, cum, prev, ALU.is_gt))
            q.did(nc.vector.tensor_scalar(none, nid[:, :], float(EP), None, ALU.add))
            q.do(nc.vector.scalar_tensor_tensor(out=cum, in0=cum, scalar=-float(EP + 1), in1=has, op0=ALU.add, op1=ALU.mult))
            q.did(nc.vector.tensor_scalar(endix[o][:, :], cum, float(EP), None, ALU.add))
            q.do(nc.vector.tensor_tensor(prev, prev, none, ALU.subtract))
            q.do(nc.vector.tensor_tensor(prev, prev, has, ALU.mult))
            q.do(nc.vector.tensor_tensor(spos[:, :], prev, none, ALU.add))
            v.sem_inc(S("nodes_ready"), 1)

        def nodes_pool(g_):
            g_.wait_ge(S("keyrow_out"), 16)
            g_.wait_ge(*table("parts", 0))
            g_.sem_inc(S("nt_counted0"), 2)
            g_.sem_inc(S("nt_counted1"), 2)
            base = staged(2 * NG)
            with g_.Fori(0, NG) as g:
                for b in range(2):
                    g_.wait_ge(S(f"nt_counted{b}"), g * 2 + 2)
                    g_.sem_inc(S("pool_go"), 1)
                    g_.tensor_copy(half_i[b][:, :], nt_i[0][:, bass.ds(g * BPG + 2 * b, 2)]).then_inc(S("staged"), 1)
                    g_.wait_ge(S("staged"), g * 2 + (base + b + 1))
                    g_.sem_inc(S("pool_go"), 1)
                    for j in range(2):
                        g_.indirect_dma_start(rows4[b][:, j, :], None, keyrow_t[0], bass.IndirectOffsetOnAxis(ap=half_i[b][:, j:j + 1], axis=0))\
                          .then_inc(S(f"nt_in{b}"), 16)

        def count_act(o, n, row):
            nc.scalar.activation(rsign, row, ACT.Sign, scale=-1.0, bias=nt_b[:, bass.ds(n, 1)],
                                 accum_out=nt_c[o][:, bass.ds(n + 1, 1)]).then_inc(S("nt_counted"), 1)

        def nodes_act(act):
            act.wait_ge(*table("parts", 0))
            act.wait_ge(S("dummies"), DUMMIES)
            with act.Fori(0, NG) as g:
                for b in range(2):
                    act.wait_ge(S(f"nt_in{b}"), g * 32 + 32)
                    for j in range(2):
                        n = g * BPG + (2 * b + j)
                        count_act(0, n, rows4[b][:, j, :])
                        act.wait_ge(S("nt_counted"), n + 1)
                    act.sem_inc(S(f"nt_counted{b}"), 2)

        def nodes_pe(pe, o):
            pe.wait_ge(*table("cum", o))
            nc.tensor.matmul(psD[:, 0:NB], down1[:, :], nt_c[o][:, 1:NB + 1], start=True, stop=False)
            nc.tensor.matmul(psD[:, 0:NB], wrap1[:, :], nt_c[o][:, 0:NB], start=False, stop=True).then_inc(S("nt_prev"), 1)

        def spread_sp(sp, o, t):
            sp.wait_ge(S("j0_out"), 16 * 3 * NG)
            sp.wait_ge(*table("masks", 1))
            sp.wait_ge(S("keyrow_out"), 32)
            if o:
                sp.wait_ge(*PB.on("laid", IT + 1))
            sp.dma_start(near_all, t.rearrange("(j p) w -> p j w", p=P)).then_inc(S("spread_in"), 16)

        def spread_pool(g_, o, t):
            g_.wait_ge(S("nodes_ready"), o + 1)
            g_.wait_ge(S("zeroed"), 32)
            if o:
                g_.wait_ge(S("zeroed_a"), 16 * (IT // 2))
            g_.wait_ge(S("spread_in"), 16 * (o + 1))
            for j in range(NN):
                g_.indirect_dma_start(t, bass.IndirectOffsetOnAxis(ap=spos[:, j:j + 1], axis=0), near_all[:, j, :], None).then_inc(S("spread_out"), 16)

        def payload_in(sp, c):
            sp.wait_ge(S("attr_free"), c + 1)
            r0 = c * (P * KE)
            if isinstance(c, int) and c == NPAY - 1:
                left = E - c * P * KE
                w = left // KE
                parts = [(0, w // 16 * 16, KE), (w // 16 * 16, w, KE), (w, w + 1, left - w * KE)]
            else:
                parts = [(0, P, KE)]
            for j, (a, z, k) in enumerate(parts):
                done = S("attr_in") if j == len(parts) - 1 else S("attr_part")
                if j and j == len(parts) - 1:
                    sp.wait_ge(S("attr_part"), 16 * 3 * j)
                r, n = r0 + a * KE, (z - a) * k
                sp.dma_start(attr[a:z, 0:k, :], A["edge_attr_64"][bass.ds(r, n), :].rearrange("(p t) w -> p t w", t=k)).then_inc(done, 16)
                sp.dma_start(pcol_i[a:z, 0:k], A["src"][bass.ds(r, n)].rearrange("(p t) -> p t", t=k)).then_inc(done, 16)
                sp.dma_start(pcol_f[a:z, 0:k], A["edge_weight"][bass.ds(r, n)].rearrange("(p t) -> p t", t=k)).then_inc(done, 16)

        def payload_out(sp, c):
            sp.wait_ge(S("pay_made"), c + 1)
            for t in (pay_dram, paya_dram):
                sp.dma_start(t[bass.ds(c * (P * KE), P * KE), :].rearrange("(p t) w -> p t w", t=KE), pay0[:, :, :]).then_inc(S("pay_out"), 16)

        def payload_pe(pe):
            with pe.Fori(0, NPAY) as c:
                pe.wait_ge(S("attr_in"), c * 48 + 48)
                for u in range(KE // 2):
                    ins = nc.tensor.transpose(psB[:, u // 4, (u % 4) * P:(u % 4 + 1) * P],
                                              attr[:, 2 * u:2 * u + 2, :].rearrange("p a w -> p (a w)"), ident[:, :])
                ins.then_inc(S("attr_tr"), 1)
                pe.wait_ge(S("attrT_in"), c + 1)
                for u in range(KE // 2):
                    nc.tensor.matmul(psD[:, u * 16:(u + 1) * 16], attrT[:, u, :], we2[:, :], start=True, stop=False)
                    ins = nc.tensor.matmul(psD[:, u * 16:(u + 1) * 16], ones[0:1, :], be2[:, :], start=False, stop=True)
                ins.then_inc(S("pay_mm"), 1)

        def payload_turned_act(act, c):
            act.wait_ge(S("attr_tr"), c + 1)
            nc.scalar.copy(attrT[:, :, :].rearrange("p a b -> p (a b)"), psB[:, :, :].rearrange("p a b -> p (a b)")[:, 0:KE // 2 * P])\
              .then_inc(S("attrT_in"), 1)
            act.wait_ge(S("pay_out"), c * 32 + 32)
            nc.scalar.copy(pay0[:, :, 0:1].rearrange("p t w -> p (t w)"), pcol_i[:, :]).then_inc(S("pay_cols"), 1)
            nc.scalar.copy(pay0[:, :, 1:2].rearrange("p t w -> p (t w)"), pcol_f[:, :]).then_inc(S("pay_cols"), 1)
            act.wait_ge(S("pay_cols"), c * 2 + 2)
            act.sem_inc(S("attr_free"), 1)

        def payload_made_act(act, c):
            act.wait_ge(S("pay_mm"), c + 1)
            nc.scalar.copy(pay0[:, :, 2:10], psD[:, 0:KE // 2 * 16].rearrange("p (t w) -> p t w", w=8)).then_inc(S("pay_made"), 1)

        def paysort_pool(g_):
            g_.wait_ge(*table("masks", 1))
            g_.wait_ge(S("pay_out"), 32 * NPAY + 32)
            with g_.Fori(0, IT // 2) as i:
                for b in range(2):
                    g_.wait_ge(S(f"paya_out{b}"), i * 16 + 16)
                    g_.wait_ge(S(f"paya_cols{b}"), i * 2 + 1)
                    g_.sem_inc(S("pool_go"), 1)
                    g_.tensor_copy(ix_s[b][:, :], oth_i[1][:, bass.ds(i * (2 * K) + b * K, K)]).then_inc(S(f"paya_ix{b}"), 1)
                    g_.wait_ge(S(f"paya_ix{b}"), i + 1)
                    g_.sem_inc(S("pool_go"), 1)
                    for k in range(K):
                        g_.indirect_dma_start(pay[b][:, k, :], None, pay_dram, bass.IndirectOffsetOnAxis(ap=ix_s[b][:, k:k + 1], axis=0))\
                          .then_inc(S(f"paya_in{b}"), 16)

        def paysort_dve(v):
            for b in range(2):
                v.sem_inc(S(f"paya_cols{b}"), 1)
            with v.Fori(0, IT // 2) as i:
                for b in range(2):
                    v.wait_ge(S(f"paya_in{b}"), i * (16 * K) + 16 * K)
                    cols = bass.ds(i * (2 * K) + b * K, K)
                    nc.vector.tensor_copy(oth_i[1][:, cols], pay[b][:, :, 0]).then_inc(S(f"paya_cols{b}"), 1)
                    nc.vector.tensor_copy(ew[:, cols], pay[b][:, :, 1]).then_inc(S(f"paya_cols{b}"), 1)
            for b in range(2):
                v.wait_ge(S(f"paya_cols{b}"), IT + 1)

        def weights_sp(sp):
            sp.wait_ge(S("ew_padded"), 1)
            edges_in(sp, (("edge_weight", ew),), S("ew_in"))

        def paysort_sp(sp):
            for b in range(2):
                sp.sem_inc(S(f"paya_out{b}"), 16)
            with sp.Fori(0, IT // 2) as i:
                for b in range(2):
                    sp.wait_ge(S(f"paya_in{b}"), i * (16 * K) + 16 * K)
                    sp.dma_start(paya_dram.rearrange("(p t) w -> p t w", t=T)[:, bass.ds(i * (2 * K) + b * K, K), :],
                                 pay[b][:, :, :]).then_inc(S(f"paya_out{b}"), 16)

            for b in range(2):
                sp.wait_ge(S(f"paya_out{b}"), 16 * (IT // 2) + 16)

        def pass_pool(g_, q):
            wd_s = q.tabs.shape[1]
            for nm in q.needs:
                g_.wait_ge(S(nm[0]), nm[1])
            if q is PB:
                g_.wait_ge(S("keyrow_out"), 32)
            if q.near is not None:
                g_.indirect_dma_start(head[:, 0:q.HF], None, q.tabd, bass.IndirectOffsetOnAxis(ap=head_i[q.o][:, 0:1], axis=0)).then_inc(q.s("head_in"), 16)
            with g_.Fori(0, IT // 2) as i:
                for b in range(2):
                    g_.wait_ge(*q.on(f"free{b}", i + 1))
                    g_.sem_inc(S("pool_go"), 1)
                    for k in range(K):
                        g_.indirect_dma_start(rows_s[b][:, k, 0:wd_s], None, q.tabs, bass.IndirectOffsetOnAxis(ap=ix_s[b][:, k:k + 1], axis=0))\
                          .then_inc(q.own(f"rows{b}"), 16)
                    if q is PB and b:
                        g_.wait_ge(S("nt_counted"), i + NB)
                        g_.sem_inc(S("pool_go"), 1)
                        g_.indirect_dma_start(row1, None, keyrow_t[1], bass.IndirectOffsetOnAxis(ap=row_i[:, 0:1], axis=0)).then_inc(q.own(f"rows{b}"), 16)

        def heads(t, q):
            return t[:, 0:q.H, :]

        def pass_dve(v, q):
            H, dh, F, HF = q.H, q.dh, q.F, q.HF
            f2 = lambda a: a.rearrange("p h t -> p (h t)")
            by_t = lambda a, f: a[:, 0:f * (K + 1)].rearrange("p (f t) -> p f t", t=K + 1)
            stv, bvv, hv = by_t(st, F), by_t(bv, F), by_t(hold, HF)
            bvh = bvv.rearrange("p (h j) t -> p h j t", h=H)
            p0 = Seq(v, q.s("prep"), q.base("prep"))
            p0.did(nc.vector.memset(stv, 0.0))
            p0.did(nc.vector.memset(bvv[:, :, 0:1], 0.0))
            p0.did(nc.vector.memset(m_ext[:, :, :], -BIG))
            p0.did(nc.vector.memset(by_t(nsb, D)[:, :, 0:1], 0.0))
            p0.did(nc.vector.memset(by_t(abig, D)[:, :, 0:1], 0.0))
            p0.wait()
            if q is PA:
                v.wait_ge(S("edges_ready"), 1)
            if q is PB:
                nc.vector.tensor_copy(row_i[:, :], nt_i[1][:, 0:1]).then_inc(S("row_staged"), 1)
                v.wait_ge(S("row_staged"), 1)
            for b in range(2):
                nc.vector.tensor_copy(ix_s[b][:, :], oth_i[q.o][:, b * K:(b + 1) * K]).then_inc(q.s(f"free{b}"), 1)
            if q is P1:
                bias_dve(v, bo_1)
            with v.Fori(0, IT // 2) as i:
                for b in range(2):
                    c = Seq(v, q.s("steps"), q.base("steps") + b * q.steps, i, 2 * q.steps)
                    t0 = i * (2 * K) + b * K
                    cols = bass.ds(t0, K)
                    rs, rd = rows_s[b], rows_d[b]
                    s = heads(s_ext, q)[:, :, 1:K + 1]
                    decay = abig if q.soft or b else nsb

                    def leave():
                        c.did(nc.vector.tensor_copy(ix_s[b][:, :], oth_i[q.o][:, bass.ds(t0 + 2 * K, K)]))
                        if q is PB and b:
                            nc.vector.tensor_copy(row_i[:, :], nt_i[1][:, bass.ds(i + 1, 1)]).then_inc(S("row_staged"), 1)
                            v.wait_ge(S("row_staged"), i + 2)
                        c.wait()
                        v.sem_inc(q.s(f"free{b}"), 1)

                    if q.near is not None:
                        v.wait_ge(*q.on("made", i * (2 * q.made) + (b + 1) * q.made))
                        n = HF * (K + 1)
                        c.do(nc.vector.tensor_tensor_scan(hold[:, 0:n], (nsb if q.soft or not b else abig)[:, 0:n], zt[:, 0:n], 0.0, ALU.mult, ALU.add))
                        v.sem_inc(q.s("held"), 1)
                    rows = K + (q is PB and b)
                    v.wait_ge(q.own(f"rows{b}"), i * (16 * rows) + 16 * rows)
                    if q in (PB, PA, P1):
                        c.do(nc.vector.tensor_tensor(rd[:, :, :], rs[:, :, 0:D], hv[:, :, 1:K + 1].rearrange("p f t -> p t f"), ALU.mult))
                        c.did(nc.vector.tensor_reduce(s.rearrange("p h t -> p t h"), rd[:, :, :].rearrange("p t (h d) -> p t h d", h=H), AX.X, ALU.add))
                    if q is PB:
                        leave()
                    if q is PA:
                        c.wait()
                        c.did(nc.vector.tensor_tensor(heads(ww, q), s, rs[:, :, 2 * D:2 * D + H].rearrange("p t h -> p h t"), ALU.subtract))
                    if q is P1:
                        v.wait_ge(S(f"bias_in{b}"), i * 16 + 16)
                        c.wait()
                        c.do(nc.vector.scalar_tensor_tensor(out=s, in0=s, scalar=float(dh) ** -0.5, in1=pay[b][:, :, 2:2 + H].rearrange("p t h -> p h t"),
                                                            op0=ALU.mult, op1=ALU.add))
                        v.sem_inc(S(f"bias_used{b}"), 1)
                    if q is P2:
                        c.do(nc.vector.tensor_tensor(s, rs[:, :, D:D + H].rearrange("p t h -> p h t"), hv[:, :, 1:K + 1], ALU.add))
                        c.do(nc.vector.scalar_tensor_tensor(out=s, in0=s, scalar=0.2, in1=s, op0=ALU.mult, op1=ALU.max))
                    if q.soft:
                        smx = heads(s_max, q) if q is P2 else heads(s_ext, q)
                        if q is P2:
                            c.did(nc.vector.tensor_scalar(smx[:, :, 1:K + 1], s, 0.0, None, ALU.max))
                        rsh, mx = heads(rst, q), heads(m_ext, q)
                        c.did(nc.vector.tensor_copy(smx[:, :, 0:1], mx[:, :, K:K + 1]))
                        c.did(nc.vector.tensor_copy(rsh[:, :, 1:K + 1], restart[q.o][:, cols].unsqueeze(1).to_broadcast([P, H, K])))
                        v.wait_ge(*q.on("laid", i * 2 + b + 1))
                        c.wait()
                        c.do(nc.vector.tensor_tensor_scan(f2(mx), f2(rsh), f2(smx), -BIG, ALU.add, ALU.max))
                        c.did(nc.vector.tensor_tensor(heads(dtmp, q), mx[:, :, 0:K], mx[:, :, 1:K + 1], ALU.subtract))
                        c.did(nc.vector.tensor_tensor(heads(ww, q), s, mx[:, :, 1:K + 1], ALU.subtract))
                        c.wait()
                        c.did(nc.vector.tensor_tensor(heads(dd, q)[:, :, 1:K + 1], heads(dtmp, q), rsh[:, :, 1:K + 1], ALU.add))
                    if q.soft or q is PA:
                        c.wait()
                        v.sem_inc(q.s("arg"), 1)
                    if q is P3:
                        c.did(nc.vector.tensor_tensor(bvv[:, :, 1:K + 1], rs[:, :, 0:D].rearrange("p t f -> p f t"),
                                                      ew[:, cols].unsqueeze(1).to_broadcast([P, D, K]), ALU.mult))
                    elif q is PA:
                        v.wait_ge(*q.on("expw", i * 2 + b + 1))
                        c.do(nc.vector.tensor_tensor(heads(ww, q), heads(ww, q), rs[:, :, 2 * D + H:2 * D + 2 * H].rearrange("p t h -> p h t"), ALU.mult))
                        c.did(nc.vector.tensor_tensor(bvh[:, :, :, 1:K + 1], rs[:, :, D:2 * D].rearrange("p t (h j) -> p h j t", h=H),
                                                      heads(ww, q).unsqueeze(2).to_broadcast([P, H, 32, K]), ALU.mult))
                    elif dh:
                        v.wait_ge(*q.on("expw", i * 2 + b + 1))
                        off = D if q is P1 else 0
                        c.did(nc.vector.tensor_tensor(bvh[:, :, 0:dh, 1:K + 1], rs[:, :, off:off + D].rearrange("p t (h j) -> p h j t", h=H),
                                                      bvh[:, :, dh:dh + 1, 1:K + 1].to_broadcast([P, H, dh, K]), ALU.mult))
                    if q is not PB:
                        leave()
                    c.wait()
                    if q.soft:
                        v.wait_ge(*q.on("decay", i * 2 + b + 1))
                    else:
                        v.wait_ge(*q.on("made", i * (2 * q.made) + (b + 1) * q.made))
                        v.wait_ge(*q.on("laid", i * 2 + b + 1))
                    c.do(nc.vector.tensor_tensor_scan(st[:, 0:F * (K + 1)], decay[:, 0:F * (K + 1)], bv[:, 0:F * (K + 1)], 0.0, ALU.mult, ALU.add))
                    v.sem_inc(q.s("scanned"), 1)
                    assert c.k == q.steps, (q.name, c.k, q.steps)

        def near_act(act, q, i, b):
            all_t = lambda a: a[:, 0:q.HF * (K + 1)].rearrange("p (f t) -> p f t", t=K + 1)
            by_t = lambda a: all_t(a)[:, :, 1:K + 1]
            first = isinstance(i, int) and i == 0 and b == 0
            if q.near is not None:
                if first:
                    act.wait_ge(*q.on("head_in", 16))
                    nc.scalar.copy(all_t(zt)[:, :, 0:1], head[:, 0:q.HF].unsqueeze(2)).then_inc(q.s("made"), 1)
                else:
                    act.wait_ge(*q.on("held", i * 2 + b))
                    nc.scalar.copy(all_t(zt)[:, :, 0:1], all_t(hold)[:, :, K:K + 1]).then_inc(q.s("made"), 1)
                act.wait_ge(*q.on(f"near_in{b}", i * 16 + 16))
                nc.scalar.copy(by_t(zt), rows_d[b][:, :, :].rearrange("p t w -> p (t w)")[:, 0:K * q.HF].rearrange("p (t f) -> p f t", f=q.HF))\
                  .then_inc(q.s("made"), 1)
            nc.scalar.activation(by_t(nsb if q.soft or not b else abig), restart[q.o][:, bass.ds(i * (2 * K) + b * K, K)].unsqueeze(1).to_broadcast([P, q.HF, K]),
                                 ACT.Exp).then_inc(q.s("made"), 1)

        def pass_act(act, q):
            H, dh, F, W = q.H, q.dh, q.F, q.W
            act.sem_inc(q.s("laid"), 1)
            act.wait_ge(*q.on("prep", 5))
            bvh = bv[:, 0:F * (K + 1)].rearrange("p (h j t) -> p h j t", h=H, t=K + 1)
            stv = st[:, 0:F * (K + 1)].rearrange("p (f t) -> p f t", t=K + 1)

            def two(i, last):
                for b in range(2):
                    if q.soft or q is PA:
                        act.wait_ge(*q.on("arg", i * 2 + b + 1))
                    if q.soft:
                        nc.scalar.activation(bvh[:, :, dh, 1:K + 1], heads(ww, q), ACT.Exp).then_inc(q.s("expw"), 1)
                        nc.scalar.activation(abig[:, 0:F * (K + 1)].rearrange("p (h j t) -> p h j t", h=H, t=K + 1),
                                             heads(dd, q).unsqueeze(2).to_broadcast([P, H, dh + 1, K + 1]), ACT.Exp).then_inc(q.s("decay"), 1)
                    elif q is PA:
                        nc.scalar.activation(heads(ww, q), heads(ww, q), ACT.Exp).then_inc(q.s("expw"), 1)
                    if not (last and b):
                        near_act(act, q, i + b, 1 - b)
                    if q is PB:
                        (payload_made_act if b else payload_turned_act)(act, i)
                        if b:
                            count_act(1, i, row1)
                            act.wait_ge(S("nt_counted"), i + (NB + 1))
                    act.wait_ge(*q.on("scanned", i * 2 + b + 1))
                    act.wait_ge(*q.on(f"sent{b}", i * 16 + 16))
                    pr = psrow[b][:, 0:K * W].rearrange("p (t w) -> p t w", w=W)
                    nc.scalar.copy(bvh.rearrange("p h j t -> p (h j) t")[:, :, 0:1], stv[:, :, K:K + 1])
                    ins = nc.scalar.copy(pr[:, :, 0:F], stv[:, :, 1:K + 1].rearrange("p f t -> p t f"))
                    if q.soft:
                        ins = nc.scalar.copy(pr[:, :, F:F + H], heads(m_ext, q)[:, :, 1:K + 1].rearrange("p h t -> p t h"))
                    if q is PB:
                        ins = nc.scalar.copy(pr[:, :, F + H:F + H + 1].rearrange("p t w -> p (t w)"), cnt[:, bass.ds(i * (2 * K) + b * K, K)])
                    ins.then_inc(q.s("laid"), 1)
                    act.wait_ge(*q.on("laid", i * 2 + b + 2))
                    act.sem_inc(q.s(f"laid{b}"), 1)

            near_act(act, q, 0, 0)
            with act.Fori(0, IT // 2 - 1) as i:
                two(i, False)
            two(IT // 2 - 1, True)

        def pass_store(sp, q, i, b):
            sp.wait_ge(*q.on(f"laid{b}", i + 1))
            sp.dma_start(q.ps[0:EP, :].rearrange("(p t) w -> p t w", t=T)[:, bass.ds(i * (2 * K) + b * K, K), :],
                         psrow[b][:, 0:K * q.W].rearrange("p (t w) -> p t w", w=q.W)).then_inc(q.s(f"sent{b}"), 16)

        def bias_load(sp, n, b):
            sp.dma_start(pay[b][:, :, :], paya_dram.rearrange("(p t) w -> p t w", t=T)[:, bass.ds(n * (2 * K) + b * K, K), :])\
              .then_inc(S(f"bias_in{b}"), 16)

        def near_load(sp, q, i, b):
            sp.dma_start(rows_d[b][:, :, :].rearrange("p t w -> p (t w)")[:, 0:K * q.HF].rearrange("p (t w) -> p t w", w=q.HF),
                         q.near[0:EP, :].rearrange("(p t) w -> p t w", t=T)[:, bass.ds(i * (2 * K) + b * K, K), :]).then_inc(q.s(f"near_in{b}"), 16)

        def pass_sp(sp, q):
            for b in range(2):
                sp.sem_inc(q.s(f"sent{b}"), 16)
            if q is PB:
                sp.sem_inc(S("pay_out"), 32)
            if q.near is not None:
                for nm in q.started:
                    sp.wait_ge(S(nm[0]), nm[1])
            for b in range(2):
                if q.near is not None:
                    near_load(sp, q, 0, b)
                if q is P1:
                    bias_load(sp, 0, b)

            def two(i, last):
                if q is PB:
                    zeros_chunk_sp(sp, i)
                for b in range(2):
                    if not last and q.near is not None:
                        sp.wait_ge(*q.on(f"free{b}", i + 2))
                        near_load(sp, q, i + 1, b)
                    if not last and q is P1:
                        sp.wait_ge(S(f"bias_used{b}"), i + 1)
                        bias_load(sp, i + 1, b)
                    if q is PB and not b and not last:
                        payload_in(sp, i + 1)
                    pass_store(sp, q, i, b)
                if q is PB:
                    payload_out(sp, i)

            if q is PB:
                payload_in(sp, 0)
            peeled = 2 if q is PB else 1
            with sp.Fori(0, IT // 2 - peeled) as i:
                two(i, False)
            for i in range(IT // 2 - peeled, IT // 2):
                two(i, i == IT // 2 - 1)

        def carry_dve(v, q):
            H, dh, F = q.H, q.dh, q.F
            c = line(v)
            stv = st[:, 0:F * (K + 1)].rearrange("p (f t) -> p f t", t=K + 1)
            v.wait_ge(*q.on("laid", IT + 1))
            c.do(nc.vector.tensor_copy(cst[:, 0:F].unsqueeze(2), stv[:, :, K:K + 1]))
            if q is PB:
                c.do(nc.vector.tensor_copy(cst[:, F:F + 1], cnt[:, T - 1:T]))
            if q.soft:
                dw = dwide[:, 0:H * P].rearrange("p (h r) -> p h r", h=H)
                c.do(nc.vector.tensor_tensor(dw, ident[:, :].unsqueeze(1).to_broadcast([P, H, P]),
                                             heads(m_ext, q)[:, :, K:K + 1].to_broadcast([P, H, P]), ALU.mult))
                v.sem_inc(q.s("carry_dve"), 1)
                v.wait_ge(*q.on("carry_pe", 1))
                pm = psC[:, 0:H * P].rearrange("p (h r) -> p h r", h=H)
                c.do(nc.vector.tensor_tensor(dw, pm, bias2[q.o][:, :].unsqueeze(1).to_broadcast([P, H, P]), ALU.add))
                c.do(nc.vector.tensor_reduce(mcar[:, 0:H], dw, AX.X, ALU.max))
                c.do(nc.vector.tensor_tensor(dw, dw, mcar[:, 0:H].unsqueeze(2).to_broadcast([P, H, P]), ALU.subtract))
                v.sem_inc(q.s("carry_dve"), 1)
            else:
                v.sem_inc(q.s("carry_dve"), 1)
            v.wait_ge(*q.on("prow_in", 16))
            if q.soft:
                m = pmx[:, :, 0:H]
                pm = prow[:, F:F + H]
                c.do(nc.vector.tensor_tensor(m[:, 0], pm, mcar[:, 0:H], ALU.max))
                c.did(nc.vector.tensor_tensor(m[:, 1], pm, m[:, 0], ALU.subtract))
                c.did(nc.vector.tensor_tensor(m[:, 2], mcar[:, 0:H], m[:, 0], ALU.subtract))
                c.wait()
                v.sem_inc(q.s("carry_dve"), 1)
                v.wait_ge(*q.on("carry_act", 4))
                by_h = lambda a: a.rearrange("p (h d) -> p h d", h=H)
                wide = lambda k: m[:, k].unsqueeze(2).to_broadcast([P, H, dh + 1])
                v.wait_ge(*q.on("carry_pe", 3))
                c.did(nc.vector.tensor_tensor(by_h(prow[:, 0:F]), by_h(prow[:, 0:F]), wide(1), ALU.mult))
                c.did(nc.vector.tensor_tensor(by_h(cst[:, 0:F]), by_h(psD[:, 0:F]), wide(2), ALU.mult))
                c.did(nc.vector.tensor_copy(pm, m[:, 0]))
                c.wait()
                c.did(nc.vector.tensor_tensor(prow[:, 0:F], prow[:, 0:F], cst[:, 0:F], ALU.add))
                if q is PB:
                    c.did(nc.vector.tensor_tensor(prow[:, F + H:F + H + 1], prow[:, F + H:F + H + 1], psD[:, F:F + 1], ALU.add))
            else:
                v.wait_ge(*q.on("carry_pe", 1))
                c.did(nc.vector.tensor_tensor(prow[:, 0:F], prow[:, 0:F], psD[:, 0:F], ALU.add))
            c.wait()
            v.sem_inc(q.s("patched"), 1)

        def carry_pool(g_, q):
            for b in range(2):
                g_.wait_ge(*q.on(f"sent{b}", 16 * (IT // 2) + 16))
            at = bass.IndirectOffsetOnAxis(ap=patch_i[q.o][:, 0:1], axis=0)
            g_.indirect_dma_start(prow[:, 0:q.W], None, q.ps, at).then_inc(q.s("prow_in"), 16)
            g_.wait_ge(*q.on("patched", 1))
            g_.indirect_dma_start(q.ps, at, prow[:, 0:q.W], None).then_inc(q.s("prow_out"), 16)

        def carry_pe(pe, q):
            H, dh, F = q.H, q.dh, q.F
            pe.wait_ge(*q.on("carry_dve", 1))
            if not q.soft:
                nc.tensor.matmul(psD[:, 0:F], contT[q.o][:, :], cst[:, 0:F], start=True, stop=True).then_inc(q.s("carry_pe"), 1)
                return
            for a in range(0, H * P, 512):
                ins = nc.tensor.matmul(psC[:, a:a + 512], ones[:, :], dwide[:, a:a + 512], start=True, stop=True)
            ins.then_inc(q.s("carry_pe"), 1)
            pe.wait_ge(*q.on("carry_act", 1))
            for h in range(H):
                ins = nc.tensor.transpose(psB[:, h // 4, (h % 4) * P:(h % 4 + 1) * P], wwide[:, h * P:(h + 1) * P], ident[:, :])
            ins.then_inc(q.s("carry_pe"), 1)
            pe.wait_ge(*q.on("carry_act", 2))
            for h in range(H):
                f = slice(h * (dh + 1), (h + 1) * (dh + 1))
                ins = nc.tensor.matmul(psD[:, f], dwide[:, h * P:(h + 1) * P], cst[:, f], start=True, stop=True)
            if q is PB:
                ins = nc.tensor.matmul(psD[:, F:F + 1], contT[q.o][:, :], cst[:, F:F + 1], start=True, stop=True)
            ins.then_inc(q.s("carry_pe"), 1)

        def carry_act(act, q):
            if not q.soft:
                return
            n = q.H * P
            act.wait_ge(*q.on("carry_dve", 2))
            nc.scalar.activation(wwide[:, 0:n], dwide[:, 0:n], ACT.Exp).then_inc(q.s("carry_act"), 1)
            act.wait_ge(*q.on("carry_pe", 2))
            nc.scalar.copy(dwide[:, 0:n], psB[:, :, :].rearrange("p a b -> p (a b)")[:, 0:n]).then_inc(q.s("carry_act"), 1)
            act.wait_ge(*q.on("carry_dve", 3))
            for k in (1, 2):
                nc.scalar.activation(pmx[:, k, 0:q.H], pmx[:, k, 0:q.H], ACT.Exp).then_inc(q.s("carry_act"), 1)

        def ends_pool(g_, q):
            g_.wait_ge(*q.on("prow_out", 16))
            g_.wait_ge(S("dummy_rows"), 16 * NDUMMY)
            for g in range(NG + 1):
                if g < NG:
                    for j in range(g * BPG, (g + 1) * BPG):
                        g_.indirect_dma_start(ends(q)[:, j, :], None, q.ps, bass.IndirectOffsetOnAxis(ap=endix[q.o][:, j:j + 1], axis=0))\
                          .then_inc(q.s(f"ends_in{g % 2}"), 16)
                if g:
                    g_.wait_ge(*q.on(f"ends_in{(g - 1) % 2}", 16 * BPG * ((g + 1) // 2)))
                    g_.sem_inc(q.s("ends_ready"), 1)

        def group_of(q, g):
            return ends(q)[:, bass.ds(g * BPG, BPG), :]

        def inverse_dve(v, q, g, c):
            v.wait_ge(*q.on("ends_ready", g + 1))
            c.do(nc.vector.tensor_scalar(mx4[:, 1, :, 0:q.H], group_of(q, g)[:, :, 0:q.F].rearrange("p j (h d) -> p j h d", h=q.H)[:, :, :, q.dh],
                                         1e-10, None, ALU.max if q is PB else ALU.add))
            c.do(nc.vector.reciprocal(mx4[:, 1, :, 0:q.H], mx4[:, 1, :, 0:q.H]))

        def stats_dve(v):
            q = PB
            with v.Fori(0, NG) as g:
                c = Seq(v, S("stats_steps"), 0, g, 4)
                inverse_dve(v, q, g, c)
                e = group_of(q, g)
                n = q.F + q.H
                to = stat[:, bass.ds(g * BPG, BPG), :, :]
                c.did(nc.vector.tensor_copy(to[:, :, 0, :], e[:, :, q.F:n]))
                c.do(nc.vector.tensor_tensor(to[:, :, 1, :], mx4[:, 1, :, 0:H0], e[:, :, n:n + 1].to_broadcast([P, BPG, H0]), ALU.mult))
            v.sem_inc(S("stats_done"), 1)

        def stats_sp(sp):
            with sp.Fori(0, NG) as g:
                sp.wait_ge(S("stats_steps"), g * 4 + 4)
                sp.dma_start(grows(qm0_t, g)[:, :, 2 * D:2 * D + 2 * H0],
                             stat[:, bass.ds(g * BPG, BPG), :, :].rearrange("p j a h -> p j (a h)")).then_inc(S("qm_out"), 16)

        def bias_dve(v, b):
            line(v).do(nc.vector.tensor_tensor(xsb[:, :, :], xsb[:, :, :], b[:, :].unsqueeze(1).to_broadcast([P, NB, D]), ALU.add))

        def end0_dve(v):
            q = PA
            with v.Fori(0, NG) as g:
                v.wait_ge(*q.on("ends_ready", g + 1))
                v.wait_ge(S("e0_tr"), g + 1)
                nc.vector.tensor_copy(hst[:, :, :], group_of(q, g)).then_inc(S("e0_steps"), 1)
            c = line(v)
            v.wait_ge(S("e0_hid"), NG)
            hid = hT_all[:, 0:N]
            c.do(nc.vector.tensor_reduce(bncol[:, 3:4], hid, AX.X, ALU.add))
            c.do(nc.vector.tensor_scalar(bncol[:, 3:4], bncol[:, 3:4], -1.0 / N, None, ALU.mult))
            c.do(nc.vector.tensor_scalar(hT_all[:, :], hT_all[:, :], bncol[:, 3:4], None, ALU.add))
            v.sem_inc(S("bn_by_dve"), 1)
            v.wait_ge(S("bn_by_act"), 1)
            c.do(nc.vector.tensor_scalar(bncol[:, 4:5], bncol[:, 4:5], 1.0 / N, EPS, ALU.mult, ALU.add))
            v.sem_inc(S("bn_by_dve"), 1)
            v.wait_ge(S("bn_by_act"), 2)
            c.do(nc.vector.reciprocal(bncol[:, 5:6], bncol[:, 5:6]))
            c.do(nc.vector.tensor_tensor(bncol[:, 5:6], bncol[:, 5:6], bncol[:, 1:2], ALU.mult))
            v.sem_inc(S("bn_by_dve"), 1)

            def add(g):
                v.wait_ge(S("e0_mm"), g + 1)
                xg = xsb[:, bass.ds(g * BPG, BPG), :]
                nc.vector.tensor_tensor(xg, xg, psC[:, 0:GN].rearrange("p (j d) -> p j d", j=BPG), ALU.add).then_inc(S("e0_added"), 1)
                v.wait_ge(S("e0_added"), g + 2)
                v.sem_inc(S("dve_go"), 1)

            v.sem_inc(S("e0_added"), 1)
            v.sem_inc(S("proj_psfree"), 1)
            add(0)
            norm_dve(v, "j1", 0)
            with v.Fori(1, NG) as g:
                add(g)
                norm_dve(v, "j1", g)
                take_dve(v, "j1", 3 * D, g - 1)
            take_dve(v, "j1", 3 * D, NG - 1)

        def end0_pe(pe):
            pe.sem_inc(S("e0_tr"), 1)
            with pe.Fori(0, NG) as g:
                pe.wait_ge(S("e0_steps"), g + 1)
                pe.wait_ge(S("e0_at"), g + 1)
                for j in range(BPG):
                    ins = nc.tensor.transpose(psA[:, j * P:(j + 1) * P], hst[:, j, :], ident[:, :])
                ins.then_inc(S("e0_tr"), 1)
                pe.wait_ge(S("e0_at"), g + 2)
                pe.wait_ge(S("e0_hid0"), g + 1)
                nc.tensor.matmul(psD[:, :], w1_0[:, :], hT[:, 0, :], start=True, stop=True).then_inc(S("e0_w1"), 1)

            def second(g):
                pe.wait_ge(S("e0_relu"), g + 1)
                pe.wait_ge(S("e0_added"), g + 1)
                for j in range(BPG):
                    ins = nc.tensor.matmul(psC[:, j * P:(j + 1) * P], hT[:, 0, j * P:(j + 1) * P], w2_0[:, :], start=True, stop=True)
                ins.then_inc(S("e0_mm"), 1)

            pe.sem_inc(S("proj_tr"), 1)
            second(0)
            with pe.Fori(0, NG - 1) as g:
                second(g + 1)
                proj_pe(pe, "j1", wcat1[:, :], 3 * D, g)
            proj_pe(pe, "j1", wcat1[:, :], 3 * D, NG - 1)

        def end0_act(act):
            act.sem_inc(S("e0_at"), 1)
            act.sem_inc(S("e0_hid0"), 1)
            with act.Fori(0, NG) as g:
                act.wait_ge(S("e0_tr"), g + 2)
                nc.scalar.copy(hT[:, 0, :], psA[:, :]).then_inc(S("e0_at"), 1)
                act.wait_ge(S("e0_w1"), g + 1)
                nc.scalar.activation(hT_all[:, bass.ds(g * GN, GN)], psD[:, :], ACT.Identity, bias=bncol[:, 0:1]).then_inc(S("e0_hid"), 1)
                act.wait_ge(S("e0_hid"), g + 1)
                act.sem_inc(S("e0_hid0"), 1)
            act.wait_ge(S("bn_by_dve"), 1)
            nc.scalar.activation(work[:, 0:N], hT_all[:, 0:N], ACT.Square, accum_out=bncol[:, 4:5]).then_inc(S("bn_by_act"), 1)
            act.wait_ge(S("bn_by_dve"), 2)
            nc.scalar.activation(bncol[:, 5:6], bncol[:, 4:5], ACT.Sqrt).then_inc(S("bn_by_act"), 1)
            act.wait_ge(S("bn_by_dve"), 3)

            def relu(g):
                nc.scalar.activation(hT[:, 0, :], hT_all[:, bass.ds(g * GN, GN)], ACT.Relu, bias=bncol[:, 2:3], scale=bncol[:, 5:6])\
                  .then_inc(S("e0_relu"), 1)

            act.sem_inc(S("proj_ht"), 1)
            relu(0)
            with act.Fori(0, NG - 1) as g:
                act.wait_ge(S("e0_mm"), g + 1)
                relu(g + 1)
                proj_act(act, "j1", g)
            proj_act(act, "j1", NG - 1)

        def values_dve(v, q, g, c, to, first_write):
            inverse_dve(v, q, g, c)
            first_write()
            c.do(nc.vector.tensor_tensor(to.rearrange("p j (h d) -> p j h d", h=q.H),
                                         group_of(q, g)[:, :, 0:q.F].rearrange("p j (h d) -> p j h d", h=q.H)[:, :, :, 0:q.dh],
                                         mx4[:, 1, :, 0:q.H].unsqueeze(3).to_broadcast([P, BPG, q.H, q.dh]), ALU.mult))

        vals = zero_t[:, :].rearrange("p (j d) -> p j d", d=D)

        def end1_dve(v):
            def values(g):
                c = group_seq(v, S("e1_steps"), g, 3)
                values_dve(v, P1, g, c, vals, lambda: v.wait_ge(S("end_tr"), g + 1))

            def add(g):
                v.wait_ge(S("end_mm"), g + 1)
                xg = xsb[:, bass.ds(g * BPG, BPG), :]
                nc.vector.tensor_tensor(xg, xg, psC[:, 0:GN].rearrange("p (j d) -> p j d", j=BPG), ALU.add).then_inc(S("e1_added"), 1)
                v.wait_ge(S("e1_added"), g + 2)
                v.sem_inc(S("dve_go"), 1)

            v.sem_inc(S("e1_added"), 1)
            v.sem_inc(S("proj_psfree"), 1)
            values(0)
            values(1)
            add(0)
            norm_dve(v, "j2", 0)
            with v.Fori(1, NG - 1) as g:
                values(g + 1)
                add(g)
                norm_dve(v, "j2", g)
                take_dve(v, "j2", D + 8, g - 1)
            add(NG - 1)
            norm_dve(v, "j2", NG - 1)
            take_dve(v, "j2", D + 8, NG - 2)
            take_dve(v, "j2", D + 8, NG - 1)

        E2 = 4 + LN_STEPS - 1

        def end2_dve(v):
            with v.Fori(0, NG) as g:
                c = Seq(v, S("j3_steps"), 0, g, E2)
                values_dve(v, P2, g, c, hst2[:, :, :], lambda: None)
                xg = xsb[:, bass.ds(g * BPG, BPG), :]
                c.do(nc.vector.tensor_tensor(xg, xg, hst2[:, :, :], ALU.add))
                v.sem_inc(S("dve_go"), 1)
                norm_group(v, "j3", g, c, lambda: v.wait_ge(*proj_on("j3", "tabfree", g + 1)))

        def end2_act(act):
            with act.Fori(0, NG) as g:
                sqrt_act(act, "j3", g)

        def end1_pe(pe):
            def product(g):
                pe.wait_ge(S("e1_steps"), g * 3 + 3)
                for j in range(BPG):
                    ins = nc.tensor.transpose(psD[:, j * P:(j + 1) * P], vals[:, j, :], ident[:, :])
                ins.then_inc(S("end_tr"), 1)
                pe.wait_ge(S("end_at"), g + 1)
                pe.wait_ge(S("e1_added"), g + 1)
                for j in range(BPG):
                    ins = nc.tensor.matmul(psC[:, j * P:(j + 1) * P], hT[:, 0, j * P:(j + 1) * P], wo_1[:, :], start=True, stop=True)
                ins.then_inc(S("end_mm"), 1)

            pe.sem_inc(S("end_tr"), 1)
            pe.sem_inc(S("proj_tr"), 1)
            product(0)
            with pe.Fori(0, NG - 1) as g:
                product(g + 1)
                proj_pe(pe, "j2", w_2[:, :], D + 8, g)
            proj_pe(pe, "j2", w_2[:, :], D + 8, NG - 1)

        def end1_act(act):
            def turned(g):
                act.wait_ge(S("end_tr"), g + 2)
                nc.scalar.copy(hT[:, 0, :], psD[:, :]).then_inc(S("end_at"), 1)

            act.sem_inc(S("proj_ht"), 1)
            turned(0)
            with act.Fori(0, NG - 1) as g:
                turned(g + 1)
                proj_act(act, "j2", g)
            proj_act(act, "j2", NG - 1)

        def weights3_pe(pe):
            pe.wait_ge(S("loaded"), 16 * NLOADS)
            pe.wait_ge(S("consts"), CONSTS)
            for j in range(2):
                ins = nc.tensor.transpose(psA[:, j * P:(j + 1) * P], w3raw[:, j, :], ident[:, :])
            ins.then_inc(S("w3_tr"), 1)
            pe.wait_ge(S("w3_in"), 1)

        def weights3_act(act):
            act.wait_ge(S("w3_tr"), 1)
            nc.scalar.copy(w3t[:, :, :].rearrange("p a b -> p (a b)"), psA[:, 0:2 * P]).then_inc(S("w3_in"), 1)

        def end3_dve(v):
            q = P3
            q3 = line(v)
            q3.do(nc.vector.tensor_tensor(b3[:, 0, :], b3[:, 0, :], b3[:, 1, :], ALU.add))
            v.wait_ge(S("h3_in"), 16)

            def factors(g, base, i):
                c = Seq(v, S("e3_factors"), base, i, 2)
                v.wait_ge(*q.on("ends_ready", g + 1))
                v.wait_ge(S("end_tr"), g + (NG + 1))
                h = h3_all[:, bass.ds(g * BPG, BPG), :]
                c.did(nc.vector.tensor_tensor(hst[:, :, :], group_of(q, g), h, ALU.add))
                c.did(nc.vector.tensor_tensor(tab[:, :, 0:D], group_of(q, g), h, ALU.mult))

            def finish(g, base, i):
                c = Seq(v, S("e3_out"), base + 3, i, 3)
                v.wait_ge(S("end_mm"), g + (NG + 1))
                v.wait_ge(S("y_out"), g * 16 + 16)
                c.do(nc.vector.tensor_tensor(hst2[:, :, :], psB[:, 2, :].rearrange("p (j d) -> p j d", j=BPG),
                                             b3[:, 0, :].unsqueeze(1).to_broadcast([P, BPG, D]), ALU.add))
                c.do(nc.vector.scalar_tensor_tensor(out=hst2[:, :, :], in0=hst2[:, :, :], scalar=0.2, in1=hst2[:, :, :], op0=ALU.mult, op1=ALU.max))
                c.did(nc.vector.tensor_tensor(hst2[:, :, :], hst2[:, :, :], xsb[:, bass.ds(g * BPG, BPG), :], ALU.add))

            v.sem_inc(S("e3_out"), 3)
            factors(0, 0, None)
            with v.Fori(0, NG - 1) as g:
                factors(g + 1, 2, g)
                finish(g, 0, g)
            finish(NG - 1, 3 * (NG - 1), None)

        def end3_pe(pe):
            with pe.Fori(0, NG) as g:
                pe.wait_ge(S("e3_factors"), g * 2 + 2)
                for u, t in ((0, hst), (1, tab)):
                    for j in range(BPG):
                        ins = nc.tensor.transpose(psB[:, u, j * P:(j + 1) * P], t[:, j, 0:D], ident[:, :])
                ins.then_inc(S("end_tr"), 1)
                pe.wait_ge(S("end_at"), g + (NG + 1))
                pe.wait_ge(S("e3_out"), g * 3 + 1)
                for j in range(BPG):
                    for u in range(2):
                        ins = nc.tensor.matmul(psB[:, 2, j * P:(j + 1) * P], hT[:, u, j * P:(j + 1) * P], w3t[:, u, :], start=(u == 0), stop=(u == 1))
                ins.then_inc(S("end_mm"), 1)

        def end3_act(act):
            with act.Fori(0, NG) as g:
                act.wait_ge(S("end_tr"), g + (NG + 2))
                nc.scalar.copy(hT[:, :, :], psB[:, 0:2, :]).then_inc(S("end_at"), 1)

        def end3_sp(sp):
            sp.sem_inc(S("y_out"), 16)
            sp.wait_ge(S("j3_out"), 16 * NG)
            sp.wait_ge(*P3.on("laid", IT + 1))
            sp.dma_start(h3_all, x3_t.rearrange("(j p) w -> p j w", p=P)).then_inc(S("h3_in"), 16)

            def group(g):
                sp.wait_ge(S("e3_out"), g * 3 + 6)

            with sp.Fori(0, NG - 1) as g:
                group(g)
                sp.dma_start(grows(out, g), hst2[:, :, :]).then_inc(S("y_out"), 16)
            group(NG - 1)
            r0 = (NG - 1) * GN
            whole, rest = (N - r0) // P, (N - r0) % P
            if whole:
                sp.dma_start(out[r0:r0 + whole * P, :].rearrange("(j p) w -> p j w", p=P), hst2[:, 0:whole, :]).then_inc(S("y_out"), 16)
            sp.dma_start(out[r0 + whole * P:N, :], hst2[0:rest, whole, :]).then_inc(S("y_out"), 16)
            sp.wait_ge(S("y_out"), 16 * NG + 16 * (2 if whole else 1))

        block = ctx.enter_context(nc.Block())

        @block.sync
        def _(sp):
            loads_sp(sp)
            keys_sp(sp)
            sort_sp(sp, 0)
            with sp.If(unsorted(sp) > 0):
                sort_sp(sp, 1)
            order_sp(sp, 0)
            order_sp(sp, 1)
            spread_sp(sp, 0, q0_t)
            pass_sp(sp, PB)
            spread_sp(sp, 1, k0_t)
            stats_sp(sp)
            sp.wait_ge(S("pay_out"), 32 * NPAY + 32)
            with sp.If(unsorted(sp) > 0):
                paysort_sp(sp)
            with sp.If(unsorted(sp) < 1):
                weights_sp(sp)
            pass_sp(sp, PA)
            proj_sp(sp, "j1", [(q1_t, 0, D), (kv1_t, D, 3 * D)])
            pass_sp(sp, P1)
            proj_sp(sp, "j2", [(h2_t, 0, D + 4), (ed2_t, D + 4, D + 8)])
            pass_sp(sp, P2)
            proj_sp(sp, "j3", [(x3_t, 0, D)])
            pass_sp(sp, P3)
            end3_sp(sp)

        @block.gpsimd
        def _(g_):
            constants_pool(g_)
            proj0_pool(g_)
            nodes_pool(g_)
            spread_pool(g_, 0, qxb_t)
            pass_pool(g_, PB)
            spread_pool(g_, 1, qxa_t)
            carry_pool(g_, PB)
            ends_pool(g_, PB)
            with g_.If(unsorted(g_) > 0):
                paysort_pool(g_)
            pass_pool(g_, PA)
            carry_pool(g_, PA)
            ends_pool(g_, PA)
            scatter_pool(g_, "j1", 0, D, qxa_t)
            pass_pool(g_, P1)
            carry_pool(g_, P1)
            ends_pool(g_, P1)
            scatter_pool(g_, "j2", D + 4, D + 8, edx_t)
            pass_pool(g_, P2)
            carry_pool(g_, P2)
            ends_pool(g_, P2)
            pass_pool(g_, P3)
            carry_pool(g_, P3)
            ends_pool(g_, P3)

        @block.vector
        def _(v):
            padding_dve(v)
            keys_dve(v)
            flag_dve(v)
            proj0_dve(v)
            sort_dve(v, 0)
            with v.If(unsorted(v) > 0):
                sort_dve(v, 1)
            order_dve(v, 0)
            node_parts_dve(v, 0)
            masks_dve(v, 0)
            order_dve(v, 1)
            node_parts_dve(v, 1)
            masks_dve(v, 1)
            bias_dve(v, b2_0)
            node_ends_dve(v, 0)
            pass_dve(v, PB)
            node_ends_dve(v, 1)
            carry_dve(v, PB)
            stats_dve(v)
            with v.If(unsorted(v) > 0):
                paysort_dve(v)
            with v.If(unsorted(v) < 1):
                nc.vector.memset(ew[PAD_ROW:P, PAD_COL:T], 0.0).then_inc(S("ew_padded"), 1)
            v.sem_inc(S("edges_ready"), 1)
            pass_dve(v, PA)
            carry_dve(v, PA)
            end0_dve(v)
            pass_dve(v, P1)
            carry_dve(v, P1)
            end1_dve(v)
            pass_dve(v, P2)
            carry_dve(v, P2)
            end2_dve(v)
            with v.If(unsorted(v) < 1):
                v.wait_ge(S("ew_in"), 32)
            pass_dve(v, P3)
            carry_dve(v, P3)
            end3_dve(v)

        @block.scalar
        def _(act):
            act.sem_inc(S("attr_free"), 1)
            weights3_act(act)
            proj0_act(act)
            sort_act(act, 0)
            with act.If(unsorted(act) > 0):
                sort_act(act, 1)
            nodes_act(act)
            pass_act(act, PB)
            carry_act(act, PB)
            pass_act(act, PA)
            carry_act(act, PA)
            end0_act(act)
            pass_act(act, P1)
            carry_act(act, P1)
            end1_act(act)
            pass_act(act, P2)
            carry_act(act, P2)
            end2_act(act)
            pass_act(act, P3)
            carry_act(act, P3)
            end3_act(act)

        @block.tensor
        def _(pe):
            weights3_pe(pe)
            flag_pe(pe)
            proj0_pe(pe)
            sort_pe(pe, 0)
            with pe.If(unsorted(pe) > 0):
                sort_pe(pe, 1)
            order_pe(pe, 0)
            order_pe(pe, 1)
            nodes_pe(pe, 0)
            payload_pe(pe)
            nodes_pe(pe, 1)
            carry_pe(pe, PB)
            carry_pe(pe, PA)
            end0_pe(pe)
            carry_pe(pe, P1)
            end1_pe(pe)
            carry_pe(pe, P2)
            carry_pe(pe, P3)
            end3_pe(pe)


_INS = ["x", "src", "dst", "edge_attr_64", "edge_weight",
        "L0_gnn_Wk", "L0_gnn_bk", "L0_gnn_Wm", "L0_gnn_bm", "L0_gnn_Wq", "L0_gnn_bq", "L0_gnn_W1", "L0_gnn_b1",
        "L0_gnn_gamma", "L0_gnn_beta", "L0_gnn_W2", "L0_gnn_b2",
        "L1_gnn_Wq", "L1_gnn_bq", "L1_gnn_Wk", "L1_gnn_bk", "L1_gnn_Wv", "L1_gnn_bv", "L1_gnn_We", "L1_gnn_be", "L1_gnn_Wo", "L1_gnn_bo",
        "L2_gnn_W", "L2_gnn_a_src", "L2_gnn_a_dst", "L3_gnn_W1", "L3_gnn_b1", "L3_gnn_W2", "L3_gnn_b2"]


def kernel(**inputs):
    import numpy as _np
    import concourse.bacc as _bacc
    from concourse import mybir as _mybir
    from concourse.bass_utils import run_bass_kernel_spmd as _run

    nc = _bacc.Bacc("TRN2", target_bir_lowering=False, num_devices=1)
    arrays, args = {}, {}
    for name in _INS:
        a = _np.ascontiguousarray(inputs[name])
        arrays[f"in_{name}_dram"] = a
        args[name] = nc.dram_tensor(f"in_{name}_dram", a.shape, _mybir.dt.from_np(a.dtype), kind="ExternalInput").ap()
    out = nc.dram_tensor("out_0_dram", (N, D), F32, kind="ExternalOutput").ap()
    graph_layers_kernel(nc, args, out)
    r = _run(nc, [arrays], core_ids=[0])
    return r.results[0]["out_0_dram"]
```
